# Optimizing a Trainium2 kernel written in Bass

```python
import numpy as np
import jax
import jax.numpy as jnp

def _softmax(x, axis=-1):
    return jax.nn.softmax(x, axis=axis)

def _gelu(x):
    return jax.nn.gelu(x, approximate=True)

def _silu(x):
    return jax.nn.silu(x)

def _sigmoid(x):
    return jax.nn.sigmoid(x)

def _layernorm(x, axis=-1, eps=1e-05):
    m = jnp.mean(x, axis=axis, keepdims=True)
    v = jnp.var(x, axis=axis, keepdims=True)
    return (x - m) / jnp.sqrt(v + eps)

def _scatter_add(tgt, idx, src, axis=0):
    return tgt.at[idx].add(src)

def _segment_sum(src, seg, n):
    return jax.ops.segment_sum(src, seg, n)
kernel_name = 'mk_pixart_resid_d4_seqx_r8_904fbf'

def setup_inputs(seed: int=0):
    np.random.seed(seed)
    _w = jnp.asarray

    def _rec_inputs():
        import jax
        import jax.numpy as jnp
        _rk = jax.random.key(seed)
        x = -0.0002928 + 1 * jax.random.normal(jax.random.fold_in(_rk, 1), (4, 512, 128), jnp.float32)
        _lenS = 512 - jax.random.randint(jax.random.fold_in(_rk, 7), (4,), 0, max(1, 512 // 4) + 1, jnp.int32)
        _lenS2 = 77 - jax.random.randint(jax.random.fold_in(_rk, 8), (4,), 0, max(1, 77 // 4) + 1, jnp.int32)
        _ctx_1024P = jax.random.normal(jax.random.fold_in(_rk, 11), (4, 16, 128), jnp.float32)
        _ctx_1024c = jax.random.dirichlet(jax.random.fold_in(_rk, 511), 0.3 * jnp.ones((16,), jnp.float32), (4, 77))
        _ctx_1024t = jnp.einsum('bsk,bkd->bsd', _ctx_1024c, _ctx_1024P)
        _ctx_1024t = _ctx_1024t * jax.lax.rsqrt(jnp.mean(jnp.square(_ctx_1024t)) + 1e-12) * 0.953939
        ctx_1024 = -1.39393e-06 + 0.999914 * (_ctx_1024t + 0.3 * jax.random.normal(jax.random.fold_in(_rk, 611), (4, 77, 128), jnp.float32))
        condB_tau = jax.random.uniform(jax.random.fold_in(_rk, 12), (4,), jnp.float32, 0.0, 1.23395)
        fside_BxS2_0 = -0.00205293 + 0.99739 * jax.random.normal(jax.random.fold_in(_rk, 13), (4, 77), jnp.float32)
        condB_pt = jax.random.uniform(jax.random.fold_in(_rk, 15), (4,), jnp.float32, 0.0, 226.919)
        return (x, ctx_1024, condB_tau, fside_BxS2_0, condB_pt, _lenS2)
    x, ctx_1024, condB_tau, fside_BxS2_0, condB_pt, _lenS2 = _rec_inputs()

    def _L0_xcond_setup():
        import jax, jax.numpy as jnp
        import numpy as np
        B, S, D, H = (2, 256, 128, 16)
        DK = D // H

        def _split_heads(x):
            b, s, _ = x.shape
            return x.reshape(b, s, H, DK).transpose(0, 2, 1, 3)
        key = jax.random.key(seed)
        ks = jax.random.split(key, 14)
        inp = {'query': jax.random.normal(ks[0], (B, S, D), jnp.float32), 'key': jax.random.normal(ks[1], (B, S, D), jnp.float32), 'value': jax.random.normal(ks[2], (B, S, D), jnp.float32), 'tau': jax.random.uniform(ks[3], (B, 1), jnp.float32, 0.5, 1.5), 'delta': jax.random.normal(ks[4], (B, S), jnp.float32)}
        sc = 1.0 / np.sqrt(D)
        for i, name in enumerate(['q', 'k', 'v', 'o']):
            inp[f'W{name}'] = jax.random.normal(ks[5 + 2 * i], (D, D), jnp.float32) * sc
            inp[f'b{name}'] = jax.random.normal(ks[6 + 2 * i], (D,), jnp.float32) * 0.01
        return inp
    _L0_xcond_all = _L0_xcond_setup()
    _L0_xcond_in = {k: v for k, v in _L0_xcond_all.items() if k in ('Wq', 'bq', 'Wk', 'bk', 'Wv', 'bv', 'Wo', 'bo')}
    del _L0_xcond_all

    def _L0_ffn_setup():
        import math
        import jax, jax.numpy as jnp
        import numpy as np
        D_MODEL = 128
        D_FF = 512
        E = 8
        K = 2
        CF = 1.25
        CLAMP = 10000.0
        key = jax.random.key(seed)
        k0, k1, k2, k3 = jax.random.split(key, 4)
        B, S = (4, 256)
        x = jax.random.normal(k0, (B, S, D_MODEL), dtype=jnp.float32)
        ln_gamma = jnp.ones((D_MODEL,), jnp.float32)
        ln_beta = jnp.zeros((D_MODEL,), jnp.float32)
        rb = 0.02 * math.sqrt(3.0)
        Wr = jax.random.uniform(k1, (E, D_MODEL), jnp.float32, -rb, rb)
        b12 = math.sqrt(6.0 / (D_MODEL + 2 * D_FF))
        W12 = jax.random.uniform(k2, (E, 2 * D_FF, D_MODEL), jnp.float32, -b12, b12)
        b3 = math.sqrt(6.0 / (D_FF + D_MODEL))
        W3 = jax.random.uniform(k3, (E, D_MODEL, D_FF), jnp.float32, -b3, b3)
        return {'x': x, 'ln_gamma': ln_gamma, 'ln_beta': ln_beta, 'Wr': Wr, 'W12': W12, 'W3': W3}
    _L0_ffn_all = _L0_ffn_setup()
    _L0_ffn_in = {k: v for k, v in _L0_ffn_all.items() if k in ('ln_gamma', 'ln_beta', 'Wr', 'W12', 'W3')}
    del _L0_ffn_all

    def _L1_xcond_setup():
        import jax, jax.numpy as jnp
        import numpy as np
        D_MODEL = 128
        N_HEADS = 16
        key = jax.random.key(seed)
        ks = jax.random.split(key, 16)
        B, L, S, D = (4, 256, 256, D_MODEL)
        inp = {'q': jax.random.normal(ks[0], (B, L, D), jnp.float32), 'k': jax.random.normal(ks[1], (B, S, D), jnp.float32), 'v': jax.random.normal(ks[2], (B, S, D), jnp.float32), 'tau': jax.random.uniform(ks[3], (B, 1), jnp.float32, 0.5, 1.5), 'delta': jax.random.normal(ks[4], (B, S), jnp.float32)}
        s = 1.0 / np.sqrt(D)
        inp['Wq'] = jax.random.normal(ks[5], (D, D), jnp.float32) * s
        inp['bq'] = jnp.zeros((D,), jnp.float32)
        inp['Wk'] = jax.random.normal(ks[6], (D, D), jnp.float32) * s
        inp['bk'] = jnp.zeros((D,), jnp.float32)
        inp['Wv'] = jax.random.normal(ks[7], (D, D), jnp.float32) * s
        inp['bv'] = jnp.zeros((D,), jnp.float32)
        inp['Wo'] = jax.random.normal(ks[8], (D, D), jnp.float32) * s
        inp['bo'] = jnp.zeros((D,), jnp.float32)
        return inp
    _L1_xcond_all = _L1_xcond_setup()
    _L1_xcond_in = {k: v for k, v in _L1_xcond_all.items() if k in ('Wq', 'bq', 'Wk', 'bk', 'Wv', 'bv', 'Wo', 'bo')}
    del _L1_xcond_all

    def _L1_ffn_setup():
        import jax, jax.numpy as jnp
        import numpy as np
        B, S, D_MODEL, D_HIDDEN = (4, 256, 128, 512)

        def act_quant(x):
            scale = 127.0 / jnp.clip(jnp.max(jnp.abs(x), axis=-1, keepdims=True), 1e-05)
            return jnp.clip(jnp.round(x * scale), -128, 127) / scale

        def weight_quant(w):
            scale = 1.0 / jnp.clip(jnp.mean(jnp.abs(w)), 1e-05)
            return jnp.clip(jnp.round(w * scale), -1, 1) / scale

        def bit_linear(x, w):
            xq = x + jax.lax.stop_gradient(act_quant(x) - x)
            wq = w + jax.lax.stop_gradient(weight_quant(w) - w)
            return jnp.einsum('bsd,hd->bsh', xq, wq)

        def depthwise_conv1d(x_bcl, w, b):
            y = jax.lax.conv_general_dilated(x_bcl, w, window_strides=(1,), padding=[(1, 1)], dimension_numbers=('NCH', 'OIH', 'NCH'), feature_group_count=x_bcl.shape[1])
            return y + b[None, :, None]
        key = jax.random.key(seed)
        ks = jax.random.split(key, 5)
        lim1 = 1.0 / np.sqrt(D_MODEL)
        lim2 = 1.0 / np.sqrt(D_HIDDEN)
        limc = 1.0 / np.sqrt(3.0)
        return {'x': jax.random.normal(ks[0], (B, S, D_MODEL), dtype=jnp.float32), 'w1': jax.random.uniform(ks[1], (D_HIDDEN, D_MODEL), jnp.float32, -lim1, lim1), 'conv_w': jax.random.uniform(ks[2], (D_HIDDEN, 1, 3), jnp.float32, -limc, limc), 'conv_b': jax.random.uniform(ks[3], (D_HIDDEN,), jnp.float32, -limc, limc), 'w2': jax.random.uniform(ks[4], (D_MODEL, D_HIDDEN), jnp.float32, -lim2, lim2)}
    _L1_ffn_all = _L1_ffn_setup()
    _L1_ffn_in = {k: v for k, v in _L1_ffn_all.items() if k in ('w1', 'conv_w', 'conv_b', 'w2')}
    del _L1_ffn_all

    def _L2_xcond_setup():
        import jax, jax.numpy as jnp
        import numpy as np
        N, L, H, Q = (64, 258, 128, 32)
        WINDOW = 16.0
        DEV_POW = 128.0
        key = jax.random.key(seed)
        k1, k2, k3, k4, k5, k6 = jax.random.split(key, 6)
        encoder_outputs = jax.random.normal(k1, (N, L, H), dtype=jnp.float32)
        decoder_h_t = jax.random.normal(k2, (N, Q, H), dtype=jnp.float32)
        src_len = jax.random.randint(k3, (N,), 32, L + 1).astype(jnp.int32)
        p_t = jax.random.uniform(k4, (N,), dtype=jnp.float32) * (src_len.astype(jnp.float32) - 1.0)
        W_a = jax.random.normal(k5, (H, H), dtype=jnp.float32) * (1.0 / np.sqrt(H))
        W_c = jax.random.normal(k6, (H, 2 * H), dtype=jnp.float32) * (1.0 / np.sqrt(2 * H))
        return {'encoder_outputs': encoder_outputs, 'decoder_h_t': decoder_h_t, 'src_len': src_len, 'p_t': p_t, 'W_a': W_a, 'W_c': W_c}
    _L2_xcond_all = _L2_xcond_setup()
    _L2_xcond_in = {k: v for k, v in _L2_xcond_all.items() if k in ('W_a', 'W_c')}
    del _L2_xcond_all

    def _L2_ffn_setup():
        import jax, jax.numpy as jnp
        import numpy as np
        DIM = 128
        DEPTH = 6
        HEADS = 16
        DIM_HEAD = 64
        WINDOW = 32
        INNER = HEADS * DIM_HEAD
        DIM_INNER = int(DIM * 4 * 2 / 3)
        QK_SCALE = 8.0

        def shift_tokens(t):
            a, s = jnp.split(t, 2, -1)
            s = jnp.pad(s, ((0, 0), (1, 0), (0, 0)))[:, :-1]
            return jnp.concatenate([a, s], -1)

        def l2norm(t):
            return t / jnp.maximum(jnp.linalg.norm(t, axis=-1, keepdims=True), 1e-12)

        def rotate_half(x):
            x1, x2 = jnp.split(x, 2, -1)
            return jnp.concatenate([-x2, x1], -1)

        def rotary_tables(n):
            half = jnp.arange(0, DIM_HEAD, 2, dtype=jnp.float32)
            inv_freq = 1.0 / 10000.0 ** (half / DIM_HEAD)
            t = jnp.arange(n, dtype=jnp.float32)
            freqs = t[:, None] * inv_freq[None, :]
            freqs = jnp.concatenate([freqs, freqs], -1)
            base_scale = (half + 0.4 * DIM_HEAD) / (1.4 * DIM_HEAD)
            power = (t - n // 2) / (WINDOW // 2)
            scale = base_scale[None, :] ** power[:, None]
            scale = jnp.concatenate([scale, scale], -1)
            return (freqs, scale)

        def local_attention(q, k, v):
            b, h, n, d = q.shape
            w = WINDOW
            nw = n // w
            bq = q.reshape(b, h, nw, w, d)
            bk = k.reshape(b, h, nw, w, d)
            bv = v.reshape(b, h, nw, w, d)

            def look(t):
                p = jnp.pad(t, ((0, 0), (0, 0), (1, 0), (0, 0), (0, 0)))
                return jnp.concatenate([p[:, :, :nw], p[:, :, 1:]], axis=3)
            bk2, bv2 = (look(bk), look(bv))
            seq = jnp.arange(n).reshape(nw, w)
            seq_p = jnp.pad(seq, ((1, 0), (0, 0)), constant_values=-1)
            jt = jnp.concatenate([seq_p[:nw], seq_p[1:]], axis=1)
            it = seq[:, :, None]
            jb = jt[:, None, :]
            mask = (it < jb) | (it > jb + w) | (jb == -1)
            sim = jnp.einsum('bhwie,bhwje->bhwij', bq, bk2) * QK_SCALE
            sim = jnp.where(mask, -jnp.finfo(sim.dtype).max, sim)
            attn = jax.nn.softmax(sim, -1)
            out = jnp.einsum('bhwij,bhwje->bhwie', attn, bv2)
            return out.reshape(b, h, n, d)

        def attn_layer(x, Wqkv, qs, ksc, Wo):
            b, n, _ = x.shape
            qkv = x @ Wqkv
            q, k, v = jnp.split(qkv, 3, -1)
            sh = lambda t: t.reshape(b, n, HEADS, DIM_HEAD).transpose(0, 2, 1, 3)
            q, k, v = (sh(q), sh(k), sh(v))
            q = l2norm(q) * qs
            k = l2norm(k) * ksc
            freqs, scale = rotary_tables(n)
            cos, sin = (jnp.cos(freqs), jnp.sin(freqs))
            q = q * cos * scale + rotate_half(q) * sin * scale
            inv = 1.0 / scale
            k = k * cos * inv + rotate_half(k) * sin * inv
            out = local_attention(q, k, v)
            out = out.transpose(0, 2, 1, 3).reshape(b, n, INNER)
            return out @ Wo

        def ffn_layer(x, g, bln, W1, b1, W2, b2):
            mu = x.mean(-1, keepdims=True)
            var = ((x - mu) ** 2).mean(-1, keepdims=True)
            xn = (x - mu) / jnp.sqrt(var + 1e-05) * g + bln
            hg = xn @ W1 + b1
            a, gate = jnp.split(hg, 2, -1)
            return a * jax.nn.gelu(gate, approximate=False) @ W2 + b2
        key = jax.random.key(seed)
        ks = jax.random.split(key, 8)
        B, N = (2, 256)
        init = lambda k, shape: jax.random.normal(k, shape, jnp.float32) * 0.02
        return {'x': jax.random.normal(ks[0], (B, N, DIM), jnp.float32), 'Wqkv': init(ks[1], (DEPTH, DIM, 3 * INNER)), 'q_scale': jnp.ones((DEPTH, DIM_HEAD), jnp.float32), 'k_scale': jnp.ones((DEPTH, DIM_HEAD), jnp.float32), 'Wo': init(ks[2], (DEPTH, INNER, DIM)), 'ln_g': jnp.ones((DEPTH, DIM), jnp.float32), 'ln_b': jnp.zeros((DEPTH, DIM), jnp.float32), 'W1': init(ks[3], (DEPTH, DIM, 2 * DIM_INNER)), 'b1': jnp.zeros((DEPTH, 2 * DIM_INNER), jnp.float32), 'W2': init(ks[4], (DEPTH, DIM_INNER, DIM)), 'b2': jnp.zeros((DEPTH, DIM), jnp.float32)}
    _L2_ffn_all = _L2_ffn_setup()
    _L2_ffn_in = {k: v for k, v in _L2_ffn_all.items() if k in ('Wqkv', 'q_scale', 'k_scale', 'Wo', 'ln_g', 'ln_b', 'W1', 'b1', 'W2', 'b2')}
    del _L2_ffn_all

    def _L3_xcond_setup():
        import jax, jax.numpy as jnp
        import numpy as np
        B, S, D, H = (2, 256, 128, 16)
        DK = D // H

        def _split_heads(x):
            b, s, _ = x.shape
            return x.reshape(b, s, H, DK).transpose(0, 2, 1, 3)
        key = jax.random.key(seed)
        ks = jax.random.split(key, 14)
        inp = {'query': jax.random.normal(ks[0], (B, S, D), jnp.float32), 'key': jax.random.normal(ks[1], (B, S, D), jnp.float32), 'value': jax.random.normal(ks[2], (B, S, D), jnp.float32), 'tau': jax.random.uniform(ks[3], (B, 1), jnp.float32, 0.5, 1.5), 'delta': jax.random.normal(ks[4], (B, S), jnp.float32)}
        sc = 1.0 / np.sqrt(D)
        for i, name in enumerate(['q', 'k', 'v', 'o']):
            inp[f'W{name}'] = jax.random.normal(ks[5 + 2 * i], (D, D), jnp.float32) * sc
            inp[f'b{name}'] = jax.random.normal(ks[6 + 2 * i], (D,), jnp.float32) * 0.01
        return inp
    _L3_xcond_all = _L3_xcond_setup()
    _L3_xcond_in = {k: v for k, v in _L3_xcond_all.items() if k in ('Wq', 'bq', 'Wk', 'bk', 'Wv', 'bv', 'Wo', 'bo')}
    del _L3_xcond_all

    def _L3_ffn_setup():
        import jax, jax.numpy as jnp
        import numpy as np
        E = 8
        K = 2
        CAP_RATIO = 1.05
        key = jax.random.key(seed)
        ks = jax.random.split(key, 4)
        B, S, D, H = (2, 256, 128, 512)
        x = jax.random.normal(ks[0], (B, S, D), jnp.float32)
        Wg = jax.random.normal(ks[1], (E, D), jnp.float32) * 0.02
        W1 = jax.random.normal(ks[2], (E, D, H), jnp.float32) * 0.02
        b1 = jnp.zeros((E, H), jnp.float32)
        W2 = jax.random.normal(ks[3], (E, H, D), jnp.float32) * 0.02
        b2 = jnp.zeros((E, D), jnp.float32)
        return {'x': x, 'Wg': Wg, 'W1': W1, 'b1': b1, 'W2': W2, 'b2': b2}
    _L3_ffn_all = _L3_ffn_setup()
    _L3_ffn_in = {k: v for k, v in _L3_ffn_all.items() if k in ('Wg', 'W1', 'b1', 'W2', 'b2')}
    del _L3_ffn_all
    return {'x': x, 'ctx_1024': ctx_1024, 'condB_tau': condB_tau, 'fside_BxS2_0': fside_BxS2_0, 'condB_pt': condB_pt, '_lenS2': _lenS2, 'L0_xcond_Wq': _L0_xcond_in['Wq'], 'L0_xcond_bq': _L0_xcond_in['bq'], 'L0_xcond_Wk': _L0_xcond_in['Wk'], 'L0_xcond_bk': _L0_xcond_in['bk'], 'L0_xcond_Wv': _L0_xcond_in['Wv'], 'L0_xcond_bv': _L0_xcond_in['bv'], 'L0_xcond_Wo': _L0_xcond_in['Wo'], 'L0_xcond_bo': _L0_xcond_in['bo'], 'L0_ffn_ln_gamma': _L0_ffn_in['ln_gamma'], 'L0_ffn_ln_beta': _L0_ffn_in['ln_beta'], 'L0_ffn_Wr': _L0_ffn_in['Wr'], 'L0_ffn_W12': _L0_ffn_in['W12'], 'L0_ffn_W3': _L0_ffn_in['W3'], 'L1_xcond_Wq': _L1_xcond_in['Wq'], 'L1_xcond_bq': _L1_xcond_in['bq'], 'L1_xcond_Wk': _L1_xcond_in['Wk'], 'L1_xcond_bk': _L1_xcond_in['bk'], 'L1_xcond_Wv': _L1_xcond_in['Wv'], 'L1_xcond_bv': _L1_xcond_in['bv'], 'L1_xcond_Wo': _L1_xcond_in['Wo'], 'L1_xcond_bo': _L1_xcond_in['bo'], 'L1_ffn_w1': _L1_ffn_in['w1'], 'L1_ffn_conv_w': _L1_ffn_in['conv_w'], 'L1_ffn_conv_b': _L1_ffn_in['conv_b'], 'L1_ffn_w2': _L1_ffn_in['w2'], 'L2_xcond_W_a': _L2_xcond_in['W_a'], 'L2_xcond_W_c': _L2_xcond_in['W_c'], 'L2_ffn_Wqkv': _L2_ffn_in['Wqkv'], 'L2_ffn_q_scale': _L2_ffn_in['q_scale'], 'L2_ffn_k_scale': _L2_ffn_in['k_scale'], 'L2_ffn_Wo': _L2_ffn_in['Wo'], 'L2_ffn_ln_g': _L2_ffn_in['ln_g'], 'L2_ffn_ln_b': _L2_ffn_in['ln_b'], 'L2_ffn_W1': _L2_ffn_in['W1'], 'L2_ffn_b1': _L2_ffn_in['b1'], 'L2_ffn_W2': _L2_ffn_in['W2'], 'L2_ffn_b2': _L2_ffn_in['b2'], 'L3_xcond_Wq': _L3_xcond_in['Wq'], 'L3_xcond_bq': _L3_xcond_in['bq'], 'L3_xcond_Wk': _L3_xcond_in['Wk'], 'L3_xcond_bk': _L3_xcond_in['bk'], 'L3_xcond_Wv': _L3_xcond_in['Wv'], 'L3_xcond_bv': _L3_xcond_in['bv'], 'L3_xcond_Wo': _L3_xcond_in['Wo'], 'L3_xcond_bo': _L3_xcond_in['bo'], 'L3_ffn_Wg': _L3_ffn_in['Wg'], 'L3_ffn_W1': _L3_ffn_in['W1'], 'L3_ffn_b1': _L3_ffn_in['b1'], 'L3_ffn_W2': _L3_ffn_in['W2'], 'L3_ffn_b2': _L3_ffn_in['b2']}

def reference(x, ctx_1024, condB_tau, fside_BxS2_0, condB_pt, _lenS2, L0_xcond_Wq, L0_xcond_bq, L0_xcond_Wk, L0_xcond_bk, L0_xcond_Wv, L0_xcond_bv, L0_xcond_Wo, L0_xcond_bo, L0_ffn_ln_gamma, L0_ffn_ln_beta, L0_ffn_Wr, L0_ffn_W12, L0_ffn_W3, L1_xcond_Wq, L1_xcond_bq, L1_xcond_Wk, L1_xcond_bk, L1_xcond_Wv, L1_xcond_bv, L1_xcond_Wo, L1_xcond_bo, L1_ffn_w1, L1_ffn_conv_w, L1_ffn_conv_b, L1_ffn_w2, L2_xcond_W_a, L2_xcond_W_c, L2_ffn_Wqkv, L2_ffn_q_scale, L2_ffn_k_scale, L2_ffn_Wo, L2_ffn_ln_g, L2_ffn_ln_b, L2_ffn_W1, L2_ffn_b1, L2_ffn_W2, L2_ffn_b2, L3_xcond_Wq, L3_xcond_bq, L3_xcond_Wk, L3_xcond_bk, L3_xcond_Wv, L3_xcond_bv, L3_xcond_Wo, L3_xcond_bo, L3_ffn_Wg, L3_ffn_W1, L3_ffn_b1, L3_ffn_W2, L3_ffn_b2):
    import jax
    import jax.numpy as jnp

    def _L0_xcond_ref(query, key, value, tau, delta, Wq, bq, Wk, bk, Wv, bv, Wo, bo):
        import jax, jax.numpy as jnp
        import numpy as np
        B, S, D, H = (2, 256, 128, 16)
        DK = D // H

        def _split_heads(x):
            b, s, _ = x.shape
            return x.reshape(b, s, H, DK).transpose(0, 2, 1, 3)
        q = _split_heads(query @ Wq.T + bq)
        k = _split_heads(key @ Wk.T + bk)
        v = _split_heads(value @ Wv.T + bv)
        scores = jnp.einsum('bhqd,bhkd->bhqk', q, k)
        scores = scores * tau[:, :, None, None] + delta[:, None, None, :]
        scores = scores / jnp.sqrt(jnp.asarray(DK, scores.dtype))
        p_attn = jax.nn.softmax(scores, axis=-1)
        x = jnp.einsum('bhqk,bhkd->bhqd', p_attn, v)
        x = x.transpose(0, 2, 1, 3).reshape(query.shape[0], -1, H * DK)
        return x @ Wo.T + bo

    def _L0_ffn_ref(x, ln_gamma, ln_beta, Wr, W12, W3):
        import math
        import jax, jax.numpy as jnp
        import numpy as np
        D_MODEL = 128
        D_FF = 512
        E = 8
        K = 2
        CF = 1.25
        CLAMP = 10000.0
        B, S, D = x.shape
        T = B * S
        xf = x.reshape(T, D)
        mu = xf.mean(-1, keepdims=True)
        var = ((xf - mu) ** 2).mean(-1, keepdims=True)
        xn = (xf - mu) / jnp.sqrt(var + 1e-05) * ln_gamma + ln_beta
        logits = jnp.clip(xn @ Wr.T, -CLAMP, CLAMP)
        m = logits.max(-1, keepdims=True)
        ex = jnp.exp(logits - m)
        probs = ex / (ex.sum(-1, keepdims=True) + 1e-12)
        top_p, top_i = jax.lax.top_k(probs, K)
        Sslots = T * K
        experts = top_i.reshape(-1)
        weights = top_p.reshape(-1)
        tokens = jnp.repeat(jnp.arange(T, dtype=jnp.int32), K)
        order = jnp.argsort(experts, stable=True)
        e_s = experts[order]
        w_s = weights[order]
        t_s = tokens[order]
        counts = jnp.bincount(e_s, length=E)
        offsets = jnp.concatenate([jnp.zeros((1,), counts.dtype), jnp.cumsum(counts)])
        rank = jnp.arange(Sslots, dtype=counts.dtype) - offsets[e_s]
        cap = max(1, math.ceil(math.ceil(T * K * CF) / E))
        kept = rank < cap
        pos = jnp.where(kept, rank, cap)
        buf = jnp.zeros((E, cap, D), x.dtype).at[e_s, pos].set(xn[t_s], mode='drop')
        gu = jnp.einsum('ecd,efd->ecf', buf, W12)
        g, u = (gu[..., :D_FF], gu[..., D_FF:])
        h = jax.nn.silu(g) * u
        y = jnp.einsum('ecf,edf->ecd', h, W3)
        y_slot = y[e_s, jnp.minimum(pos, cap - 1)] * (w_s * kept.astype(x.dtype))[:, None]
        out = jnp.zeros((T, D), x.dtype).at[t_s].add(y_slot)
        return out.reshape(B, S, D)

    def _L1_xcond_ref(q, k, v, tau, delta, Wq, bq, Wk, bk, Wv, bv, Wo, bo):
        import jax, jax.numpy as jnp
        import numpy as np
        D_MODEL = 128
        N_HEADS = 16
        B, L, D = q.shape
        S = k.shape[1]
        H = N_HEADS
        E = D // H
        qh = (q @ Wq.T + bq).reshape(B, L, H, E)
        kh = (k @ Wk.T + bk).reshape(B, S, H, E)
        vh = (v @ Wv.T + bv).reshape(B, S, H, E)
        scale = 1.0 / np.sqrt(E).astype(np.float32)
        scores = jnp.einsum('blhe,bshe->bhls', qh, kh)
        scores = scores * tau[:, None, None, :] + delta[:, None, None, :]
        a = jax.nn.softmax(scale * scores, axis=-1)
        out = jnp.einsum('bhls,bshd->blhd', a, vh).reshape(B, L, D)
        return out @ Wo.T + bo

    def _L1_ffn_ref(x, w1, conv_w, conv_b, w2):
        import jax, jax.numpy as jnp
        import numpy as np
        B, S, D_MODEL, D_HIDDEN = (4, 256, 128, 512)

        def act_quant(x):
            scale = 127.0 / jnp.clip(jnp.max(jnp.abs(x), axis=-1, keepdims=True), 1e-05)
            return jnp.clip(jnp.round(x * scale), -128, 127) / scale

        def weight_quant(w):
            scale = 1.0 / jnp.clip(jnp.mean(jnp.abs(w)), 1e-05)
            return jnp.clip(jnp.round(w * scale), -1, 1) / scale

        def bit_linear(x, w):
            xq = x + jax.lax.stop_gradient(act_quant(x) - x)
            wq = w + jax.lax.stop_gradient(weight_quant(w) - w)
            return jnp.einsum('bsd,hd->bsh', xq, wq)

        def depthwise_conv1d(x_bcl, w, b):
            y = jax.lax.conv_general_dilated(x_bcl, w, window_strides=(1,), padding=[(1, 1)], dimension_numbers=('NCH', 'OIH', 'NCH'), feature_group_count=x_bcl.shape[1])
            return y + b[None, :, None]
        h = bit_linear(x, w1)
        h = depthwise_conv1d(h.transpose(0, 2, 1), conv_w, conv_b)
        h = h.transpose(0, 2, 1)
        h = jax.nn.silu(h)
        return bit_linear(h, w2)

    def _L2_xcond_ref(encoder_outputs, decoder_h_t, src_len, p_t, W_a, W_c):
        import jax, jax.numpy as jnp
        import numpy as np
        N, L, H, Q = (64, 258, 128, 32)
        WINDOW = 16.0
        DEV_POW = 128.0
        n, l, h = encoder_outputs.shape
        idx = jnp.arange(l, dtype=jnp.float32)
        src_end = src_len.astype(jnp.float32)
        attn_start = jnp.maximum(p_t - WINDOW, 0.0)
        attn_end = jnp.minimum(p_t + WINDOW, src_end)
        mask = (idx[None, :] < attn_start[:, None]) | (idx[None, :] > attn_end[:, None])
        score = jnp.einsum('nqh,hk,nlk->nql', decoder_h_t, W_a, encoder_outputs)
        score = jnp.where(mask[:, None, :], -1000000000.0, score)
        align = jax.nn.softmax(score, axis=2)
        gauss = jnp.exp(-(idx[None, :] - p_t[:, None]) ** 2 / DEV_POW)
        align = align * gauss[:, None, :]
        context = jnp.einsum('nql,nlh->nqh', align, encoder_outputs)
        cat = jnp.concatenate([context, decoder_h_t], axis=2)
        return jnp.tanh(cat @ W_c.T)

    def _L2_ffn_ref(x, Wqkv, q_scale, k_scale, Wo, ln_g, ln_b, W1, b1, W2, b2):
        import jax, jax.numpy as jnp
        import numpy as np
        DIM = 128
        DEPTH = 6
        HEADS = 16
        DIM_HEAD = 64
        WINDOW = 32
        INNER = HEADS * DIM_HEAD
        DIM_INNER = int(DIM * 4 * 2 / 3)
        QK_SCALE = 8.0

        def shift_tokens(t):
            a, s = jnp.split(t, 2, -1)
            s = jnp.pad(s, ((0, 0), (1, 0), (0, 0)))[:, :-1]
            return jnp.concatenate([a, s], -1)

        def l2norm(t):
            return t / jnp.maximum(jnp.linalg.norm(t, axis=-1, keepdims=True), 1e-12)

        def rotate_half(x):
            x1, x2 = jnp.split(x, 2, -1)
            return jnp.concatenate([-x2, x1], -1)

        def rotary_tables(n):
            half = jnp.arange(0, DIM_HEAD, 2, dtype=jnp.float32)
            inv_freq = 1.0 / 10000.0 ** (half / DIM_HEAD)
            t = jnp.arange(n, dtype=jnp.float32)
            freqs = t[:, None] * inv_freq[None, :]
            freqs = jnp.concatenate([freqs, freqs], -1)
            base_scale = (half + 0.4 * DIM_HEAD) / (1.4 * DIM_HEAD)
            power = (t - n // 2) / (WINDOW // 2)
            scale = base_scale[None, :] ** power[:, None]
            scale = jnp.concatenate([scale, scale], -1)
            return (freqs, scale)

        def local_attention(q, k, v):
            b, h, n, d = q.shape
            w = WINDOW
            nw = n // w
            bq = q.reshape(b, h, nw, w, d)
            bk = k.reshape(b, h, nw, w, d)
            bv = v.reshape(b, h, nw, w, d)

            def look(t):
                p = jnp.pad(t, ((0, 0), (0, 0), (1, 0), (0, 0), (0, 0)))
                return jnp.concatenate([p[:, :, :nw], p[:, :, 1:]], axis=3)
            bk2, bv2 = (look(bk), look(bv))
            seq = jnp.arange(n).reshape(nw, w)
            seq_p = jnp.pad(seq, ((1, 0), (0, 0)), constant_values=-1)
            jt = jnp.concatenate([seq_p[:nw], seq_p[1:]], axis=1)
            it = seq[:, :, None]
            jb = jt[:, None, :]
            mask = (it < jb) | (it > jb + w) | (jb == -1)
            sim = jnp.einsum('bhwie,bhwje->bhwij', bq, bk2) * QK_SCALE
            sim = jnp.where(mask, -jnp.finfo(sim.dtype).max, sim)
            attn = jax.nn.softmax(sim, -1)
            out = jnp.einsum('bhwij,bhwje->bhwie', attn, bv2)
            return out.reshape(b, h, n, d)

        def attn_layer(x, Wqkv, qs, ksc, Wo):
            b, n, _ = x.shape
            qkv = x @ Wqkv
            q, k, v = jnp.split(qkv, 3, -1)
            sh = lambda t: t.reshape(b, n, HEADS, DIM_HEAD).transpose(0, 2, 1, 3)
            q, k, v = (sh(q), sh(k), sh(v))
            q = l2norm(q) * qs
            k = l2norm(k) * ksc
            freqs, scale = rotary_tables(n)
            cos, sin = (jnp.cos(freqs), jnp.sin(freqs))
            q = q * cos * scale + rotate_half(q) * sin * scale
            inv = 1.0 / scale
            k = k * cos * inv + rotate_half(k) * sin * inv
            out = local_attention(q, k, v)
            out = out.transpose(0, 2, 1, 3).reshape(b, n, INNER)
            return out @ Wo

        def ffn_layer(x, g, bln, W1, b1, W2, b2):
            mu = x.mean(-1, keepdims=True)
            var = ((x - mu) ** 2).mean(-1, keepdims=True)
            xn = (x - mu) / jnp.sqrt(var + 1e-05) * g + bln
            hg = xn @ W1 + b1
            a, gate = jnp.split(hg, 2, -1)
            return a * jax.nn.gelu(gate, approximate=False) @ W2 + b2
        for i in range(DEPTH):
            x = attn_layer(shift_tokens(x), Wqkv[i], q_scale[i], k_scale[i], Wo[i]) + x
            x = ffn_layer(shift_tokens(x), ln_g[i], ln_b[i], W1[i], b1[i], W2[i], b2[i]) + x
        return x

    def _L3_xcond_ref(query, key, value, tau, delta, Wq, bq, Wk, bk, Wv, bv, Wo, bo):
        import jax, jax.numpy as jnp
        import numpy as np
        B, S, D, H = (2, 256, 128, 16)
        DK = D // H

        def _split_heads(x):
            b, s, _ = x.shape
            return x.reshape(b, s, H, DK).transpose(0, 2, 1, 3)
        q = _split_heads(query @ Wq.T + bq)
        k = _split_heads(key @ Wk.T + bk)
        v = _split_heads(value @ Wv.T + bv)
        scores = jnp.einsum('bhqd,bhkd->bhqk', q, k)
        scores = scores * tau[:, :, None, None] + delta[:, None, None, :]
        scores = scores / jnp.sqrt(jnp.asarray(DK, scores.dtype))
        p_attn = jax.nn.softmax(scores, axis=-1)
        x = jnp.einsum('bhqk,bhkd->bhqd', p_attn, v)
        x = x.transpose(0, 2, 1, 3).reshape(query.shape[0], -1, H * DK)
        return x @ Wo.T + bo

    def _L3_ffn_ref(x, Wg, W1, b1, W2, b2):
        import jax, jax.numpy as jnp
        import numpy as np
        E = 8
        K = 2
        CAP_RATIO = 1.05
        B, S, D = x.shape
        T = B * S
        xf = x.reshape(T, D)
        gates = jax.nn.softmax(xf @ Wg.T, axis=-1)
        topw, topi = jax.lax.top_k(gates, K)
        C = int(round(K * T * CAP_RATIO / E))
        e_ord = topi.T.reshape(-1)
        tok_ord = jnp.tile(jnp.arange(T), K)
        oh = jax.nn.one_hot(e_ord, E, dtype=jnp.int32)
        cnt = jnp.take_along_axis(jnp.cumsum(oh, 0) - oh, e_ord[:, None], 1)[:, 0]
        within = cnt < C
        pos = jnp.where(within, cnt, C)
        x_disp = xf[tok_ord]
        buf = jnp.zeros((E, C + 1, D), xf.dtype).at[e_ord, pos].add(x_disp)[:, :C]
        h = jax.nn.gelu(jnp.einsum('ecd,edh->ech', buf, W1) + b1[:, None, :], approximate=False)
        y = jnp.einsum('ech,ehd->ecd', h, W2) + b2[:, None, :]
        y_ord = y[e_ord, jnp.minimum(pos, C - 1)] * within[:, None].astype(y.dtype)
        y_tk = y_ord.reshape(K, T, D).transpose(1, 0, 2)
        cw = topw * within.reshape(K, T).T.astype(topw.dtype)
        out = jnp.einsum('tk,tkd->td', cw, y_tk)
        return out.reshape(B, S, D)
    x = x + _L0_xcond_ref(_layernorm(x, axis=-1), ctx_1024, ctx_1024, condB_tau[:, None], fside_BxS2_0, L0_xcond_Wq, L0_xcond_bq, L0_xcond_Wk, L0_xcond_bk, L0_xcond_Wv, L0_xcond_bv, L0_xcond_Wo, L0_xcond_bo)
    x = x + _L0_ffn_ref(_layernorm(x, axis=-1), L0_ffn_ln_gamma, L0_ffn_ln_beta, L0_ffn_Wr, L0_ffn_W12, L0_ffn_W3)
    x = x + _L1_xcond_ref(_layernorm(x, axis=-1), ctx_1024, ctx_1024, condB_tau[:, None], fside_BxS2_0, L1_xcond_Wq, L1_xcond_bq, L1_xcond_Wk, L1_xcond_bk, L1_xcond_Wv, L1_xcond_bv, L1_xcond_Wo, L1_xcond_bo)
    x = x + _L1_ffn_ref(_layernorm(x, axis=-1), L1_ffn_w1, L1_ffn_conv_w, L1_ffn_conv_b, L1_ffn_w2)
    x = x + _L2_xcond_ref(ctx_1024, _layernorm(x, axis=-1), _lenS2, condB_pt, L2_xcond_W_a, L2_xcond_W_c)
    x = x + _L2_ffn_ref(_layernorm(x, axis=-1), L2_ffn_Wqkv, L2_ffn_q_scale, L2_ffn_k_scale, L2_ffn_Wo, L2_ffn_ln_g, L2_ffn_ln_b, L2_ffn_W1, L2_ffn_b1, L2_ffn_W2, L2_ffn_b2)
    x = x + _L3_xcond_ref(_layernorm(x, axis=-1), ctx_1024, ctx_1024, condB_tau[:, None], fside_BxS2_0, L3_xcond_Wq, L3_xcond_bq, L3_xcond_Wk, L3_xcond_bk, L3_xcond_Wv, L3_xcond_bv, L3_xcond_Wo, L3_xcond_bo)
    x = x + _L3_ffn_ref(_layernorm(x, axis=-1), L3_ffn_Wg, L3_ffn_W1, L3_ffn_b1, L3_ffn_W2, L3_ffn_b2)
    return x

_drawn_inputs = setup_inputs


def setup_inputs(seed=0):
    import zlib

    import numpy as np

    out = dict(_drawn_inputs(seed))
    spreads = {'L0_ffn_ln_gamma': (1.0, 0.6),
     'L0_ffn_ln_beta': (0.0, 0.8),
     'L1_xcond_bq': (0.0, 0.73),
     'L1_xcond_bk': (0.0, 2.0),
     'L1_xcond_bv': (0.0, 0.1),
     'L1_xcond_bo': (0.0, 0.1),
     'L2_ffn_q_scale': (1.0, 0.6),
     'L2_ffn_k_scale': (1.0, 0.6),
     'L2_ffn_ln_g': (1.0, 0.6),
     'L2_ffn_ln_b': (0.0, 0.8),
     'L2_ffn_b1': (0.0, 0.8),
     'L2_ffn_b2': (0.0, 0.1),
     'L3_ffn_b1': (0.0, 0.8),
     'L3_ffn_b2': (0.0, 0.8)}
    factors = {'condB_pt': 8.0,
     'L0_xcond_bq': 8.0,
     'L0_xcond_bk': 200.0,
     'L0_xcond_bv': 6.457,
     'L0_xcond_bo': 7.307,
     'L2_ffn_W1': 4.636,
     'L2_ffn_W2': 4.645,
     'L3_xcond_bq': 200.0,
     'L3_xcond_bk': 200.0,
     'L3_xcond_bv': 22.44,
     'L3_xcond_bo': 30.501,
     'L3_ffn_Wg': 6.922,
     'L3_ffn_W1': 8.0,
     'L3_ffn_W2': 8.0}
    for name, (base, spread) in spreads.items():
        noise = np.random.default_rng([zlib.crc32(name.encode()), seed]).standard_normal(out[name].shape)
        drawn = base * np.exp(spread * noise) if base else spread * noise
        out[name] = jnp.asarray(drawn.astype(out[name].dtype))
    for name, factor in factors.items():
        out[name] = (out[name] * factor).astype(out[name].dtype)
    return out
```

```python
from contextlib import ExitStack

import numpy as np
import concourse.bass as bass
from concourse import mybir

F32 = mybir.dt.float32
BF16 = mybir.dt.bfloat16
I32 = mybir.dt.int32
U32 = mybir.dt.uint32
ALU = mybir.AluOpType
ACT = mybir.ActivationFunctionType
AX = mybir.AxisListType

B, S, D, L = 4, 512, 128, 77
NT = B * S // 128
H = 16
E = 8
DEPTH = 6
CAP0 = 640
CAP3 = 538
ROUND = float(3 << 22)
NEG = -1.0e30
ENGINES = ("tensor", "vector", "scalar", "gpsimd", "sync")


class Program:

    def __init__(self, nc, ctx):
        self.nc, self.ctx = nc, ctx
        self.queue = {e: [] for e in ENGINES}
        self.sems, self.count = {}, {}
        for e in ENGINES:
            self.semaphore(e)

    def semaphore(self, name):
        self.sems[name] = self.ctx.enter_context(self.nc.semaphore("s_" + name))
        self.count[name] = 0

    def step(self, engine, fn, after):
        self.count[engine] += 1
        self.queue[engine].append((fn, list(flat(after)), engine, 1))
        return (engine, self.count[engine])

    def pe(self, fn, *after):
        return self.step("tensor", fn, after)

    def dve(self, fn, *after):
        return self.step("vector", fn, after)

    def act(self, fn, *after):
        return self.step("scalar", fn, after)

    def pool(self, fn, *after):
        return self.step("gpsimd", fn, after)

    def load(self, group, out, in_, *after, engine="sync"):
        if group not in self.sems:
            self.semaphore(group)
        self.count[group] += 16
        self.queue[engine].append((lambda e: e.dma_start(out, in_), list(flat(after)), group, 16))

    def loaded(self, group):
        return (group, self.count[group])

    def barrier(self):
        now = [(e, self.count[e]) for e in ENGINES[:4]]
        for e in ENGINES:
            self.queue[e].append((None, now, None, 0))
        return now

    def emit(self, engine, eng):
        seen = {}
        for fn, after, sem, by in self.queue[engine]:
            for name, value in after:
                if seen.get(name, 0) < value:
                    eng.wait_ge(self.sems[name], value)
                    seen[name] = value
            if fn is not None:
                fn(eng).then_inc(self.sems[sem], by)


def flat(tokens):
    for t in tokens:
        if t is None:
            continue
        if isinstance(t, list):
            yield from flat(t)
        else:
            yield t


def matmuls(*group):
    def run(e):
        for out, lhsT, rhs, start, stop in group:
            last = e.matmul(out, lhsT, rhs, start=start, stop=stop, skip_group_check=True)
        return last
    return run


def transposes(*group):
    def run(e):
        for out, in_, ident in group:
            last = e.transpose(out, in_, ident)
        return last
    return run


def bc(ap, axis, n):
    ap = ap.unsqueeze(axis)
    shape = list(ap.shape)
    shape[axis] = n
    return ap.to_broadcast(shape)


def build(nc, d, kept, out, stages):
    ctx = ExitStack()
    with ctx:
        P = Program(nc, ctx)
        WORDS = 51600
        mem = ctx.enter_context(nc.sbuf_tensor("mem", [128, WORDS], F32))
        ps = ctx.enter_context(nc.psum_tensor("ps", [128, 8, 512], F32))
        at = [0]

        def words(n):
            a = at[0]
            at[0] += n
            assert at[0] <= WORDS, at[0]
            return mem[:, a:a + n]

        def view(ap, pat, **k):
            return ap.rearrange(pat, **k)

        def tile3(a, b):
            return view(words(a * b), "p (a b) -> p a b", a=a)

        def tile4(a, b, c):
            return view(words(a * b * c), "p (a b c) -> p a b c", a=a, b=b)

        X = tile3(NT, D)
        XN = tile3(NT, D)
        xT = tile3(B, 32 + S)
        ident = words(128)
        onesf = words(128)
        lower = words(128)
        shiftm = words(128)
        carrym = words(128)
        ones3 = words(64).bitcast(BF16)
        hm = words(H)
        iota8 = words(E)
        identb = words(64).bitcast(BF16)
        maskb = view(words(512).bitcast(BF16), "p (m c) -> p m c", m=2)
        rotc = tile4(4, 2, 64)
        rots = tile4(4, 2, 64)
        ctxT = tile3(B, L)
        ctxk = tile3(B, D)
        tauB = words(B)
        ptB = words(B)
        lenI = words(B).bitcast(I32)
        lenB = words(B)
        idx = words(L)
        sel3 = words(3)
        dl3 = view(words(2 * 4 * L).bitcast(BF16), "p (a b c) -> p a b c", a=B, b=4)
        st = tile3(NT, 6)
        mv = tile3(NT, 2)
        va, rs, rt = words(NT), words(NT), words(NT)
        xw = {}

        def xweights(n):
            xw[n] = {k: words(128) for k in ("Wq", "Wk", "Wv", "Wo", "bv", "bo")}
            xw[n].update({k: words(1) for k in ("bq", "bk")})

        xweights("3")
        WgT = words(E)
        l2 = []
        for _ in range(2):
            l2.append(dict(Wqkv=words(3072), Wo=tile3(8, 128), W1=words(682), W2=tile3(3, 128), b1=words(6),
                           g=words(1), b=words(1), b2=words(128), qs=tile3(2, 64)))
        base5 = at[0]
        xweights("0")
        xweights("1")
        w1T, w2T = words(512), tile3(4, 128)
        cvw, cvb = tile3(4, 3), words(4)
        Wa, WcT = words(128), tile3(2, 128)
        lng, lnb = words(1), words(1)
        WrT = words(E)
        base = at[0]
        masks = tile3(2, 64)
        dlf, dl1, dlt = tile3(B, L), tile3(B, L), tile3(B, L)
        dlh = view(words(3 * 2 * L).bitcast(BF16), "p (a b c) -> p a b c", a=3, b=B)

        free = {b: None for b in range(8)}

        g = "first"
        P.load(g, X, d["x"].rearrange("(t p) d -> p t d", p=128))
        P.load(g, ident, d["ident"])
        for t, n in ((ctxT, "ctxT"), (lower, "lower"), (shiftm, "shiftm"), (carrym, "carrym"), (hm, "hm"),
                     (rotc, "rotc"), (rots, "rots"), (masks, "masks")):
            P.load(g, t, d[n])
        P.load(g, ctxk[0:L], d["ctxk"])
        P.load(g, tauB, d["tau"].partition_broadcast(128))
        P.load(g, ptB, d["pt"].partition_broadcast(128))
        P.load(g, lenI, d["len"].partition_broadcast(128))
        P.load(g, idx, d["idx"].partition_broadcast(128))
        P.load(g, iota8, d["idx"][0:E].partition_broadcast(128))
        P.load(g, sel3[0:3], d["sel3"])
        P.load(g, dlf[0:3], d["delta"].partition_broadcast(3))
        for n in "013":
            g = "xw" + n
            for k in ("Wq", "Wk", "Wv", "Wo"):
                P.load(g, xw[n][k], d[f"L{n}{k}"])
            for k in ("bq", "bk"):
                P.load(g, xw[n][k], d[f"L{n}{k}"])
            for k in ("bv", "bo"):
                P.load(g, xw[n][k][0:1], d[f"L{n}{k}"])
        g = "small"
        for t, n in ((w1T, "w1T"), (w2T, "w2T"), (cvw, "cvw"), (cvb, "cvb"), (Wa, "Wa"), (WcT, "WcT"), (lng, "lng"),
                     (lnb, "lnb"), (WrT, "WrT"), (WgT, "WgT")):
            P.load(g, t, d[n])

        def load_l2(i, *after):
            w, g = l2[i % 2], f"l2_{i}"
            P.load(g, w["Wqkv"], d["Wqkv"][i], *after)
            P.load(g, w["Wo"], d["L2Wo"][i])
            P.load(g, w["W1"], d["W1"][i])
            P.load(g, w["W2"][:, 0:2, :], d["W2"][i, 0:256, :].rearrange("(c p) n -> p c n", p=128))
            P.load(g, w["W2"][0:85, 2, :], d["W2"][i, 256:341, :])
            P.load(g, w["b1"], d["b1"][i])
            P.load(g, w["g"], d["ln_g"][i])
            P.load(g, w["b"], d["ln_b"][i])
            P.load(g, w["b2"][0:1], d["b2"][i])
            P.load(g, w["qs"], d["qks"][i].partition_broadcast(128))

        load_l2(0)
        load_l2(1)
        first, small = P.loaded("first"), P.loaded("small")

        c_ones = P.pool(lambda e: e.memset(onesf, 1.0))
        c_pad = P.pool(lambda e: e.memset(xT[:, :, 0:32], 0.0))
        c_ones3 = P.dve(lambda e: e.memset(ones3, 1.0))
        c_idb = P.dve(lambda e: e.tensor_copy(identb, ident), first)
        c_mask = [P.dve(lambda e, m=m: e.tensor_copy(view(maskb[:, m, :], "p (a k) -> p a k", a=8),
                                                     bc(masks[:, m, :], 1, 8)), first) for m in range(2)]
        c_tau = P.dve(lambda e: e.tensor_scalar(tauB, tauB, float(np.float32(1 / np.sqrt(8.0))), None, ALU.mult), first)
        c_len = P.dve(lambda e: e.tensor_copy(lenB, lenI), first)
        q3 = slice(0, 3)
        t = P.dve(lambda e: e.tensor_scalar(dl1[q3], dlf[q3], float(np.float32(1 / np.sqrt(8.0))), None, ALU.mult), first)
        for j in range(3):
            t = P.dve(lambda e, j=j: e.tensor_copy(dlh[q3, j], dl1[q3]), t)
            if j < 2:
                t = P.dve(lambda e, j=j: e.tensor_tensor(dl1[q3], dl1[q3], dlh[q3, j], ALU.subtract), t)
        t = P.dve(lambda e: e.tensor_scalar(dlt[q3], dlh[q3, 0], sel3[q3, 0:1], None, ALU.mult), t)
        for j in (1, 2):
            t = P.dve(lambda e, j=j: e.scalar_tensor_tensor(dlt[q3], dlh[q3, j], sel3[q3, j:j + 1], dlt[q3],
                                                            ALU.mult, ALU.add), t)
        for h in range(4):
            c_dl = P.dve(lambda e, h=h: e.tensor_copy(dl3[q3, :, h, :], dlt[q3]), t)
        P.barrier()

        def rsqrt(y, a, tmp, *after):
            yi, ai = y.bitcast(I32), a.bitcast(I32)
            t = P.dve(lambda e: e.tensor_scalar(yi, ai, 1, None, ALU.arith_shift_right), *after)
            t = P.dve(lambda e: e.tensor_scalar(yi, yi, -1.0, float(0x5F3759DF), ALU.mult, ALU.add), t)
            for _ in range(3):
                t = P.dve(lambda e: e.tensor_tensor(tmp, y, y, ALU.mult), t)
                t = P.dve(lambda e: e.scalar_tensor_tensor(tmp, tmp, -0.5, a, ALU.mult, ALU.mult), t)
                t = P.dve(lambda e: e.scalar_tensor_tensor(y, tmp, 1.5, y, ALU.add, ALU.mult), t)
            return t

        def layernorm(src, dst, *after, before_write=None):
            for i in range(NT):
                a = P.dve(lambda e, i=i: e.bn_stats(st[:, i, :], src[:, i, :]), *after)
            for i in range(NT):
                a = P.dve(lambda e, i=i: e.bn_aggr(mv[:, i, :], st[:, i, :]), a)
            a = P.dve(lambda e: e.tensor_scalar(va, mv[:, :, 1], 1e-5, None, ALU.add), a)
            a = rsqrt(rs, va, rt, a)
            return [P.dve(lambda e, i=i: e.tensor_scalar(dst[:, i, :], src[:, i, :], mv[:, i, 0:1], rs[:, i:i + 1],
                                                         ALU.subtract, ALU.mult), a, before_write) for i in range(NT)]

        def turn(src, ready, bank, evac):
            got = []
            for b in range(B):
                k = bank[b % len(bank)]
                t = P.pe(transposes(*[(ps[:, k, 128 * j:128 * j + 128], src[:, 4 * b + j, :], ident)
                                      for j in range(4)]), ready[4 * b:4 * b + 4], free[k])
                free[k] = evac(b, ps[:, k, :], t)
                got.append(free[k])
            return got

        def to_xT(b, p, t):
            return P.act(lambda e: e.activation(xT[:, b, 32:32 + S], p, ACT.Copy), t)

        def chunk(b):
            return xT[:, b, 32:32 + S]

        def tokens(i):
            return xT[:, i // 4, 32 + 128 * (i % 4):160 + 128 * (i % 4)]

        def add_rows(b, k, t):
            free[k] = P.dve(lambda e: e.tensor_tensor(X[:, 4 * b:4 * b + 4, :], X[:, 4 * b:4 * b + 4, :],
                                                      view(ps[:, k, :], "p (a c) -> p a c", a=4), ALU.add), t)
            return free[k]

        def xcond(n):
            at[0] = base + 12288
            w, wl = xw[n], P.loaded("xw" + n)
            kTs = words(B * L)
            kbd = tile4(B, H, L)
            vx = tile4(B, H, 9)
            qT = tile3(B, S)
            pb = [words(8 * L) for _ in range(2)]
            pts = [tile3(8, 128) for _ in range(2)]
            mx = [words(8) for _ in range(2)]
            rc = [words(H) for _ in range(2)]
            att = XN
            oT = words(512)

            ln = layernorm(X, XN)
            t = P.pe(matmuls((ps[:, 7, 0:B * L], w["Wk"], view(ctxT, "p b l -> p (b l)"), True, True)), wl, free[7])
            k = P.act(lambda e: e.activation(kTs, ps[:, 7, 0:B * L], ACT.Identity, bias=w["bk"]), t)
            free[7] = k
            t = P.pe(matmuls(*[m for b in range(B) for m in (
                (ps[0:L, 6, 128 * b:128 * b + 128], ctxT[:, b, :], w["Wv"], True, False),
                (ps[0:L, 6, 128 * b:128 * b + 128], onesf[0:1, 0:L], w["bv"][0:1], False, True))]), wl, free[6])
            v1 = P.pool(lambda e: e.memset(vx[0:L, :, :, 8:9], 1.0))
            v = P.act(lambda e: e.activation(view(vx, "p b h e -> p (b h) e")[0:L, :, 0:8],
                                             view(ps[0:L, 6, :], "p (a c) -> p a c", c=8), ACT.Copy), t)
            free[6] = v
            kb = [P.pool(lambda e, b=b: e.tensor_tensor(kbd[:, b], bc(kTs[:, b * L:b * L + L], 1, H), bc(hm, 2, L),
                                                        ALU.mult), k) for b in range(B)]
            xt = turn(XN, ln, (6, 7), to_xT)
            q = []
            for b in range(B):
                f = 6 + b % 2
                t = P.pe(matmuls((ps[:, f, :], w["Wq"], chunk(b), True, True)), xt[b], free[f])
                free[f] = P.dve(lambda e, b=b, f=f: e.tensor_scalar(qT[:, b, :], ps[:, f, :], w["bq"], tauB[:, b:b + 1],
                                                                    ALU.add, ALU.mult), t)
                q.append(free[f])

            NU = 2 * NT
            scored, exped, attd, sub_done = {}, {}, {}, {}
            pb_free, pts_free, rc_free = [None, None], [None, None], [None, None]

            def score(u):
                i, hf, r = u // 2, u % 2, u % 2
                b = i // 4
                ms = []
                for j in range(2):
                    o = ps[:, 2 * r + j, 0:4 * L]
                    h0 = 8 * hf + 4 * j
                    ms += [(o, ones3[0:3, 0:128], view(dl3[0:3, b], "p h l -> p (h l)"), True, False),
                           (o, qT[:, b, 128 * (i % 4):128 * (i % 4) + 128],
                            view(kbd[:, b, h0:h0 + 4, :], "p h l -> p (h l)"), False, True)]
                scored[u] = P.pe(matmuls(*ms), q[b], kb[b], free[2 * r])

            def soft(u):
                r = u % 2
                sc = view(ps[:, 2 * r:2 * r + 2, 0:4 * L], "p a (h l) -> p a h l", h=4)
                m = view(mx[r], "p (a h) -> p a h", a=2)
                o = view(pb[r], "p (a h l) -> p a h l", a=2, h=4)
                t = P.dve(lambda e: e.tensor_reduce(m, sc, AX.X, ALU.max), scored[u])
                t = P.dve(lambda e: e.tensor_tensor(o, sc, bc(m, 3, L), ALU.subtract), t, pb_free[r])
                free[2 * r] = t
                exped[u] = P.act(lambda e: e.activation(pb[r], pb[r], ACT.Exp), t)

            def values(u):
                i, hf, r = u // 2, u % 2, u % 2
                b = i // 4
                pw = []
                for j in range(2):
                    k = 4 + j
                    t = P.pe(transposes(*[(ps[0:L, k, 128 * h:128 * h + 128],
                                           pb[r][:, (4 * j + h) * L:(4 * j + h + 1) * L], ident)
                                          for h in range(4)]), exped[u], free[k])
                    if j == 1:
                        pb_free[r] = t
                    o, s = view(pts[r][0:L, 4 * j:4 * j + 4, :], "p h c -> p (h c)"), ps[0:L, k, :]
                    if j == 0:
                        free[k] = P.act(lambda e, o=o, s=s: e.activation(o, s, ACT.Copy), t, pts_free[r])
                    else:
                        free[k] = P.dve(lambda e, o=o, s=s: e.tensor_copy(o, s), t, pts_free[r])
                    pw.append(free[k])
                av = view(ps[:, 6, 0:288], "p (a h c) -> p a h c", a=2, h=H)
                t = P.pe(matmuls(*[(av[:, i % 2, 8 * hf + h, :], pts[r][0:L, h, :], vx[0:L, b, 8 * hf + h, :], True, True)
                                   for h in range(8)]), pw, v, v1, attd.get(i - 2), free[6])
                pts_free[r] = t
                if hf == 1:
                    z = i % 2
                    t = P.dve(lambda e: e.reciprocal(rc[z], av[:, z, :, 8]), t)
                    attd[i] = P.dve(lambda e: e.tensor_tensor(view(att[:, i, :], "p (h c) -> p h c", h=H),
                                                              av[:, z, :, 0:8], bc(rc[z], 2, 8), ALU.mult), t)

            def project(b):
                t = P.pe(transposes(*[(ps[:, 7, 128 * j:128 * j + 128], att[:, 4 * b + j, :], ident)
                                      for j in range(4)]), attd[4 * b + 3], free[7])
                t = P.act(lambda e: e.activation(oT, ps[:, 7, :], ACT.Copy), t)
                t = P.pe(matmuls(*[m for j in range(4) for m in (
                    (ps[:, 7, 128 * j:128 * j + 128], oT[:, 128 * j:128 * j + 128], w["Wo"], True, False),
                    (ps[:, 7, 128 * j:128 * j + 128], onesf[0:1, :], w["bo"][0:1], False, True))]), t)
                add_rows(b, 7, t)

            for u in range(NU + 3):
                if u < NU:
                    score(u)
                    soft(u)
                if 1 <= u <= NU:
                    values(u - 1)
                if u >= 10 and (u - 10) % 8 == 0 and (u - 10) // 8 < B:
                    project((u - 10) // 8)
            P.barrier()
            free[6] = None

        def gates(probs, gate, k_major, cap, *after):
            m8, ix, ixf = tile3(NT, 8), tile3(NT, 8), tile3(2, NT)
            oh = tile4(2, NT, E)
            a, c, kept = tile4(2, NT, E), tile4(2, NT, E), tile4(2, NT, E)
            pre = tile4(2, NT, E)
            iu = ix.bitcast(U32)
            for i in range(NT):
                t = P.dve(lambda e, i=i: e.max(m8[:, i, :], probs[:, i, :]), *after)
            for i in range(NT):
                t = P.dve(lambda e, i=i: e.max_index(iu[:, i, :], m8[:, i, :], probs[:, i, :]), t)
            for k in range(2):
                t2 = P.dve(lambda e, k=k: e.tensor_copy(ixf[:, k, :], iu[:, :, k]), t)
            for k in range(2):
                t = P.dve(lambda e, k=k: e.tensor_tensor(oh[:, k], bc(iota8, 1, NT), bc(ixf[:, k, :], 2, E),
                                                         ALU.is_equal), t2)
            n = 2 * NT * E
            fl = lambda z: view(z, "p k t e -> p (k t e)")
            t = P.pe(matmuls((ps[:, 0, 0:n], lower, fl(oh), True, True),
                             (ps[:, 1, 0:n], onesf, fl(oh), True, True)), t, free[0], free[1])
            x1 = P.dve(lambda e: e.tensor_copy(fl(pre), ps[:, 0, 0:n]), t)
            t = P.dve(lambda e: e.tensor_copy(fl(a), ps[:, 1, 0:n]), t)
            free[0] = free[1] = t
            src, dst = a, c
            for s in (1, 2, 4, 8):
                t1 = P.dve(lambda e, s=s, o=dst, i=src: e.tensor_tensor(o[:, :, s:, :], i[:, :, s:, :], i[:, :, :NT - s, :],
                                                                      ALU.add), t)
                t = P.dve(lambda e, s=s, o=dst, i=src: e.tensor_copy(o[:, :, :s, :], i[:, :, :s, :]), t)
                src, dst = dst, src
            assert src is a
            t = P.dve(lambda e: e.tensor_tensor(fl(pre), fl(pre), fl(a), ALU.add), t, x1)
            t = P.dve(lambda e: e.tensor_tensor(fl(pre), fl(pre), ps[:, 1, 0:n], ALU.subtract), t)
            free[1] = t
            r0, r1 = pre[:, 0], pre[:, 1]
            if k_major:
                t = P.dve(lambda e: e.tensor_tensor(r1, r1, bc(a[:, 0, NT - 1, :], 1, NT), ALU.add), t)
            else:
                t = P.dve(lambda e: e.tensor_tensor(r0, r0, r1, ALU.add), t)
                t = P.dve(lambda e: e.tensor_copy(r1, r0), t)
            t = P.dve(lambda e: e.tensor_scalar(fl(kept), fl(pre), float(cap), None, ALU.is_lt), t)
            t = P.dve(lambda e: e.tensor_tensor(fl(kept), fl(kept), fl(oh), ALU.mult), t)
            for k in range(2):
                t2 = P.dve(lambda e, k=k: e.tensor_tensor(kept[:, k], kept[:, k], bc(m8[:, :, k], 2, E), ALU.mult), t)
            return P.dve(lambda e: e.tensor_tensor(gate, kept[:, 0], kept[:, 1], ALU.add), t2)

        def softmax8(lg, probs, eps, *after):
            m, s = words(NT), words(NT)
            t = P.dve(lambda e: e.tensor_reduce(m, lg, AX.X, ALU.max), *after)
            t = P.dve(lambda e: e.tensor_tensor(probs, lg, bc(m, 2, E), ALU.subtract), t)
            t = P.act(lambda e: e.activation(probs, probs, ACT.Exp), t)
            t = P.dve(lambda e: e.tensor_reduce(s, probs, AX.X, ALU.add), t)
            if eps:
                t = P.dve(lambda e: e.tensor_scalar(s, s, eps, None, ALU.add), t)
            t = P.dve(lambda e: e.reciprocal(s, s), t)
            return P.dve(lambda e: e.tensor_tensor(probs, probs, bc(s, 2, E), ALU.mult), t)

        def router(wT, lg, xt, lo, hi):
            t = P.pe(matmuls(*[(ps[:, 2, E * i:E * i + E], tokens(i), wT, True, True) for i in range(NT)]), xt, small, free[2])
            free[2] = P.dve(lambda e: e.tensor_scalar(lg, view(ps[:, 2, 0:NT * E], "p (t e) -> p t e", e=E), lo, hi,
                                                      ALU.max, ALU.min), t)
            return free[2]

        def experts(up, ups, down, bias, ready):
            hT = [tile3(4, 512) for _ in range(2)]
            hfree = [None, None]
            added = {}
            jobs = [(b, e) for b in range(B) for e in range(E)]
            hid = {}

            def y(n):
                b, e = jobs[n]
                k = 6 + n % 2
                ms = []
                for j in range(4):
                    o = ps[:, k, 128 * j:128 * j + 128]
                    ms += [(o, hT[n % 2][:, c, 128 * j:128 * j + 128], down[:, e, c, :], c == 0, c == 3 and bias is None)
                           for c in range(4)]
                    if bias is not None:
                        ms.append((o, onesf[0:1, :], bias[0:1, e, :], False, True))
                t = P.pe(matmuls(*ms), hid[n], free[k])
                hfree[n % 2] = t
                for j in range(4):
                    i = 4 * b + j
                    t2 = P.dve(lambda en, i=i, j=j, k=k: en.scalar_tensor_tensor(
                        X[:, i, :], ps[:, k, 128 * j:128 * j + 128], ready[1][:, i, e:e + 1], X[:, i, :],
                        ALU.mult, ALU.add), t, ready[0], added.get(i))
                    added[i] = t2
                free[k] = t2

            cell = [0]
            for n in range(len(jobs) + 1):
                if n < len(jobs):
                    b, e = jobs[n]
                    toks = []
                    for c in range(4):
                        toks.append(up(e, c, b, hT[n % 2][:, c, :], cell[0], hfree[n % 2]))
                        cell[0] += 1
                    hid[n] = toks
                if n >= 1:
                    y(n - 1)

        def l0_ffn():
            at[0] = base
            W12 = tile3(E, 1024)
            W3 = tile4(E, 4, 128)
            lg, probs, gate = tile3(NT, E), tile3(NT, E), tile3(NT, E)
            sg = [words(512) for _ in range(3)]
            sgf = [None] * 3
            wl = P.loaded("moe0")
            ln = layernorm(X, XN)
            ln = layernorm(XN, XN, ln)

            def affine(b, p, t):
                return P.act(lambda e: e.activation(chunk(b), p, ACT.Identity, bias=lnb, scale=lng), t, small)

            xt = turn(XN, ln, (6, 7), affine)
            t = router(WrT, lg, xt, -10000.0, 10000.0)
            t = softmax8(lg, probs, 1e-12, t)
            gt = gates(probs, gate, False, CAP0, t)

            def up(e, c, b, o, cell, hfree):
                r = cell % 3
                k = 2 * r
                t = P.pe(matmuls((ps[:, k, :], W12[:, e, 128 * c:128 * c + 128], chunk(b), True, True),
                                 (ps[:, k + 1, :], W12[:, e, 512 + 128 * c:640 + 128 * c], chunk(b), True, True)),
                         xt[b], wl, free[k], free[k + 1])
                a = P.act(lambda en: en.activation(sg[r], ps[:, k, :], ACT.Silu), t, sgf[r])
                m = P.dve(lambda en: en.tensor_tensor(o, ps[:, k + 1, :], sg[r], ALU.mult), a, hfree)
                sgf[r] = free[k] = free[k + 1] = m
                return m

            experts(up, 2, W3, None, (gt, gate))
            P.barrier()

        def l3_ffn():
            at[0] = base
            W1 = tile3(E, 512)
            W2 = tile4(E, 4, 128)
            b1 = tile3(E, 4)
            b2 = tile3(E, 128)
            at[0] = max(at[0], base + 12288)
            lg, probs, gate = tile3(NT, E), tile3(NT, E), tile3(NT, E)
            wl = P.loaded("moe3")
            ln = layernorm(X, XN)
            xt = turn(XN, ln, (6, 7), to_xT)
            t = router(WgT, lg, xt, -3.0e38, 3.0e38)
            t = softmax8(lg, probs, 0.0, t)
            gt = gates(probs, gate, True, CAP3, t)

            def up(e, c, b, o, cell, hfree):
                k = cell % 6
                t = P.pe(matmuls((ps[:, k, :], W1[:, e, 128 * c:128 * c + 128], chunk(b), True, True)), xt[b], wl, free[k])
                free[k] = P.act(lambda en: en.activation(o, ps[:, k, :], ACT.Gelu, bias=b1[:, e, c:c + 1]), t, hfree)
                return free[k]

            experts(up, 1, W2, b2, (gt, gate))
            P.barrier()

        def load_moe0():
            at[0] = base
            W12 = tile3(E, 1024)
            W3 = tile4(E, 4, 128)
            for e in range(E):
                P.load("moe0", W12[:, e, :], d["W12T"][e])
                P.load("moe0", W3[:, e], d["W3T"][e])

        def load_moe3():
            at[0] = base
            W1 = tile3(E, 512)
            W2 = tile4(E, 4, 128)
            b1 = tile3(E, 4)
            b2 = tile3(E, 128)
            for e in range(E):
                P.load("moe3", W1[:, e, :], d["L3W1"][e])
                P.load("moe3", W2[:, e], d["L3W2"][e].rearrange("(c p) n -> p c n", p=128))
            P.load("moe3", b1, d["L3b1"])
            P.load("moe3", b2[0:1], d["L3b2"])

        def l1_ffn():
            at[0] = base
            hp = tile4(B, 4, S + 2)
            y = tile4(4, B, S)
            hs = view(view(hp, "p b c s -> p b (c s)")[:, :, 0:2048], "p b (t c) -> p b t c", t=4)
            q2 = view(y, "p a b c -> p (a b c)")[:, 0:4096].bitcast(BF16)
            q2 = view(q2, "p (t c) -> p t c", t=NT)
            q2T = view(words(2 * 256).bitcast(BF16), "p (r c n) -> p r c n", r=2, c=4)
            amax, sc1, inv = words(NT), words(NT), words(NT)
            wq1 = words(512)
            wq2 = view(words(256).bitcast(BF16), "p (c n) -> p c n", c=4)
            wt = words(512)
            ws, wm, wr = words(2), words(2), words(2)

            ln = layernorm(X, XN)
            w2f = view(w2T, "p c n -> p (c n)")
            t = P.dve(lambda e: e.tensor_reduce(ws[:, 0:1], w1T, AX.X, ALU.add, apply_absolute_value=True), small)
            t = P.dve(lambda e: e.tensor_reduce(ws[:, 1:2], w2f, AX.X, ALU.add, apply_absolute_value=True), small)
            t = P.pe(matmuls((ps[:, 0, 0:2], onesf, ws, True, True)), t, free[0])
            t = P.dve(lambda e: e.tensor_scalar(wm, ps[:, 0, 0:2], 1.0 / 65536, 1e-5, ALU.mult, ALU.max), t)
            free[0] = t
            wmt = t
            t = P.dve(lambda e: e.reciprocal(wr, wm), t)
            a = P.dve(lambda e: e.tensor_scalar(wt, w1T, wr[:, 0:1], ROUND, ALU.mult, ALU.add), t)
            a = P.dve(lambda e: e.tensor_scalar(wt, wt, ROUND, -1.0, ALU.subtract, ALU.max), a)
            w1d = P.dve(lambda e: e.tensor_scalar(wq1, wt, 1.0, wm[:, 0:1], ALU.min, ALU.mult), a)
            a = P.dve(lambda e: e.tensor_scalar(wt, w2f, wr[:, 1:2], ROUND, ALU.mult, ALU.add), w1d)
            a = P.dve(lambda e: e.tensor_scalar(wt, wt, ROUND, -1.0, ALU.subtract, ALU.max), a)
            w2d = P.dve(lambda e: e.tensor_scalar(view(wq2, "p c n -> p (c n)"), wt, 1.0, None, ALU.min), a)

            def scales(src, *after):
                o = amax if len(src.shape) == 3 else view(amax, "p (b t) -> p b t", b=B)
                t = P.dve(lambda e: e.tensor_reduce(o, src, AX.X, ALU.max, apply_absolute_value=True), *after)
                t = P.dve(lambda e: e.tensor_scalar(amax, amax, 1e-5, None, ALU.max), t)
                t1 = P.dve(lambda e: e.tensor_scalar(inv, amax, 1.0 / 127, None, ALU.mult), t)
                t = P.dve(lambda e: e.reciprocal(sc1, amax), t)
                return P.dve(lambda e: e.tensor_scalar(sc1, sc1, 127.0, None, ALU.mult), t), t1

            t = scales(XN, ln)[0]
            rows = []
            a = [P.dve(lambda e, i=i: e.tensor_scalar(XN[:, i, :], XN[:, i, :], sc1[:, i:i + 1], ROUND,
                                                      ALU.mult, ALU.add), t) for i in range(NT)]
            a = [P.dve(lambda e, i=i: e.tensor_scalar(XN[:, i, :], XN[:, i, :], ROUND, -128.0,
                                                      ALU.subtract, ALU.max), a[i]) for i in range(NT)]
            rows = [P.dve(lambda e, i=i: e.tensor_scalar(XN[:, i, :], XN[:, i, :], 127.0, inv[:, i:i + 1],
                                                         ALU.min, ALU.mult), a[i]) for i in range(NT)]
            xt = turn(XN, rows, (6, 7), to_xT)
            pads = [P.pool(lambda e, s=s: e.memset(hp[:, :, :, s:s + 1], 0.0)) for s in (0, S + 1)]
            silu = {}
            n = 0
            hsd = {}

            def back(b):
                out = []
                for j in range(4):
                    i = 4 * b + j
                    k = 4 + i % 2
                    t = P.pe(transposes(*[(ps[:, k, 128 * c:128 * c + 128], y[:, c, b, 128 * j:128 * j + 128], ident)
                                          for c in range(4)]), [silu[(b, c)] for c in range(4)], free[k])
                    free[k] = P.act(lambda e, i=i, k=k: e.activation(hs[:, i // 4, i % 4, :], ps[:, k, :], ACT.Copy), t)
                    out.append(free[k])
                hsd[b] = out

            for b in range(B):
                for c in range(4):
                    k = n % 4
                    n += 1
                    t = P.pe(matmuls((ps[:, k, :], wq1[:, 128 * c:128 * c + 128], chunk(b), True, True)), xt[b], w1d, free[k])
                    t = P.act(lambda e, b=b, c=c, k=k: e.activation(hp[:, b, c, 1:S + 1], ps[:, k, :], ACT.Copy), t)
                    free[k] = t
                    o = y[:, c, b, :]
                    t = P.dve(lambda e, o=o, b=b, c=c: e.tensor_scalar(o, hp[:, b, c, 0:S], cvw[:, c, 0:1], cvb[:, c:c + 1],
                                                                       ALU.mult, ALU.add), t, pads)
                    for s in (1, 2):
                        t = P.dve(lambda e, o=o, b=b, c=c, s=s: e.scalar_tensor_tensor(
                            o, hp[:, b, c, s:s + S], cvw[:, c, s:s + 1], o, ALU.mult, ALU.add), t)
                    silu[(b, c)] = P.act(lambda e, o=o: e.activation(o, o, ACT.Silu), t)
                if b >= 1:
                    back(b - 1)
            back(B - 1)
            t = scales(hs, [hsd[b] for b in range(B)])
            inv2 = P.dve(lambda e: e.tensor_scalar(inv, inv, wm[:, 1:2], None, ALU.mult), t[1])
            a = [P.dve(lambda e, i=i: e.tensor_scalar(hs[:, i // 4, i % 4, :], hs[:, i // 4, i % 4, :], sc1[:, i:i + 1], ROUND,
                                                      ALU.mult, ALU.add), t[0]) for i in range(NT)]
            a = [P.dve(lambda e, i=i: e.tensor_scalar(hs[:, i // 4, i % 4, :], hs[:, i // 4, i % 4, :], ROUND, -128.0,
                                                      ALU.subtract, ALU.max), a[i]) for i in range(NT)]
            rows = [P.dve(lambda e, i=i: e.tensor_scalar(q2[:, i, :], hs[:, i // 4, i % 4, :], 127.0, None, ALU.min), a[i],
                          [hsd[b] for b in range(B)]) for i in range(NT)]
            qf = [None, None]
            for i in range(NT):
                r = i % 2
                pt = ps[:, 4 + r, 0:256].bitcast(BF16)
                t = P.pe(transposes(*[(pt[:, 128 * c:128 * c + 128], q2[:, i, 128 * c:128 * c + 128], identb)
                                      for c in range(4)]), rows[i], free[4 + r])
                t = P.act(lambda e, r=r, pt=pt: e.activation(view(q2T[:, r], "p c n -> p (c n)"), pt, ACT.Copy), t, qf[r])
                free[4 + r] = t
                k = 6 + r
                t = P.pe(matmuls(*[(ps[:, k, 0:128], q2T[:, r, c, :], wq2[:, c, :], c == 0, c == 3) for c in range(4)]),
                         t, w2d, free[k])
                qf[r] = t
                free[k] = P.dve(lambda e, i=i, k=k: e.scalar_tensor_tensor(X[:, i, :], ps[:, k, 0:128], inv[:, i:i + 1],
                                                                           X[:, i, :], ALU.mult, ALU.add), t, inv2)
            P.barrier()

        def l2_xcond():
            at[0] = base
            st_, en_ = words(B), words(B)
            m1, keep, neg, gs = tile3(B, L), tile3(B, L), tile3(B, L), tile3(B, L)
            zT = tile3(B, S)
            sb = [words(L) for _ in range(2)]
            mx = words(NT)
            sm = words(NT)
            pT = [words(512) for _ in range(2)]
            cT = [words(512) for _ in range(2)]
            th = [words(512) for _ in range(2)]
            ln = layernorm(X, XN)
            ib = bc(idx, 1, B)
            t = P.dve(lambda e: e.tensor_scalar(st_, ptB, 16.0, 0.0, ALU.subtract, ALU.max))
            t2 = P.dve(lambda e: e.tensor_scalar(en_, ptB, 16.0, None, ALU.add))
            t2 = P.dve(lambda e: e.tensor_tensor(en_, en_, lenB, ALU.min), t2)
            t = P.dve(lambda e: e.tensor_tensor(m1, ib, bc(st_, 2, L), ALU.is_lt), t)
            t2 = P.dve(lambda e: e.tensor_tensor(neg, ib, bc(en_, 2, L), ALU.is_gt), t2)
            t = P.dve(lambda e: e.tensor_tensor(m1, m1, neg, ALU.max), t, t2)
            t1 = P.dve(lambda e: e.tensor_scalar(keep, m1, -1.0, 1.0, ALU.mult, ALU.add), t)
            t2 = P.dve(lambda e: e.tensor_scalar(neg, m1, -1.0e9, None, ALU.mult), t)
            t = P.dve(lambda e: e.tensor_tensor(gs, ib, bc(ptB, 2, L), ALU.subtract))
            t = P.act(lambda e: e.activation(gs, gs, ACT.Square), t)
            gd = P.act(lambda e: e.activation(gs, gs, ACT.Exp, scale=-1.0 / 128), t)
            xt = turn(XN, ln, (6, 7), to_xT)
            z = []
            for b in range(B):
                k = 6 + b % 2
                t = P.pe(matmuls((ps[:, k, :], Wa, chunk(b), True, True)), xt[b], small, free[k])
                free[k] = P.act(lambda e, b=b, k=k: e.activation(zT[:, b, :], ps[:, k, :], ACT.Copy), t)
                z.append(free[k])
            sc, sf, pTf, cTf, thf = {}, [None, None], [None, None], [None, None], [None, None]
            ex, turned = {}, {}

            def score(i):
                b, k = i // 4, i % 2
                t = P.pe(matmuls((ps[:, k, 0:L], zT[:, b, 128 * (i % 4):128 * (i % 4) + 128], ctxT[:, b, :], True, True)),
                         z[b], free[k])
                s = sb[k]
                t = P.dve(lambda e: e.tensor_tensor(s, ps[:, k, 0:L], keep[:, b, :], ALU.mult), t, t1, sf[k])
                free[k] = t
                t = P.dve(lambda e: e.tensor_tensor(s, s, neg[:, b, :], ALU.add), t, t2)
                t = P.dve(lambda e: e.tensor_reduce(mx[:, i:i + 1], s, AX.X, ALU.max, negate=True), t)
                t = P.act(lambda e: e.activation(s, s, ACT.Exp, bias=mx[:, i:i + 1], accum_out=sm[:, i:i + 1]), t)
                t = P.dve(lambda e: e.reciprocal(sm[:, i:i + 1], sm[:, i:i + 1]), t)
                ex[i] = P.dve(lambda e: e.scalar_tensor_tensor(s, s, sm[:, i:i + 1], gs[:, b, :], ALU.mult, ALU.mult), t, gd)

            def tp(i):
                b, k = i // 4, 2 + i % 2
                t = P.pe(transposes((ps[0:L, k, 0:128], sb[i % 2], ident)), ex[i], free[k])
                sf[i % 2] = t
                j = i % 4
                o = pT[b % 2][0:L, 128 * j:128 * j + 128]
                free[k] = P.act(lambda e: e.activation(o, ps[0:L, k, 0:128], ACT.Copy), t, pTf[b % 2] if j == 0 else None)
                turned[i] = free[k]

            def tail(b):
                r = b % 2
                k = 4 + r
                t = P.pe(matmuls((ps[:, k, :], ctxk[0:L, b, :], pT[r][0:L], True, True)), turned[4 * b + 3], free[k])
                pTf[r] = t
                t = P.act(lambda e: e.activation(cT[r], ps[:, k, :], ACT.Copy), t, cTf[r])
                free[k] = t
                t = P.pe(matmuls(*[m for j in range(4) for m in (
                    (ps[:, 6 + r, 128 * j:128 * j + 128], cT[r][:, 128 * j:128 * j + 128], WcT[:, 0, :], True, False),
                    (ps[:, 6 + r, 128 * j:128 * j + 128], tokens(4 * b + j), WcT[:, 1, :], False, True))]), t, free[6 + r])
                cTf[r] = t
                t = P.act(lambda e: e.activation(th[r], ps[:, 6 + r, :], ACT.Tanh), t, thf[r])
                free[6 + r] = t
                thf[r] = P.dve(lambda e: e.tensor_tensor(X[:, 4 * b:4 * b + 4, :], X[:, 4 * b:4 * b + 4, :],
                                                         view(th[r], "p (a c) -> p a c", a=4), ALU.add), t)

            for i in range(NT + 2):
                if i < NT:
                    score(i)
                if 1 <= i <= NT:
                    tp(i - 1)
                if i >= 5 and (i - 5) % 4 == 0:
                    tail((i - 5) // 4)
            P.barrier()

        def shift():
            c = P.pool(lambda e: e.tensor_copy(XN[:, :, 0:64], X[:, :, 0:64]))
            done = []
            for g in range(2):
                xs = view(X[:, 8 * g:8 * g + 8, 64:128], "p (b t) c -> p b t c", b=2)
                o = view(ps[:, g, :], "p (b t c) -> p b t c", b=2, t=4)
                t = P.pe(matmuls((ps[:, g, :], shiftm, X[:, 8 * g:8 * g + 8, 64:128], True, False),
                                 (o[:, :, 1:4, :], carrym, xs[:, :, 0:3, :], False, True)), free[g])
                free[g] = P.act(lambda e, g=g: e.activation(XN[:, 8 * g:8 * g + 8, 64:128],
                                                            view(ps[:, g, :], "p (t c) -> p t c", t=8), ACT.Copy), t)
                done += [[free[g], c]] * 8
            return done

        def attention(l, m):
            w, wl = l2[l % 2], P.loaded(f"l2_{l}")
            Qbd, kT, T1, T2, SQ, PB, PT, VW, oT, CT, SN = (m[k] for k in (
                "Qbd", "kT", "T1", "T2", "SQ", "PB", "PT", "VW", "oT", "CT", "SN"))
            ss, sr, stmp, mxs, sms = m["ss"], m["sr"], m["stmp"], m["mxs"], m["sms"]
            sh = shift()
            xt = turn(XN, sh, (6, 7), to_xT)
            tab = []
            for k in range(2):
                tab.append(P.pool(lambda e, k=k: e.tensor_tensor(CT[:, :, k, :], rotc[:, :, k, :], bc(w["qs"][:, k, :], 1, 4),
                                                                 ALU.mult), wl))
                for a in range(2):
                    tab.append(P.pool(lambda e, k=k, a=a: e.tensor_tensor(
                        SN[:, :, k, 32 * a:32 * a + 32], rots[:, :, k, 32 * a:32 * a + 32],
                        bc(w["qs"][:, k, 32 - 32 * a:64 - 32 * a], 1, 4), ALU.mult), wl))

            T1f, T2f, SQf = [None, None], None, None
            Qf, Kf = [None, None], [None, None]
            qd, kd = {}, {}
            cnt = [0]

            def half(u, bb, k):
                nonlocal T2f, SQf
                bp, t4 = u // 4, u % 4
                b = 2 * bp + bb
                r = cnt[0] % 2
                cnt[0] += 1
                xcols = xT[:, b, 32 + 128 * t4:160 + 128 * t4]
                t1, t2, sq = T1[r], T2, SQ
                h3 = lambda z: view(z, "p (h c) -> p h c", c=64)
                for j in range(2):
                    hh = slice(8 * j, 8 * j + 8)
                    p = P.pe(matmuls((ps[:, j, :], xcols, w["Wqkv"][:, 1024 * k + 512 * j:1024 * k + 512 * j + 512],
                                      True, True)), xt[b], wl, free[j])
                    src = h3(ps[:, j, :])
                    s1 = P.act(lambda e, j=j: e.activation(sq[:, 512 * j:512 * j + 512], ps[:, j, :], ACT.Square), p, SQf)
                    a1 = P.dve(lambda e, hh=hh, src=src: e.tensor_tensor(h3(t1)[:, hh], src, bc(CT[:, t4, k, :], 1, 8),
                                                                         ALU.mult), s1, tab, T1f[r])
                    for a in range(2):
                        a2 = P.dve(lambda e, a=a, hh=hh, src=src: e.tensor_tensor(
                            h3(t2)[:, hh, 32 * a:32 * a + 32], src[:, :, 32 - 32 * a:64 - 32 * a],
                            bc(SN[:, t4, k, 32 * a:32 * a + 32], 1, 8), ALU.mult), s1, T2f)
                    free[j] = a2
                ad = P.pool(lambda e: e.tensor_tensor(t1, t1, t2, ALU.add), a1, a2)
                T2f = ad
                sd = P.dve(lambda e: e.tensor_reduce(ss[r], h3(sq), AX.X, ALU.add), s1, m["ssf"][r])
                SQf = sd
                sd = P.dve(lambda e: e.tensor_scalar(ss[r], ss[r], 1e-24, None, ALU.max), sd)
                sd = rsqrt(sr[r], ss[r], stmp[r], sd)
                nm = P.dve(lambda e: e.tensor_tensor(h3(t1), h3(t1), bc(sr[r], 2, 64), ALU.mult), sd, ad)
                m["ssf"][r] = nm
                ur = u % 2
                out = []
                for j in range(2):
                    x = P.pe(transposes(*[(ps[:, 2, 128 * c:128 * c + 128],
                                           t1[:, 128 * (4 * j + c):128 * (4 * j + c) + 128], ident) for c in range(4)]),
                             nm, free[2])
                    if j == 1:
                        T1f[r] = x
                    if k == 0:
                        pv = view(ps[:, 2, :], "p (c w q) -> p c w q", c=4, w=4)
                        e1 = P.act(lambda e, j=j: e.activation(Qbd[ur][0:64, bb, 4 * j:4 * j + 4, :, 0, :], pv[0:64], ACT.Copy),
                                   x, Qf[ur])
                        e2 = P.act(lambda e, j=j: e.activation(Qbd[ur][64:128, bb, 4 * j:4 * j + 4, :, 1, :], pv[64:128], ACT.Copy),
                                   x, Qf[ur])
                        free[2] = e2
                        out += [e1, e2]
                    else:
                        pv = view(ps[:, 2, :], "p (c q) -> p c q", c=4)
                        free[2] = P.act(lambda e, j=j: e.activation(kT[ur][:, bb, 4 * j:4 * j + 4, 32:160], pv, ACT.Copy),
                                        x, Kf[ur])
                        out.append(free[2])
                if k == 1:
                    if t4 == 0:
                        cp = P.pool(lambda e: e.memset(kT[ur][:, bb, :, 0:32], 0.0), Kf[ur])
                    else:
                        cp = P.pool(lambda e: e.tensor_copy(kT[ur][:, bb, :, 0:32], kT[1 - ur][:, bb, :, 128:160]),
                                    kd[(u - 1, bb)], Kf[ur])
                    kd[(u, bb)] = out + [cp]
                else:
                    qd[(u, bb)] = out

            soft, VWf, PBf, PTf, oTf = {}, [None, None], [None, None], None, None
            vd, unit_out, xvd, xVf, xV = {}, {}, {}, [None, None], m["xV"]

            def scores(g):
                u, wp = g // 2, g % 2
                ur, r = u % 2, g % 2
                sub = []
                for bb in range(2):
                    k = 3 + bb
                    first_w = 1 if (u % 4 == 0 and wp == 0) else 0
                    ms = [(ps[:, k, :], identb, maskb[:, first_w, :], True, False)]
                    for wi in range(2):
                        wl_ = 2 * wp + wi
                        for c in range(8):
                            ms.append((ps[64 * wi:64 * wi + 64, k, 64 * c:64 * c + 64],
                                       view(Qbd[ur][:, bb, c, wl_], "p h q -> p (h q)"),
                                       kT[ur][:, bb, c, 32 * wl_:32 * wl_ + 64], False, c == 7))
                    t = P.pe(matmuls(*ms), qd[(u, bb)], kd[(u, bb)], free[k])
                    if wp == 1 and bb == 1:
                        Qf[ur], Kf[ur] = t, t
                    s = view(ps[:, k, :], "p (c j) -> p c j", c=8)
                    mxv = mxs[r][:, 8 * bb:8 * bb + 8]
                    t = P.dve(lambda e, s=s, mxv=mxv: e.tensor_reduce(mxv, s, AX.X, ALU.max), t, m["mxf"][r])
                    t = P.dve(lambda e, s=s, mxv=mxv, bb=bb: e.tensor_tensor(PB[r][:, :, bb, :], s, bc(mxv, 2, 64), ALU.subtract),
                              t, PBf[r])
                    free[k] = t
                    sub.append(t)
                fl = view(PB[r], "p c b j -> p (c b j)")
                f3 = view(PB[r], "p c b j -> p (c b) j")
                t = P.act(lambda e: e.activation(fl, fl, ACT.Exp), sub)
                t = P.dve(lambda e: e.tensor_reduce(sms[r], f3, AX.X, ALU.add), t)
                t = P.dve(lambda e: e.reciprocal(sms[r], sms[r]), t)
                soft[g] = P.pool(lambda e: e.tensor_tensor(f3, f3, bc(sms[r], 2, 64), ALU.mult), t)
                m["mxf"][r] = soft[g]

            def window_values(g, wi):
                u, wp = g // 2, g % 2
                r = g % 2
                out = []
                for j in range(2):
                    t = P.pe(matmuls((ps[:, 6, :], view(xV[u % 2][:, 2 * wp + wi], "p b k -> p (b k)"),
                                      w["Wqkv"][:, 2048 + 512 * j:2560 + 512 * j], True, True)), xvd[u], wl, free[6])
                    o = VW[r][:, wi, 512 * j:512 * j + 512]
                    if j == 0:
                        free[6] = P.act(lambda e, o=o: e.activation(o, ps[:, 6, :], ACT.Copy), t, VWf[r])
                    else:
                        free[6] = P.dve(lambda e, o=o: e.tensor_copy(o, ps[:, 6, :]), t, VWf[r])
                    out.append(free[6])
                xVf[u % 2] = t
                vd.setdefault(g, []).extend(out)

            def window_tokens(u):
                bp, t4 = u // 4, u % 4
                xvd[u] = [P.pool(lambda e, bb=bb, kh=kh: e.tensor_copy(
                    xV[u % 2][:, :, bb, 32 * kh:32 * kh + 32],
                    view(xT[:, 2 * bp + bb, 128 * t4 + 32 * kh:128 * t4 + 32 * kh + 128], "p (w k) -> p w k", w=4)),
                    xt, xVf[u % 2]) for bb in range(2) for kh in range(2)]

            def turn_p(g):
                nonlocal PTf
                r = g % 2
                out = []
                for j in range(2):
                    t = P.pe(transposes(*[(ps[:, 5, 128 * c:128 * c + 128],
                                           view(PB[r][:, 4 * j + c], "p b j -> p (b j)"), ident) for c in range(4)]),
                             soft[g], free[5])
                    if j == 1:
                        PBf[r] = t
                    o = view(PT[:, 4 * j:4 * j + 4, :], "p c q -> p (c q)")
                    free[5] = P.act(lambda e, o=o: e.activation(o, ps[:, 5, :], ACT.Copy), t, PTf)
                    out.append(free[5])
                return out

            def weigh(g, bb, ptd):
                nonlocal PTf
                u, wp = g // 2, g % 2
                r = g % 2
                ms = []
                h = slice(64 * bb, 64 * bb + 64)
                for c in range(8):
                    for hp in range(2):
                        for wi in range(2):
                            ms.append((ps[64 * hp:64 * hp + 64, 7, 64 * c + 32 * wi:64 * c + 32 * wi + 32],
                                       VW[r][h, wi, 128 * c + 64 * hp:128 * c + 64 * hp + 64],
                                       PT[h, c, 64 * wi + 32 * hp:64 * wi + 32 * hp + 32], True, True))
                t = P.pe(matmuls(*ms), ptd, vd[g], free[7])
                if bb == 1:
                    PTf = VWf[r] = t
                o = oT[:, :, bb, 64 * wp:64 * wp + 64]
                free[7] = P.act(lambda e: e.activation(o, view(ps[:, 7, :], "p (c q) -> p c q", c=8), ACT.Copy), t,
                                oTf if wp == 0 else None)
                unit_out.setdefault(u, []).append(free[7])

            def project(u):
                nonlocal oTf
                bp, t4 = u // 4, u % 4
                ms = []
                for bb in range(2):
                    ms += [(ps[:, 6, 128 * bb:128 * bb + 128], oT[:, c, bb, :], w["Wo"][:, c, :], c == 0, c == 7)
                           for c in range(8)]
                t = P.pe(matmuls(*ms), unit_out[u], wl, free[6])
                oTf = t
                xv = view(X, "p (b t) c -> p b t c", t=4)[:, 2 * bp:2 * bp + 2, t4, :]
                free[6] = P.dve(lambda e: e.tensor_tensor(xv, xv, view(ps[:, 6, 0:256], "p (b c) -> p b c", b=2), ALU.add), t)

            for bb in range(2):
                for k in range(2):
                    half(0, bb, k)
            window_tokens(0)
            for g in range(17):
                u = g // 2
                if g % 2 == 0 and u + 1 < 8:
                    window_tokens(u + 1)
                if g < 16:
                    scores(g)
                    if u + 1 < 8:
                        half(u + 1, g % 2, 0)
                    window_values(g, 0)
                if g >= 1:
                    ptd = turn_p(g - 1)
                if g < 16:
                    window_values(g, 1)
                if g >= 1:
                    weigh(g - 1, 0, ptd)
                if g < 16 and u + 1 < 8:
                    half(u + 1, g % 2, 1)
                if g >= 1:
                    weigh(g - 1, 1, ptd)
                    if g % 2 == 0:
                        project(g // 2 - 1)
            P.barrier()

        def feed(l, m):
            w = l2[l % 2]
            sh = shift()
            ln = layernorm(XN, XN, sh)

            def affine(b, p, t):
                return P.act(lambda e: e.activation(chunk(b), p, ACT.Identity, bias=w["b"], scale=w["g"]), t)

            xt = turn(XN, ln, (6, 7), affine)
            hT, gl = m["hT"], m["gl"]
            hf, glf = [None, None], [None] * 3
            hid = {}
            n = 0

            def y(b):
                k = 6 + b % 2
                ms = []
                for j in range(4):
                    o = ps[:, k, 128 * j:128 * j + 128]
                    for c, rows in enumerate((128, 128, 85)):
                        ms.append((o, hT[b % 2][0:rows, c, 128 * j:128 * j + 128], w["W2"][0:rows, c, :], c == 0, False))
                    ms.append((o, onesf[0:1, :], w["b2"][0:1], False, True))
                t = P.pe(matmuls(*ms), hid[b], free[k])
                hf[b % 2] = t
                add_rows(b, k, t)

            for b in range(B + 1):
                if b < B:
                    toks = []
                    for c, rows in enumerate((128, 128, 85)):
                        r = n % 3
                        n += 1
                        k = 2 * r
                        p1, p2 = ps[0:rows, k, :], ps[0:rows, k + 1, :]
                        t = P.pe(matmuls((p2, w["W1"][:, 341 + 128 * c:341 + 128 * c + rows], chunk(b), True, True),
                                         (p1, w["W1"][:, 128 * c:128 * c + rows], chunk(b), True, True)),
                                 xt[b], free[k], free[k + 1])
                        a = P.act(lambda e, c=c, r=r, rows=rows, p2=p2: e.activation(
                            gl[r][0:rows], p2, ACT.Gelu, bias=w["b1"][0:rows, 3 + c:4 + c]), t, glf[r])
                        o = hT[b % 2][0:rows, c, :]
                        s = P.dve(lambda e, c=c, r=r, rows=rows, p1=p1, o=o: e.scalar_tensor_tensor(
                            o, p1, w["b1"][0:rows, c:c + 1], gl[r][0:rows], ALU.add, ALU.mult), a, hf[b % 2])
                        glf[r] = free[k] = free[k + 1] = s
                        toks.append(s)
                    hid[b] = toks
                if b >= 1:
                    y(b - 1)
            return P.barrier()

        def l2_ffn():
            at[0] = base5
            m = dict(
                Qbd=[view(words(2 * 8 * 4 * 64), "p (b c w h q) -> p b c w h q", b=2, c=8, w=4, h=2) for _ in range(2)],
                kT=[tile4(2, 8, 160) for _ in range(2)], T1=[words(1024) for _ in range(2)], T2=words(1024),
                SQ=words(1024), PB=[tile4(8, 2, 64) for _ in range(2)], PT=tile3(8, 128),
                VW=[tile3(2, 1024) for _ in range(2)], oT=tile4(8, 2, 128), CT=tile4(4, 2, 64), SN=tile4(4, 2, 64),
                ss=[words(H) for _ in range(2)], sr=[words(H) for _ in range(2)], stmp=[words(H) for _ in range(2)],
                mxs=[words(16) for _ in range(2)], sms=[words(16) for _ in range(2)],
                xV=[tile3(4, 128) for _ in range(2)], ssf=[None, None], mxf=[None, None])
            m["xV"] = [view(z, "p w (b k) -> p w b k", b=2) for z in m["xV"]]
            end = at[0]
            keep = view(mem[:, base5:base5 + 2 * 4096], "p (r n) -> p r n", r=2)
            at[0] = base5 + 2 * 4096
            m["hT"] = [tile3(3, 512) for _ in range(2)]
            m["gl"] = [words(512) for _ in range(3)]
            at[0] = end
            P.pool(lambda e: e.memset(keep, 0.0), P.loaded("xw0"), P.loaded("xw1"), small)
            P.barrier()
            rows = kept.rearrange("(t p) d -> p t d", p=128)
            P.load("kept", rows, X)
            layernorm(X, X, before_write=P.loaded("kept"))
            P.barrier()
            for l in range(DEPTH):
                m["ssf"], m["mxf"] = [None, None], [None, None]
                attention(l, m)
                now = feed(l, m)
                if l + 2 < DEPTH:
                    load_l2(l + 2)
            P.load("back", XN, rows, now)
            P.dve(lambda e: e.tensor_tensor(X, X, XN, ALU.add), P.loaded("back"))
            P.barrier()

        if 1 in stages:
            load_moe0()
        if 0 in stages:
            xcond("0")
        if 1 in stages:
            l0_ffn()
        if 2 in stages:
            xcond("1")
        if 3 in stages:
            l1_ffn()
        if 4 in stages:
            l2_xcond()
        if 5 in stages:
            l2_ffn()
        if 7 in stages:
            load_moe3()
        if 6 in stages:
            xcond("3")
        if 7 in stages:
            l3_ffn()
        P.load("out", out.rearrange("(t p) d -> p t d", p=128), X)
        P.queue["sync"].append((None, [P.loaded(n) for n in P.sems if n not in ENGINES], None, 0))

        block = ctx.enter_context(nc.Block())

        @block.sync
        def _(e):
            P.emit("sync", e)

        @block.gpsimd
        def _(e):
            P.emit("gpsimd", e)

        @block.scalar
        def _(e):
            P.emit("scalar", e)

        @block.tensor
        def _(e):
            P.emit("tensor", e)

        @block.vector
        def _(e):
            P.emit("vector", e)


def constants():
    n, dh = S, 64
    half = np.arange(0, dh, 2, dtype=np.float32)
    inv = (1.0 / np.float32(10000.0) ** (half / np.float32(dh))).astype(np.float32)
    pos = np.arange(n, dtype=np.float32)
    fr = pos[:, None] * inv[None, :]
    fr = np.concatenate([fr, fr], -1).astype(np.float64)
    basis = ((half + np.float32(0.4 * dh)) / np.float32(1.4 * dh)).astype(np.float64)
    power = (pos.astype(np.float64) - n // 2) / 16
    scale = basis[None, :] ** power[:, None]
    scale = np.concatenate([scale, scale], -1)
    sign = np.where(np.arange(dh) < dh // 2, -1.0, 1.0)
    c = np.stack([8 * np.cos(fr) * scale, np.cos(fr) / scale], 1)
    s = np.stack([8 * np.sin(fr) * scale * sign, np.sin(fr) / scale * sign], 1)
    rows = lambda z: np.ascontiguousarray(z.reshape(4, 128, 2, dh).transpose(1, 0, 2, 3).astype(np.float32))
    p = np.arange(128)
    q, j = p[:, None] % 32, np.arange(64)[None, :]
    hidden = (j < q) | (j > q + 32)
    start = hidden | ((p[:, None] < 64) & (j < 32))
    return dict(
        ident=np.eye(128, dtype=np.float32), lower=(p[:, None] < p[None, :]).astype(np.float32),
        shiftm=(p[:, None] == p[None, :] - 1).astype(np.float32),
        carrym=((p[:, None] == 127) & (p[None, :] == 0)).astype(np.float32),
        hm=(p[:, None] // 8 == np.arange(16)[None, :]).astype(np.float32), rotc=rows(c), rots=rows(s),
        masks=np.stack([hidden, start], 1).astype(np.float32) * np.float32(NEG),
        idx=np.arange(L, dtype=np.float32), sel3=np.eye(3, dtype=np.float32))


def layout(i):
    c = np.ascontiguousarray
    a = {"x": i["x"].reshape(B * S, D), "ctxT": c(i["ctx_1024"].transpose(2, 0, 1)),
         "ctxk": c(i["ctx_1024"].transpose(1, 0, 2)), "tau": i["condB_tau"], "pt": i["condB_pt"], "len": i["_lenS2"],
         "delta": i["fside_BxS2_0"]}
    for n in "013":
        for k in "qkvo":
            a[f"L{n}W{k}"] = c(i[f"L{n}_xcond_W{k}"].T)
        for k in "qk":
            a[f"L{n}b{k}"] = i[f"L{n}_xcond_b{k}"].reshape(D, 1)
        for k in "vo":
            a[f"L{n}b{k}"] = i[f"L{n}_xcond_b{k}"].reshape(1, D)
    a["lng"], a["lnb"] = i["L0_ffn_ln_gamma"].reshape(D, 1), i["L0_ffn_ln_beta"].reshape(D, 1)
    a["WrT"], a["WgT"] = c(i["L0_ffn_Wr"].T), c(i["L3_ffn_Wg"].T)
    a["W12T"] = c(i["L0_ffn_W12"].transpose(0, 2, 1))
    a["W3T"] = c(i["L0_ffn_W3"].reshape(E, D, 4, 128).transpose(0, 3, 2, 1))
    a["w1T"] = c(i["L1_ffn_w1"].T)
    a["w2T"] = c(i["L1_ffn_w2"].reshape(D, 4, 128).transpose(2, 1, 0))
    a["cvw"] = c(i["L1_ffn_conv_w"].reshape(4, 128, 3).transpose(1, 0, 2))
    a["cvb"] = c(i["L1_ffn_conv_b"].reshape(4, 128).T)
    a["Wa"] = i["L2_xcond_W_a"]
    a["WcT"] = c(i["L2_xcond_W_c"].reshape(D, 2, 128).transpose(2, 1, 0))
    a["Wqkv"], a["W1"], a["W2"] = i["L2_ffn_Wqkv"], i["L2_ffn_W1"], i["L2_ffn_W2"]
    a["L2Wo"] = c(i["L2_ffn_Wo"].reshape(DEPTH, 8, 128, D).transpose(0, 2, 1, 3))
    b1 = np.zeros((DEPTH, 128, 6), np.float32)
    for k in range(2):
        for n, rows in enumerate((128, 128, 85)):
            b1[:, :rows, 3 * k + n] = i["L2_ffn_b1"][:, 341 * k + 128 * n:341 * k + 128 * n + rows]
    a["b1"] = b1
    a["ln_g"], a["ln_b"] = i["L2_ffn_ln_g"].reshape(DEPTH, D, 1), i["L2_ffn_ln_b"].reshape(DEPTH, D, 1)
    a["b2"] = i["L2_ffn_b2"].reshape(DEPTH, 1, D)
    a["qks"] = c(np.stack([i["L2_ffn_q_scale"], i["L2_ffn_k_scale"]], 1))
    a["L3W1"], a["L3W2"] = i["L3_ffn_W1"], i["L3_ffn_W2"]
    a["L3b1"] = c(i["L3_ffn_b1"].reshape(E, 4, 128).transpose(2, 0, 1))
    a["L3b2"] = i["L3_ffn_b2"].reshape(1, E, D)
    a.update(constants())
    return {k: c(v) for k, v in a.items()}


def declare(nc, arrays):
    d = {k: nc.dram_tensor("in_" + k, v.shape, mybir.dt.from_np(v.dtype), kind="ExternalInput").ap()
         for k, v in arrays.items()}
    kept = nc.dram_tensor("kept", (B * S, D), F32, kind="Internal").ap()
    out = nc.dram_tensor("out_x", (B * S, D), F32, kind="ExternalOutput").ap()
    return d, kept, out


def kernel(**inputs):
    import concourse.bacc as bacc
    from concourse.bass_utils import run_bass_kernel_spmd
    arrays = layout({k: np.asarray(v) for k, v in inputs.items()})
    nc = bacc.Bacc("TRN2", target_bir_lowering=False, num_devices=1)
    build(nc, *declare(nc, arrays), range(8))
    r = run_bass_kernel_spmd(nc, [{"in_" + k: v for k, v in arrays.items()}], core_ids=[0])
    return r.results[0]["out_x"].reshape(B, S, D)
```

```python
from contextlib import ExitStack

import numpy as np
import concourse.bass as bass
from concourse import mybir

F32 = mybir.dt.float32
BF16 = mybir.dt.bfloat16
I32 = mybir.dt.int32
U32 = mybir.dt.uint32
ALU = mybir.AluOpType
ACT = mybir.ActivationFunctionType
AX = mybir.AxisListType

B, S, D, L = 4, 512, 128, 77
NT = B * S // 128
H = 16
E = 8
DEPTH = 6
CAP0 = 640
CAP3 = 538
ROUND = float(3 << 22)
NEG = -1.0e30
ENGINES = ("tensor", "vector", "scalar", "gpsimd", "sync")


class Program:

    def __init__(self, nc, ctx):
        self.nc, self.ctx = nc, ctx
        self.queue = {e: [] for e in ENGINES}
        self.sems, self.count = {}, {}
        for e in ENGINES:
            self.semaphore(e)

    def semaphore(self, name):
        self.sems[name] = self.ctx.enter_context(self.nc.semaphore("s_" + name))
        self.count[name] = 0

    def step(self, engine, fn, after):
        self.count[engine] += 1
        self.queue[engine].append((fn, list(flat(after)), engine, 1))
        return (engine, self.count[engine])

    def pe(self, fn, *after):
        return self.step("tensor", fn, after)

    def dve(self, fn, *after):
        return self.step("vector", fn, after)

    def act(self, fn, *after):
        return self.step("scalar", fn, after)

    def pool(self, fn, *after):
        return self.step("gpsimd", fn, after)

    def load(self, group, out, in_, *after, engine="sync"):
        if group not in self.sems:
            self.semaphore(group)
        self.count[group] += 16
        self.queue[engine].append((lambda e: e.dma_start(out, in_), list(flat(after)), group, 16))

    def loaded(self, group):
        return (group, self.count[group])

    def barrier(self):
        now = [(e, self.count[e]) for e in ENGINES[:4]]
        for e in ENGINES:
            self.queue[e].append((None, now, None, 0))
        return now

    def emit(self, engine, eng):
        seen = {}
        for fn, after, sem, by in self.queue[engine]:
            for name, value in after:
                if seen.get(name, 0) < value:
                    eng.wait_ge(self.sems[name], value)
                    seen[name] = value
            if fn is not None:
                fn(eng).then_inc(self.sems[sem], by)


def flat(tokens):
    for t in tokens:
        if t is None:
            continue
        if isinstance(t, list):
            yield from flat(t)
        else:
            yield t


def matmuls(*group):
    def run(e):
        for out, lhsT, rhs, start, stop in group:
            last = e.matmul(out, lhsT, rhs, start=start, stop=stop, skip_group_check=True)
        return last
    return run


def transposes(*group):
    def run(e):
        for out, in_, ident in group:
            last = e.transpose(out, in_, ident)
        return last
    return run


def bc(ap, axis, n):
    ap = ap.unsqueeze(axis)
    shape = list(ap.shape)
    shape[axis] = n
    return ap.to_broadcast(shape)


def build(nc, d, kept, out, stages):
    ctx = ExitStack()
    with ctx:
        P = Program(nc, ctx)
        WORDS = 51600
        mem = ctx.enter_context(nc.sbuf_tensor("mem", [128, WORDS], F32))
        ps = ctx.enter_context(nc.psum_tensor("ps", [128, 8, 512], F32))
        at = [0]

        def words(n):
            a = at[0]
            at[0] += n
            assert at[0] <= WORDS, at[0]
            return mem[:, a:a + n]

        def view(ap, pat, **k):
            return ap.rearrange(pat, **k)

        def tile3(a, b):
            return view(words(a * b), "p (a b) -> p a b", a=a)

        def tile4(a, b, c):
            return view(words(a * b * c), "p (a b c) -> p a b c", a=a, b=b)

        X = tile3(NT, D)
        XN = tile3(NT, D)
        xT = tile3(B, 32 + S)
        ident = words(128)
        onesf = words(128)
        lower = words(128)
        shiftm = words(128)
        carrym = words(128)
        ones3 = words(64).bitcast(BF16)
        hm = words(H)
        iota8 = words(E)
        identb = words(64).bitcast(BF16)
        maskb = view(words(512).bitcast(BF16), "p (m c) -> p m c", m=2)
        rotc = tile4(4, 2, 64)
        rots = tile4(4, 2, 64)
        ctxT = tile3(B, L)
        ctxk = tile3(B, D)
        tauB = words(B)
        ptB = words(B)
        lenI = words(B).bitcast(I32)
        lenB = words(B)
        idx = words(L)
        sel3 = words(3)
        dl3 = view(words(2 * 4 * L).bitcast(BF16), "p (a b c) -> p a b c", a=B, b=4)
        st = tile3(NT, 6)
        mv = tile3(NT, 2)
        va, rs, rt = words(NT), words(NT), words(NT)
        xw = {}

        def xweights(n):
            xw[n] = {k: words(128) for k in ("Wq", "Wk", "Wv", "Wo", "bv", "bo")}
            xw[n].update({k: words(1) for k in ("bq", "bk")})

        xweights("3")
        WgT = words(E)
        l2 = []
        for _ in range(2):
            l2.append(dict(Wqkv=words(3072), Wo=tile3(8, 128), W1=words(682), W2=tile3(3, 128), b1=words(6),
                           g=words(1), b=words(1), b2=words(128), qs=tile3(2, 64)))
        base5 = at[0]
        xweights("0")
        xweights("1")
        w1T, w2T = words(512), tile3(4, 128)
        cvw, cvb = tile3(4, 3), words(4)
        Wa, WcT = words(128), tile3(2, 128)
        lng, lnb = words(1), words(1)
        WrT = words(E)
        base = at[0]
        masks = tile3(2, 64)
        dlf, dl1, dlt = tile3(B, L), tile3(B, L), tile3(B, L)
        dlh = view(words(3 * 2 * L).bitcast(BF16), "p (a b c) -> p a b c", a=3, b=B)

        free = {b: None for b in range(8)}

        g = "first"
        P.load(g, X, d["x"].rearrange("(t p) d -> p t d", p=128))
        P.load(g, ident, d["ident"])
        for t, n in ((ctxT, "ctxT"), (lower, "lower"), (shiftm, "shiftm"), (carrym, "carrym"), (hm, "hm"),
                     (rotc, "rotc"), (rots, "rots"), (masks, "masks")):
            P.load(g, t, d[n])
        P.load(g, ctxk[0:L], d["ctxk"])
        P.load(g, tauB, d["tau"].partition_broadcast(128))
        P.load(g, ptB, d["pt"].partition_broadcast(128))
        P.load(g, lenI, d["len"].partition_broadcast(128))
        P.load(g, idx, d["idx"].partition_broadcast(128))
        P.load(g, iota8, d["idx"][0:E].partition_broadcast(128))
        P.load(g, sel3[0:3], d["sel3"])
        P.load(g, dlf[0:3], d["delta"].partition_broadcast(3))
        for n in "013":
            g = "xw" + n
            for k in ("Wq", "Wk", "Wv", "Wo"):
                P.load(g, xw[n][k], d[f"L{n}{k}"])
            for k in ("bq", "bk"):
                P.load(g, xw[n][k], d[f"L{n}{k}"])
            for k in ("bv", "bo"):
                P.load(g, xw[n][k][0:1], d[f"L{n}{k}"])
        g = "small"
        for t, n in ((w1T, "w1T"), (w2T, "w2T"), (cvw, "cvw"), (cvb, "cvb"), (Wa, "Wa"), (WcT, "WcT"), (lng, "lng"),
                     (lnb, "lnb"), (WrT, "WrT"), (WgT, "WgT")):
            P.load(g, t, d[n])

        def load_l2(i, *after):
            w, g = l2[i % 2], f"l2_{i}"
            P.load(g, w["Wqkv"], d["Wqkv"][i], *after)
            P.load(g, w["Wo"], d["L2Wo"][i])
            P.load(g, w["W1"], d["W1"][i])
            P.load(g, w["W2"][:, 0:2, :], d["W2"][i, 0:256, :].rearrange("(c p) n -> p c n", p=128))
            P.load(g, w["W2"][0:85, 2, :], d["W2"][i, 256:341, :])
            P.load(g, w["b1"], d["b1"][i])
            P.load(g, w["g"], d["ln_g"][i])
            P.load(g, w["b"], d["ln_b"][i])
            P.load(g, w["b2"][0:1], d["b2"][i])
            P.load(g, w["qs"], d["qks"][i].partition_broadcast(128))

        load_l2(0)
        load_l2(1)
        first, small = P.loaded("first"), P.loaded("small")

        c_ones = P.pool(lambda e: e.memset(onesf, 1.0))
        c_pad = P.pool(lambda e: e.memset(xT[:, :, 0:32], 0.0))
        c_ones3 = P.dve(lambda e: e.memset(ones3, 1.0))
        c_idb = P.dve(lambda e: e.tensor_copy(identb, ident), first)
        c_mask = [P.dve(lambda e, m=m: e.tensor_copy(view(maskb[:, m, :], "p (a k) -> p a k", a=8),
                                                     bc(masks[:, m, :], 1, 8)), first) for m in range(2)]
        c_tau = P.dve(lambda e: e.tensor_scalar(tauB, tauB, float(np.float32(1 / np.sqrt(8.0))), None, ALU.mult), first)
        c_len = P.dve(lambda e: e.tensor_copy(lenB, lenI), first)
        q3 = slice(0, 3)
        t = P.dve(lambda e: e.tensor_scalar(dl1[q3], dlf[q3], float(np.float32(1 / np.sqrt(8.0))), None, ALU.mult), first)
        for j in range(3):
            t = P.dve(lambda e, j=j: e.tensor_copy(dlh[q3, j], dl1[q3]), t)
            if j < 2:
                t = P.dve(lambda e, j=j: e.tensor_tensor(dl1[q3], dl1[q3], dlh[q3, j], ALU.subtract), t)
        t = P.dve(lambda e: e.tensor_scalar(dlt[q3], dlh[q3, 0], sel3[q3, 0:1], None, ALU.mult), t)
        for j in (1, 2):
            t = P.dve(lambda e, j=j: e.scalar_tensor_tensor(dlt[q3], dlh[q3, j], sel3[q3, j:j + 1], dlt[q3],
                                                            ALU.mult, ALU.add), t)
        for h in range(4):
            c_dl = P.dve(lambda e, h=h: e.tensor_copy(dl3[q3, :, h, :], dlt[q3]), t)
        P.barrier()

        def rsqrt(y, a, tmp, *after):
            yi, ai = y.bitcast(I32), a.bitcast(I32)
            t = P.dve(lambda e: e.tensor_scalar(yi, ai, 1, None, ALU.arith_shift_right), *after)
            t = P.dve(lambda e: e.tensor_scalar(yi, yi, -1.0, float(0x5F3759DF), ALU.mult, ALU.add), t)
            for _ in range(3):
                t = P.dve(lambda e: e.tensor_tensor(tmp, y, y, ALU.mult), t)
                t = P.dve(lambda e: e.scalar_tensor_tensor(tmp, tmp, -0.5, a, ALU.mult, ALU.mult), t)
                t = P.dve(lambda e: e.scalar_tensor_tensor(y, tmp, 1.5, y, ALU.add, ALU.mult), t)
            return t

        def layernorm(src, dst, *after, before_write=None):
            out = []
            for b in range(B):
                g = range(4 * b, 4 * b + 4)
                c = slice(4 * b, 4 * b + 4)
                for i in g:
                    ready = [z[i] if isinstance(z, list) and len(z) == NT else z for z in after]
                    a = P.dve(lambda e, i=i: e.bn_stats(st[:, i, :], src[:, i, :]), ready)
                for i in g:
                    a = P.dve(lambda e, i=i: e.bn_aggr(mv[:, i, :], st[:, i, :]), a)
                a = P.dve(lambda e, c=c: e.tensor_scalar(va[:, c], mv[:, c, 1], 1e-5, None, ALU.add), a)
                a = rsqrt(rs[:, c], va[:, c], rt[:, c], a)
                out += [P.dve(lambda e, i=i: e.tensor_scalar(dst[:, i, :], src[:, i, :], mv[:, i, 0:1], rs[:, i:i + 1],
                                                             ALU.subtract, ALU.mult), a, before_write) for i in g]
            return out

        def turn(src, ready, bank, evac):
            got = []
            for b in range(B):
                k = bank[b % len(bank)]
                t = P.pe(transposes(*[(ps[:, k, 128 * j:128 * j + 128], src[:, 4 * b + j, :], ident)
                                      for j in range(4)]), ready[4 * b:4 * b + 4], free[k])
                free[k] = evac(b, ps[:, k, :], t)
                got.append(free[k])
            return got

        def to_xT(b, p, t):
            return P.act(lambda e: e.activation(xT[:, b, 32:32 + S], p, ACT.Copy), t)

        def chunk(b):
            return xT[:, b, 32:32 + S]

        def tokens(i):
            return xT[:, i // 4, 32 + 128 * (i % 4):160 + 128 * (i % 4)]

        def add_rows(b, k, t):
            free[k] = P.dve(lambda e: e.tensor_tensor(X[:, 4 * b:4 * b + 4, :], X[:, 4 * b:4 * b + 4, :],
                                                      view(ps[:, k, :], "p (a c) -> p a c", a=4), ALU.add), t)
            return free[k]

        def xcond(n):
            at[0] = base + 12288
            w, wl = xw[n], P.loaded("xw" + n)
            kTs = words(B * L)
            kbd = tile4(B, H, L)
            vx = tile4(B, H, 9)
            qT = tile3(B, S)
            pb = [words(8 * L) for _ in range(2)]
            pts = [tile3(8, 128) for _ in range(2)]
            mx = [words(8) for _ in range(2)]
            rc = [words(H) for _ in range(2)]
            att = XN
            oT = words(512)

            ln = layernorm(X, XN)
            t = P.pe(matmuls((ps[:, 7, 0:B * L], w["Wk"], view(ctxT, "p b l -> p (b l)"), True, True)), wl, free[7])
            k = P.act(lambda e: e.activation(kTs, ps[:, 7, 0:B * L], ACT.Identity, bias=w["bk"]), t)
            free[7] = k
            t = P.pe(matmuls(*[m for b in range(B) for m in (
                (ps[0:L, 6, 128 * b:128 * b + 128], ctxT[:, b, :], w["Wv"], True, False),
                (ps[0:L, 6, 128 * b:128 * b + 128], onesf[0:1, 0:L], w["bv"][0:1], False, True))]), wl, free[6])
            v1 = P.pool(lambda e: e.memset(vx[0:L, :, :, 8:9], 1.0))
            v = P.act(lambda e: e.activation(view(vx, "p b h e -> p (b h) e")[0:L, :, 0:8],
                                             view(ps[0:L, 6, :], "p (a c) -> p a c", c=8), ACT.Copy), t)
            free[6] = v
            kb = [P.pool(lambda e, b=b: e.tensor_tensor(kbd[:, b], bc(kTs[:, b * L:b * L + L], 1, H), bc(hm, 2, L),
                                                        ALU.mult), k) for b in range(B)]
            xt = turn(XN, ln, (6, 7), to_xT)
            q = []
            for b in range(B):
                f = 6 + b % 2
                t = P.pe(matmuls((ps[:, f, :], w["Wq"], chunk(b), True, True)), xt[b], free[f])
                free[f] = P.dve(lambda e, b=b, f=f: e.tensor_scalar(qT[:, b, :], ps[:, f, :], w["bq"], tauB[:, b:b + 1],
                                                                    ALU.add, ALU.mult), t)
                q.append(free[f])

            NU = 2 * NT
            scored, exped, attd, sub_done = {}, {}, {}, {}
            pb_free, pts_free, rc_free = [None, None], [None, None], [None, None]

            def score(u):
                i, hf, r = u // 2, u % 2, u % 2
                b = i // 4
                ms = []
                for j in range(2):
                    o = ps[:, 2 * r + j, 0:4 * L]
                    h0 = 8 * hf + 4 * j
                    ms += [(o, ones3[0:3, 0:128], view(dl3[0:3, b], "p h l -> p (h l)"), True, False),
                           (o, qT[:, b, 128 * (i % 4):128 * (i % 4) + 128],
                            view(kbd[:, b, h0:h0 + 4, :], "p h l -> p (h l)"), False, True)]
                scored[u] = P.pe(matmuls(*ms), q[b], kb[b], free[2 * r])

            def soft(u):
                r = u % 2
                sc = view(ps[:, 2 * r:2 * r + 2, 0:4 * L], "p a (h l) -> p a h l", h=4)
                m = view(mx[r], "p (a h) -> p a h", a=2)
                o = view(pb[r], "p (a h l) -> p a h l", a=2, h=4)
                t = P.dve(lambda e: e.tensor_reduce(m, sc, AX.X, ALU.max), scored[u])
                t = P.dve(lambda e: e.tensor_tensor(o, sc, bc(m, 3, L), ALU.subtract), t, pb_free[r])
                free[2 * r] = t
                exped[u] = P.act(lambda e: e.activation(pb[r], pb[r], ACT.Exp), t)

            def values(u):
                i, hf, r = u // 2, u % 2, u % 2
                b = i // 4
                pw = []
                for j in range(2):
                    k = 4 + j
                    t = P.pe(transposes(*[(ps[0:L, k, 128 * h:128 * h + 128],
                                           pb[r][:, (4 * j + h) * L:(4 * j + h + 1) * L], ident)
                                          for h in range(4)]), exped[u], free[k])
                    if j == 1:
                        pb_free[r] = t
                    o, s = view(pts[r][0:L, 4 * j:4 * j + 4, :], "p h c -> p (h c)"), ps[0:L, k, :]
                    if j == 0:
                        free[k] = P.act(lambda e, o=o, s=s: e.activation(o, s, ACT.Copy), t, pts_free[r])
                    else:
                        free[k] = P.dve(lambda e, o=o, s=s: e.tensor_copy(o, s), t, pts_free[r])
                    pw.append(free[k])
                av = view(ps[:, 6, 0:288], "p (a h c) -> p a h c", a=2, h=H)
                t = P.pe(matmuls(*[(av[:, i % 2, 8 * hf + h, :], pts[r][0:L, h, :], vx[0:L, b, 8 * hf + h, :], True, True)
                                   for h in range(8)]), pw, v, v1, attd.get(i - 2), free[6])
                pts_free[r] = t
                if hf == 1:
                    z = i % 2
                    t = P.dve(lambda e: e.reciprocal(rc[z], av[:, z, :, 8]), t)
                    attd[i] = P.dve(lambda e: e.tensor_tensor(view(att[:, i, :], "p (h c) -> p h c", h=H),
                                                              av[:, z, :, 0:8], bc(rc[z], 2, 8), ALU.mult), t)

            def project(b):
                t = P.pe(transposes(*[(ps[:, 7, 128 * j:128 * j + 128], att[:, 4 * b + j, :], ident)
                                      for j in range(4)]), attd[4 * b + 3], free[7])
                t = P.act(lambda e: e.activation(oT, ps[:, 7, :], ACT.Copy), t)
                t = P.pe(matmuls(*[m for j in range(4) for m in (
                    (ps[:, 7, 128 * j:128 * j + 128], oT[:, 128 * j:128 * j + 128], w["Wo"], True, False),
                    (ps[:, 7, 128 * j:128 * j + 128], onesf[0:1, :], w["bo"][0:1], False, True))]), t)
                add_rows(b, 7, t)

            for u in range(NU + 3):
                if u < NU:
                    score(u)
                    soft(u)
                if 1 <= u <= NU:
                    values(u - 1)
                if u >= 10 and (u - 10) % 8 == 0 and (u - 10) // 8 < B:
                    project((u - 10) // 8)
            P.barrier()
            free[6] = None

        def gates(probs, gate, k_major, cap, *after):
            m8, ix, ixf = tile3(NT, 8), tile3(NT, 8), tile3(2, NT)
            oh = tile4(2, NT, E)
            a, c, kept = tile4(2, NT, E), tile4(2, NT, E), tile4(2, NT, E)
            pre = tile4(2, NT, E)
            iu = ix.bitcast(U32)
            for i in range(NT):
                t = P.dve(lambda e, i=i: e.max(m8[:, i, :], probs[:, i, :]), *after)
            for i in range(NT):
                t = P.dve(lambda e, i=i: e.max_index(iu[:, i, :], m8[:, i, :], probs[:, i, :]), t)
            for k in range(2):
                t2 = P.dve(lambda e, k=k: e.tensor_copy(ixf[:, k, :], iu[:, :, k]), t)
            for k in range(2):
                t = P.dve(lambda e, k=k: e.tensor_tensor(oh[:, k], bc(iota8, 1, NT), bc(ixf[:, k, :], 2, E),
                                                         ALU.is_equal), t2)
            n = 2 * NT * E
            fl = lambda z: view(z, "p k t e -> p (k t e)")
            t = P.pe(matmuls((ps[:, 0, 0:n], lower, fl(oh), True, True),
                             (ps[:, 1, 0:n], onesf, fl(oh), True, True)), t, free[0], free[1])
            x1 = P.dve(lambda e: e.tensor_copy(fl(pre), ps[:, 0, 0:n]), t)
            t = P.dve(lambda e: e.tensor_copy(fl(a), ps[:, 1, 0:n]), t)
            free[0] = free[1] = t
            src, dst = a, c
            for s in (1, 2, 4, 8):
                t1 = P.dve(lambda e, s=s, o=dst, i=src: e.tensor_tensor(o[:, :, s:, :], i[:, :, s:, :], i[:, :, :NT - s, :],
                                                                      ALU.add), t)
                t = P.dve(lambda e, s=s, o=dst, i=src: e.tensor_copy(o[:, :, :s, :], i[:, :, :s, :]), t)
                src, dst = dst, src
            assert src is a
            t = P.dve(lambda e: e.tensor_tensor(fl(pre), fl(pre), fl(a), ALU.add), t, x1)
            t = P.dve(lambda e: e.tensor_tensor(fl(pre), fl(pre), ps[:, 1, 0:n], ALU.subtract), t)
            free[1] = t
            r0, r1 = pre[:, 0], pre[:, 1]
            if k_major:
                t = P.dve(lambda e: e.tensor_tensor(r1, r1, bc(a[:, 0, NT - 1, :], 1, NT), ALU.add), t)
            else:
                t = P.dve(lambda e: e.tensor_tensor(r0, r0, r1, ALU.add), t)
                t = P.dve(lambda e: e.tensor_copy(r1, r0), t)
            t = P.dve(lambda e: e.tensor_scalar(fl(kept), fl(pre), float(cap), None, ALU.is_lt), t)
            t = P.dve(lambda e: e.tensor_tensor(fl(kept), fl(kept), fl(oh), ALU.mult), t)
            for k in range(2):
                t2 = P.dve(lambda e, k=k: e.tensor_tensor(kept[:, k], kept[:, k], bc(m8[:, :, k], 2, E), ALU.mult), t)
            return P.dve(lambda e: e.tensor_tensor(gate, kept[:, 0], kept[:, 1], ALU.add), t2)

        def softmax8(lg, probs, eps, *after):
            m, s = words(NT), words(NT)
            t = P.dve(lambda e: e.tensor_reduce(m, lg, AX.X, ALU.max), *after)
            t = P.dve(lambda e: e.tensor_tensor(probs, lg, bc(m, 2, E), ALU.subtract), t)
            t = P.act(lambda e: e.activation(probs, probs, ACT.Exp), t)
            t = P.dve(lambda e: e.tensor_reduce(s, probs, AX.X, ALU.add), t)
            if eps:
                t = P.dve(lambda e: e.tensor_scalar(s, s, eps, None, ALU.add), t)
            t = P.dve(lambda e: e.reciprocal(s, s), t)
            return P.dve(lambda e: e.tensor_tensor(probs, probs, bc(s, 2, E), ALU.mult), t)

        def router(wT, lg, xt, lo, hi):
            t = P.pe(matmuls(*[(ps[:, 2, E * i:E * i + E], tokens(i), wT, True, True) for i in range(NT)]), xt, small, free[2])
            free[2] = P.dve(lambda e: e.tensor_scalar(lg, view(ps[:, 2, 0:NT * E], "p (t e) -> p t e", e=E), lo, hi,
                                                      ALU.max, ALU.min), t)
            return free[2]

        def experts(up, ups, down, bias, ready):
            hT = [tile3(4, 512) for _ in range(2)]
            hfree = [None, None]
            added = {}
            jobs = [(b, e) for b in range(B) for e in range(E)]
            hid = {}

            def y(n):
                b, e = jobs[n]
                k = 6 + n % 2
                ms = []
                for j in range(4):
                    o = ps[:, k, 128 * j:128 * j + 128]
                    ms += [(o, hT[n % 2][:, c, 128 * j:128 * j + 128], down[:, e, c, :], c == 0, c == 3 and bias is None)
                           for c in range(4)]
                    if bias is not None:
                        ms.append((o, onesf[0:1, :], bias[0:1, e, :], False, True))
                t = P.pe(matmuls(*ms), hid[n], free[k])
                hfree[n % 2] = t
                for j in range(4):
                    i = 4 * b + j
                    t2 = P.dve(lambda en, i=i, j=j, k=k: en.scalar_tensor_tensor(
                        X[:, i, :], ps[:, k, 128 * j:128 * j + 128], ready[1][:, i, e:e + 1], X[:, i, :],
                        ALU.mult, ALU.add), t, ready[0], added.get(i))
                    added[i] = t2
                free[k] = t2

            cell = [0]
            for n in range(len(jobs) + 1):
                if n < len(jobs):
                    b, e = jobs[n]
                    toks = []
                    for c in range(4):
                        toks.append(up(e, c, b, hT[n % 2][:, c, :], cell[0], hfree[n % 2]))
                        cell[0] += 1
                    hid[n] = toks
                if n >= 1:
                    y(n - 1)

        def l0_ffn():
            at[0] = base
            W12 = tile3(E, 1024)
            W3 = tile4(E, 4, 128)
            lg, probs, gate = tile3(NT, E), tile3(NT, E), tile3(NT, E)
            sg = [words(512) for _ in range(3)]
            sgf = [None] * 3
            wl = P.loaded("moe0")
            ln = layernorm(X, XN)
            ln = layernorm(XN, XN, ln)

            def affine(b, p, t):
                return P.act(lambda e: e.activation(chunk(b), p, ACT.Identity, bias=lnb, scale=lng), t, small)

            xt = turn(XN, ln, (6, 7), affine)
            t = router(WrT, lg, xt, -10000.0, 10000.0)
            t = softmax8(lg, probs, 1e-12, t)
            gt = gates(probs, gate, False, CAP0, t)

            def up(e, c, b, o, cell, hfree):
                r = cell % 3
                k = 2 * r
                t = P.pe(matmuls((ps[:, k, :], W12[:, e, 128 * c:128 * c + 128], chunk(b), True, True),
                                 (ps[:, k + 1, :], W12[:, e, 512 + 128 * c:640 + 128 * c], chunk(b), True, True)),
                         xt[b], wl, free[k], free[k + 1])
                a = P.act(lambda en: en.activation(sg[r], ps[:, k, :], ACT.Silu), t, sgf[r])
                m = P.dve(lambda en: en.tensor_tensor(o, ps[:, k + 1, :], sg[r], ALU.mult), a, hfree)
                sgf[r] = free[k] = free[k + 1] = m
                return m

            experts(up, 2, W3, None, (gt, gate))
            P.barrier()

        def l3_ffn():
            at[0] = base
            W1 = tile3(E, 512)
            W2 = tile4(E, 4, 128)
            b1 = tile3(E, 4)
            b2 = tile3(E, 128)
            at[0] = max(at[0], base + 12288)
            lg, probs, gate = tile3(NT, E), tile3(NT, E), tile3(NT, E)
            wl = P.loaded("moe3")
            ln = layernorm(X, XN)
            xt = turn(XN, ln, (6, 7), to_xT)
            t = router(WgT, lg, xt, -3.0e38, 3.0e38)
            t = softmax8(lg, probs, 0.0, t)
            gt = gates(probs, gate, True, CAP3, t)

            def up(e, c, b, o, cell, hfree):
                k = cell % 6
                t = P.pe(matmuls((ps[:, k, :], W1[:, e, 128 * c:128 * c + 128], chunk(b), True, True)), xt[b], wl, free[k])
                free[k] = P.act(lambda en: en.activation(o, ps[:, k, :], ACT.Gelu, bias=b1[:, e, c:c + 1]), t, hfree)
                return free[k]

            experts(up, 1, W2, b2, (gt, gate))
            P.barrier()

        def load_moe0():
            at[0] = base
            W12 = tile3(E, 1024)
            W3 = tile4(E, 4, 128)
            for e in range(E):
                P.load("moe0", W12[:, e, :], d["W12T"][e])
                P.load("moe0", W3[:, e], d["W3T"][e])

        def load_moe3():
            at[0] = base
            W1 = tile3(E, 512)
            W2 = tile4(E, 4, 128)
            b1 = tile3(E, 4)
            b2 = tile3(E, 128)
            for e in range(E):
                P.load("moe3", W1[:, e, :], d["L3W1"][e])
                P.load("moe3", W2[:, e], d["L3W2"][e].rearrange("(c p) n -> p c n", p=128))
            P.load("moe3", b1, d["L3b1"])
            P.load("moe3", b2[0:1], d["L3b2"])

        def l1_ffn():
            at[0] = base
            hp = tile4(B, 4, S + 2)
            y = tile4(4, B, S)
            hs = view(view(hp, "p b c s -> p b (c s)")[:, :, 0:2048], "p b (t c) -> p b t c", t=4)
            q2 = view(y, "p a b c -> p (a b c)")[:, 0:4096].bitcast(BF16)
            q2 = view(q2, "p (t c) -> p t c", t=NT)
            q2T = view(words(2 * 256).bitcast(BF16), "p (r c n) -> p r c n", r=2, c=4)
            amax, sc1, inv = words(NT), words(NT), words(NT)
            wq1 = words(512)
            wq2 = view(words(256).bitcast(BF16), "p (c n) -> p c n", c=4)
            wt = words(512)
            ws, wm, wr = words(2), words(2), words(2)

            ln = layernorm(X, XN)
            w2f = view(w2T, "p c n -> p (c n)")
            t = P.dve(lambda e: e.tensor_reduce(ws[:, 0:1], w1T, AX.X, ALU.add, apply_absolute_value=True), small)
            t = P.dve(lambda e: e.tensor_reduce(ws[:, 1:2], w2f, AX.X, ALU.add, apply_absolute_value=True), small)
            t = P.pe(matmuls((ps[:, 0, 0:2], onesf, ws, True, True)), t, free[0])
            t = P.dve(lambda e: e.tensor_scalar(wm, ps[:, 0, 0:2], 1.0 / 65536, 1e-5, ALU.mult, ALU.max), t)
            free[0] = t
            wmt = t
            t = P.dve(lambda e: e.reciprocal(wr, wm), t)
            a = P.dve(lambda e: e.tensor_scalar(wt, w1T, wr[:, 0:1], ROUND, ALU.mult, ALU.add), t)
            a = P.dve(lambda e: e.tensor_scalar(wt, wt, ROUND, -1.0, ALU.subtract, ALU.max), a)
            w1d = P.dve(lambda e: e.tensor_scalar(wq1, wt, 1.0, wm[:, 0:1], ALU.min, ALU.mult), a)
            a = P.dve(lambda e: e.tensor_scalar(wt, w2f, wr[:, 1:2], ROUND, ALU.mult, ALU.add), w1d)
            a = P.dve(lambda e: e.tensor_scalar(wt, wt, ROUND, -1.0, ALU.subtract, ALU.max), a)
            w2d = P.dve(lambda e: e.tensor_scalar(view(wq2, "p c n -> p (c n)"), wt, 1.0, None, ALU.min), a)

            def scales(src, *after):
                o = amax if len(src.shape) == 3 else view(amax, "p (b t) -> p b t", b=B)
                t = P.dve(lambda e: e.tensor_reduce(o, src, AX.X, ALU.max, apply_absolute_value=True), *after)
                t = P.dve(lambda e: e.tensor_scalar(amax, amax, 1e-5, None, ALU.max), t)
                t1 = P.dve(lambda e: e.tensor_scalar(inv, amax, 1.0 / 127, None, ALU.mult), t)
                t = P.dve(lambda e: e.reciprocal(sc1, amax), t)
                return P.dve(lambda e: e.tensor_scalar(sc1, sc1, 127.0, None, ALU.mult), t), t1

            t = scales(XN, ln)[0]
            rows = []
            a = [P.dve(lambda e, i=i: e.tensor_scalar(XN[:, i, :], XN[:, i, :], sc1[:, i:i + 1], ROUND,
                                                      ALU.mult, ALU.add), t) for i in range(NT)]
            a = [P.dve(lambda e, i=i: e.tensor_scalar(XN[:, i, :], XN[:, i, :], ROUND, -128.0,
                                                      ALU.subtract, ALU.max), a[i]) for i in range(NT)]
            rows = [P.dve(lambda e, i=i: e.tensor_scalar(XN[:, i, :], XN[:, i, :], 127.0, inv[:, i:i + 1],
                                                         ALU.min, ALU.mult), a[i]) for i in range(NT)]
            xt = turn(XN, rows, (6, 7), to_xT)
            pads = [P.pool(lambda e, s=s: e.memset(hp[:, :, :, s:s + 1], 0.0)) for s in (0, S + 1)]
            silu = {}
            n = 0
            hsd = {}

            def back(b):
                out = []
                for j in range(4):
                    i = 4 * b + j
                    k = 4 + i % 2
                    t = P.pe(transposes(*[(ps[:, k, 128 * c:128 * c + 128], y[:, c, b, 128 * j:128 * j + 128], ident)
                                          for c in range(4)]), [silu[(b, c)] for c in range(4)], free[k])
                    free[k] = P.act(lambda e, i=i, k=k: e.activation(hs[:, i // 4, i % 4, :], ps[:, k, :], ACT.Copy), t)
                    out.append(free[k])
                hsd[b] = out

            for b in range(B):
                for c in range(4):
                    k = n % 4
                    n += 1
                    t = P.pe(matmuls((ps[:, k, :], wq1[:, 128 * c:128 * c + 128], chunk(b), True, True)), xt[b], w1d, free[k])
                    t = P.act(lambda e, b=b, c=c, k=k: e.activation(hp[:, b, c, 1:S + 1], ps[:, k, :], ACT.Copy), t)
                    free[k] = t
                    o = y[:, c, b, :]
                    t = P.dve(lambda e, o=o, b=b, c=c: e.tensor_scalar(o, hp[:, b, c, 0:S], cvw[:, c, 0:1], cvb[:, c:c + 1],
                                                                       ALU.mult, ALU.add), t, pads)
                    for s in (1, 2):
                        t = P.dve(lambda e, o=o, b=b, c=c, s=s: e.scalar_tensor_tensor(
                            o, hp[:, b, c, s:s + S], cvw[:, c, s:s + 1], o, ALU.mult, ALU.add), t)
                    silu[(b, c)] = P.act(lambda e, o=o: e.activation(o, o, ACT.Silu), t)
                if b >= 1:
                    back(b - 1)
            back(B - 1)
            t = scales(hs, [hsd[b] for b in range(B)])
            inv2 = P.dve(lambda e: e.tensor_scalar(inv, inv, wm[:, 1:2], None, ALU.mult), t[1])
            a = [P.dve(lambda e, i=i: e.tensor_scalar(hs[:, i // 4, i % 4, :], hs[:, i // 4, i % 4, :], sc1[:, i:i + 1], ROUND,
                                                      ALU.mult, ALU.add), t[0]) for i in range(NT)]
            a = [P.dve(lambda e, i=i: e.tensor_scalar(hs[:, i // 4, i % 4, :], hs[:, i // 4, i % 4, :], ROUND, -128.0,
                                                      ALU.subtract, ALU.max), a[i]) for i in range(NT)]
            rows = [P.dve(lambda e, i=i: e.tensor_scalar(q2[:, i, :], hs[:, i // 4, i % 4, :], 127.0, None, ALU.min), a[i],
                          [hsd[b] for b in range(B)]) for i in range(NT)]
            qf = [None, None]
            for i in range(NT):
                r = i % 2
                pt = ps[:, 4 + r, 0:256].bitcast(BF16)
                t = P.pe(transposes(*[(pt[:, 128 * c:128 * c + 128], q2[:, i, 128 * c:128 * c + 128], identb)
                                      for c in range(4)]), rows[i], free[4 + r])
                t = P.act(lambda e, r=r, pt=pt: e.activation(view(q2T[:, r], "p c n -> p (c n)"), pt, ACT.Copy), t, qf[r])
                free[4 + r] = t
                k = 6 + r
                t = P.pe(matmuls(*[(ps[:, k, 0:128], q2T[:, r, c, :], wq2[:, c, :], c == 0, c == 3) for c in range(4)]),
                         t, w2d, free[k])
                qf[r] = t
                free[k] = P.dve(lambda e, i=i, k=k: e.scalar_tensor_tensor(X[:, i, :], ps[:, k, 0:128], inv[:, i:i + 1],
                                                                           X[:, i, :], ALU.mult, ALU.add), t, inv2)
            P.barrier()

        def l2_xcond():
            at[0] = base
            st_, en_ = words(B), words(B)
            m1, keep, neg, gs = tile3(B, L), tile3(B, L), tile3(B, L), tile3(B, L)
            zT = tile3(B, S)
            sb = [words(L) for _ in range(2)]
            mx = words(NT)
            sm = words(NT)
            pT = [words(512) for _ in range(2)]
            cT = [words(512) for _ in range(2)]
            th = [words(512) for _ in range(2)]
            ln = layernorm(X, XN)
            ib = bc(idx, 1, B)
            t = P.dve(lambda e: e.tensor_scalar(st_, ptB, 16.0, 0.0, ALU.subtract, ALU.max))
            t2 = P.dve(lambda e: e.tensor_scalar(en_, ptB, 16.0, None, ALU.add))
            t2 = P.dve(lambda e: e.tensor_tensor(en_, en_, lenB, ALU.min), t2)
            t = P.dve(lambda e: e.tensor_tensor(m1, ib, bc(st_, 2, L), ALU.is_lt), t)
            t2 = P.dve(lambda e: e.tensor_tensor(neg, ib, bc(en_, 2, L), ALU.is_gt), t2)
            t = P.dve(lambda e: e.tensor_tensor(m1, m1, neg, ALU.max), t, t2)
            t1 = P.dve(lambda e: e.tensor_scalar(keep, m1, -1.0, 1.0, ALU.mult, ALU.add), t)
            t2 = P.dve(lambda e: e.tensor_scalar(neg, m1, -1.0e9, None, ALU.mult), t)
            t = P.dve(lambda e: e.tensor_tensor(gs, ib, bc(ptB, 2, L), ALU.subtract))
            t = P.act(lambda e: e.activation(gs, gs, ACT.Square), t)
            gd = P.act(lambda e: e.activation(gs, gs, ACT.Exp, scale=-1.0 / 128), t)
            xt = turn(XN, ln, (6, 7), to_xT)
            z = []
            for b in range(B):
                k = 6 + b % 2
                t = P.pe(matmuls((ps[:, k, :], Wa, chunk(b), True, True)), xt[b], small, free[k])
                free[k] = P.act(lambda e, b=b, k=k: e.activation(zT[:, b, :], ps[:, k, :], ACT.Copy), t)
                z.append(free[k])
            sc, sf, pTf, cTf, thf = {}, [None, None], [None, None], [None, None], [None, None]
            ex, turned = {}, {}

            def score(i):
                b, k = i // 4, i % 2
                t = P.pe(matmuls((ps[:, k, 0:L], zT[:, b, 128 * (i % 4):128 * (i % 4) + 128], ctxT[:, b, :], True, True)),
                         z[b], free[k])
                s = sb[k]
                t = P.dve(lambda e: e.tensor_tensor(s, ps[:, k, 0:L], keep[:, b, :], ALU.mult), t, t1, sf[k])
                free[k] = t
                t = P.dve(lambda e: e.tensor_tensor(s, s, neg[:, b, :], ALU.add), t, t2)
                t = P.dve(lambda e: e.tensor_reduce(mx[:, i:i + 1], s, AX.X, ALU.max, negate=True), t)
                t = P.act(lambda e: e.activation(s, s, ACT.Exp, bias=mx[:, i:i + 1], accum_out=sm[:, i:i + 1]), t)
                t = P.dve(lambda e: e.reciprocal(sm[:, i:i + 1], sm[:, i:i + 1]), t)
                ex[i] = P.dve(lambda e: e.scalar_tensor_tensor(s, s, sm[:, i:i + 1], gs[:, b, :], ALU.mult, ALU.mult), t, gd)

            def tp(i):
                b, k = i // 4, 2 + i % 2
                t = P.pe(transposes((ps[0:L, k, 0:128], sb[i % 2], ident)), ex[i], free[k])
                sf[i % 2] = t
                j = i % 4
                o = pT[b % 2][0:L, 128 * j:128 * j + 128]
                free[k] = P.act(lambda e: e.activation(o, ps[0:L, k, 0:128], ACT.Copy), t, pTf[b % 2] if j == 0 else None)
                turned[i] = free[k]

            def tail(b):
                r = b % 2
                k = 4 + r
                t = P.pe(matmuls((ps[:, k, :], ctxk[0:L, b, :], pT[r][0:L], True, True)), turned[4 * b + 3], free[k])
                pTf[r] = t
                t = P.act(lambda e: e.activation(cT[r], ps[:, k, :], ACT.Copy), t, cTf[r])
                free[k] = t
                t = P.pe(matmuls(*[m for j in range(4) for m in (
                    (ps[:, 6 + r, 128 * j:128 * j + 128], cT[r][:, 128 * j:128 * j + 128], WcT[:, 0, :], True, False),
                    (ps[:, 6 + r, 128 * j:128 * j + 128], tokens(4 * b + j), WcT[:, 1, :], False, True))]), t, free[6 + r])
                cTf[r] = t
                t = P.act(lambda e: e.activation(th[r], ps[:, 6 + r, :], ACT.Tanh), t, thf[r])
                free[6 + r] = t
                thf[r] = P.dve(lambda e: e.tensor_tensor(X[:, 4 * b:4 * b + 4, :], X[:, 4 * b:4 * b + 4, :],
                                                         view(th[r], "p (a c) -> p a c", a=4), ALU.add), t)

            for i in range(NT + 2):
                if i < NT:
                    score(i)
                if 1 <= i <= NT:
                    tp(i - 1)
                if i >= 5 and (i - 5) % 4 == 0:
                    tail((i - 5) // 4)
            P.barrier()

        def shift():
            c = P.pool(lambda e: e.tensor_copy(XN[:, :, 0:64], X[:, :, 0:64]))
            done = []
            for g in range(2):
                xs = view(X[:, 8 * g:8 * g + 8, 64:128], "p (b t) c -> p b t c", b=2)
                o = view(ps[:, g, :], "p (b t c) -> p b t c", b=2, t=4)
                t = P.pe(matmuls((ps[:, g, :], shiftm, X[:, 8 * g:8 * g + 8, 64:128], True, False),
                                 (o[:, :, 1:4, :], carrym, xs[:, :, 0:3, :], False, True)), free[g])
                free[g] = P.act(lambda e, g=g: e.activation(XN[:, 8 * g:8 * g + 8, 64:128],
                                                            view(ps[:, g, :], "p (t c) -> p t c", t=8), ACT.Copy), t)
                done += [[free[g], c]] * 8
            return done

        def attention(l, m):
            w, wl = l2[l % 2], P.loaded(f"l2_{l}")
            Qbd, kT, T1, T2, SQ, PB, PT, VW, oT, CT, SN = (m[k] for k in (
                "Qbd", "kT", "T1", "T2", "SQ", "PB", "PT", "VW", "oT", "CT", "SN"))
            ss, sr, stmp, mxs, sms = m["ss"], m["sr"], m["stmp"], m["mxs"], m["sms"]
            sh = shift()
            xt = turn(XN, sh, (6, 7), to_xT)
            tab = []
            for k in range(2):
                tab.append(P.pool(lambda e, k=k: e.tensor_tensor(CT[:, :, k, :], rotc[:, :, k, :], bc(w["qs"][:, k, :], 1, 4),
                                                                 ALU.mult), wl))
                for a in range(2):
                    tab.append(P.pool(lambda e, k=k, a=a: e.tensor_tensor(
                        SN[:, :, k, 32 * a:32 * a + 32], rots[:, :, k, 32 * a:32 * a + 32],
                        bc(w["qs"][:, k, 32 - 32 * a:64 - 32 * a], 1, 4), ALU.mult), wl))

            T2f, SQf, added = [None, None], None, [None, None]
            xn = view(XN, "p t d -> p (t d)")
            T1 = [T1, [xn[:, 0:1024], xn[:, 1024:2048]]]
            T1f = [[None, None], [xt, xt]]
            Qf, Kf = [None, None], [None, None]
            qd, kd, normed = {}, {}, {}
            turns = [0]
            h3 = lambda z: view(z, "p (h c) -> p h c", c=64)

            def rotate(u, bb, i):
                nonlocal SQf
                bp, t4 = u // 4, u % 4
                b = 2 * bp + bb
                k, j = i // 2, i % 2
                if i == 0:
                    turns[0] += 1
                z = turns[0] % 2
                t1, hh, cols = T1[z][k], slice(8 * j, 8 * j + 8), slice(512 * j, 512 * j + 512)
                p = P.pe(matmuls((ps[:, j, :], xT[:, b, 32 + 128 * t4:160 + 128 * t4],
                                  w["Wqkv"][:, 1024 * k + 512 * j:1024 * k + 512 * j + 512], True, True)),
                         xt[b], wl, free[j])
                src = h3(ps[:, j, :])
                s1 = P.act(lambda e: e.activation(SQ[:, cols], ps[:, j, :], ACT.Square), p, SQf)
                a1 = P.dve(lambda e: e.tensor_tensor(h3(t1)[:, hh], src, bc(CT[:, t4, k, :], 1, 8), ALU.mult),
                           s1, tab, T1f[z][k])
                for a in range(2):
                    a2 = P.dve(lambda e, a=a: e.tensor_tensor(
                        h3(T2)[:, hh, 32 * a:32 * a + 32], src[:, :, 32 - 32 * a:64 - 32 * a],
                        bc(SN[:, t4, k, 32 * a:32 * a + 32], 1, 8), ALU.mult), s1, T2f[j])
                free[j] = a2
                T2f[j] = P.pool(lambda e: e.tensor_tensor(t1[:, cols], t1[:, cols], T2[:, cols], ALU.add), a1, a2)
                added[k] = T2f[j]
                if j == 1:
                    SQf = P.dve(lambda e: e.tensor_reduce(ss[z][:, H * k:H * k + H], h3(SQ), AX.X, ALU.add), s1, m["ssf"][z])
                if i == 3:
                    sd = P.dve(lambda e: e.tensor_scalar(ss[z], ss[z], 1e-24, None, ALU.max), SQf)
                    sd = rsqrt(sr[z], ss[z], stmp[z], sd)
                    normed[(u, bb)] = z, [P.dve(lambda e, k=k: e.tensor_tensor(
                        h3(T1[z][k]), h3(T1[z][k]), bc(sr[z][:, H * k:H * k + H], 2, 64), ALU.mult), sd, added[k])
                        for k in range(2)]
                    m["ssf"][z] = normed[(u, bb)][1][1]

            def by_feature(u, bb, i):
                z, nm = normed[(u, bb)]
                ur, k, j = u % 2, i // 2, i % 2
                x = P.pe(transposes(*[(ps[:, 2, 128 * c:128 * c + 128],
                                       T1[z][k][:, 128 * (4 * j + c):128 * (4 * j + c) + 128], ident) for c in range(4)]),
                         nm[k], free[2])
                if j == 1:
                    T1f[z][k] = x
                if k == 0:
                    pv = view(ps[:, 2, :], "p (c w q) -> p c w q", c=4, w=4)
                    for hp in range(2):
                        q = slice(64 * hp, 64 * hp + 64)
                        free[2] = P.act(lambda e, hp=hp, q=q: e.activation(
                            Qbd[ur][q, bb, 4 * j:4 * j + 4, :, hp, :], pv[q], ACT.Copy), x, Qf[ur])
                    qd.setdefault((u, bb), []).append(free[2])
                else:
                    pv = view(ps[:, 2, :], "p (c q) -> p c q", c=4)
                    free[2] = P.act(lambda e: e.activation(kT[ur][:, bb, 4 * j:4 * j + 4, 32:160], pv, ACT.Copy), x, Kf[ur])
                    kd.setdefault((u, bb), []).append(free[2])
                if i == 3:
                    if u % 4 == 0:
                        cp = P.pool(lambda e: e.memset(kT[ur][:, bb, :, 0:32], 0.0), Kf[ur])
                    else:
                        cp = P.pool(lambda e: e.tensor_copy(kT[ur][:, bb, :, 0:32], kT[1 - ur][:, bb, :, 128:160]),
                                    kd[(u - 1, bb)], Kf[ur])
                    kd[(u, bb)].append(cp)

            soft, VWf, PBf, PTf, oTf = {}, [None, None], [None, None], None, None
            vd, unit_out, xvd, xVf, xV = {}, {}, {}, [None, None], m["xV"]

            def scores(g, bb):
                u, wp = g // 2, g % 2
                ur, r = u % 2, g % 2
                k = 3 + bb
                ms = [(ps[:, k, :], identb, maskb[:, 1 if u % 4 == 0 and wp == 0 else 0, :], True, False)]
                for wi in range(2):
                    wl_ = 2 * wp + wi
                    for c in range(8):
                        ms.append((ps[64 * wi:64 * wi + 64, k, 64 * c:64 * c + 64],
                                   view(Qbd[ur][:, bb, c, wl_], "p h q -> p (h q)"),
                                   kT[ur][:, bb, c, 32 * wl_:32 * wl_ + 64], False, c == 7))
                t = P.pe(matmuls(*ms), qd[(u, bb)], kd[(u, bb)], free[k])
                if wp == 1 and bb == 1:
                    Qf[ur], Kf[ur] = t, t
                s = view(ps[:, k, :], "p (c j) -> p c j", c=8)
                mxv = mxs[r][:, 8 * bb:8 * bb + 8]
                t = P.dve(lambda e: e.tensor_reduce(mxv, s, AX.X, ALU.max), t, m["mxf"][r])
                free[k] = P.dve(lambda e: e.tensor_tensor(PB[r][:, :, bb, :], s, bc(mxv, 2, 64), ALU.subtract), t, PBf[r])

            def exponentials(g):
                fl = view(PB[g % 2], "p c b j -> p (c b j)")
                m["exp"] = P.act(lambda e: e.activation(fl, fl, ACT.Exp), free[3], free[4])

            def normalise(g):
                r = g % 2
                f3 = view(PB[r], "p c b j -> p (c b) j")
                t = P.dve(lambda e: e.tensor_reduce(sms[r], f3, AX.X, ALU.add), m["exp"])
                t = P.dve(lambda e: e.reciprocal(sms[r], sms[r]), t)
                soft[g] = P.pool(lambda e: e.tensor_tensor(f3, f3, bc(sms[r], 2, 64), ALU.mult), t)
                m["mxf"][r] = soft[g]

            def window_values(g, wi, j):
                u, wp = g // 2, g % 2
                r = g % 2
                t = P.pe(matmuls((ps[:, 6, :], view(xV[u % 2][:, 2 * wp + wi], "p b k -> p (b k)"),
                                  w["Wqkv"][:, 2048 + 512 * j:2560 + 512 * j], True, True)), xvd[u], wl, free[6])
                free[6] = P.act(lambda e: e.activation(VW[r][:, wi, 512 * j:512 * j + 512], ps[:, 6, :], ACT.Copy), t, VWf[r])
                xVf[u % 2] = t
                vd.setdefault(g, []).append(free[6])

            def window_tokens(u):
                bp, t4 = u // 4, u % 4
                xvd[u] = [P.pool(lambda e, bb=bb, kh=kh: e.tensor_copy(
                    xV[u % 2][:, :, bb, 32 * kh:32 * kh + 32],
                    view(xT[:, 2 * bp + bb, 128 * t4 + 32 * kh:128 * t4 + 32 * kh + 128], "p (w k) -> p w k", w=4)),
                    xt, xVf[u % 2]) for bb in range(2) for kh in range(2)]

            def turn_p(g, j):
                r = g % 2
                t = P.pe(transposes(*[(ps[:, 5, 128 * c:128 * c + 128],
                                       view(PB[r][:, 4 * j + c], "p b j -> p (b j)"), ident) for c in range(4)]),
                         soft[g], free[5])
                PBf[r] = t
                free[5] = P.act(lambda e: e.activation(view(PT[:, 4 * j:4 * j + 4, :], "p c q -> p (c q)"), ps[:, 5, :],
                                                       ACT.Copy), t, PTf)
                return free[5]

            def weigh(g, bb, i, ptd):
                nonlocal PTf
                u, wp = g // 2, g % 2
                r = g % 2
                h = slice(64 * bb, 64 * bb + 64)
                ms = [(ps[64 * hp:64 * hp + 64, 7, 64 * c + 32 * wi:64 * c + 32 * wi + 32],
                       VW[r][h, wi, 128 * c + 64 * hp:128 * c + 64 * hp + 64],
                       PT[h, c, 64 * wi + 32 * hp:64 * wi + 32 * hp + 32], True, True)
                      for c in range(4 * i, 4 * i + 4) for hp in range(2) for wi in range(2)]
                t = P.pe(matmuls(*ms), ptd, vd[g], free[7])
                if i == 0:
                    return
                if bb == 1:
                    PTf = VWf[r] = t
                o = oT[:, :, bb, 64 * wp:64 * wp + 64]
                free[7] = P.act(lambda e: e.activation(o, view(ps[:, 7, :], "p (c q) -> p c q", c=8), ACT.Copy), t,
                                oTf if wp == 0 else None)
                unit_out.setdefault(u, []).append(free[7])

            def project(u):
                nonlocal oTf
                bp, t4 = u // 4, u % 4
                ms = []
                for bb in range(2):
                    ms += [(ps[:, 6, 128 * bb:128 * bb + 128], oT[:, c, bb, :], w["Wo"][:, c, :], c == 0, c == 7)
                           for c in range(8)]
                t = P.pe(matmuls(*ms), unit_out[u], wl, free[6])
                oTf = t
                xv = view(X, "p (b t) c -> p b t c", t=4)[:, 2 * bp:2 * bp + 2, t4, :]
                free[6] = P.dve(lambda e: e.tensor_tensor(xv, xv, view(ps[:, 6, 0:256], "p (b c) -> p b c", b=2), ALU.add), t)

            def value(g, n):
                window_values(g, n // 2, n % 2)

            window_tokens(0)
            for bb in range(2):
                for i in range(4):
                    rotate(0, bb, i)
            for bb in range(2):
                for i in range(4):
                    by_feature(0, bb, i)
            for g in range(17):
                u = g // 2
                this, ahead, last = g < 16, u + 1 < 8, g >= 1
                ptd = []
                if last:
                    ptd.append(turn_p(g - 1, 0))
                if last and (g - 1) // 2 + 1 < 8:
                    by_feature((g - 1) // 2 + 1, (g - 1) % 2, 3)
                if last:
                    ptd.append(turn_p(g - 1, 1))
                if this:
                    scores(g, 0)
                    scores(g, 1)
                    if ahead and g % 2 == 0:
                        window_tokens(u + 1)
                    for i in range(4):
                        if ahead:
                            rotate(u + 1, g % 2, i)
                        value(g, i)
                        if i == 0:
                            exponentials(g)
                    normalise(g)
                if last:
                    weigh(g - 1, 0, 0, ptd)
                    weigh(g - 1, 0, 1, ptd)
                    weigh(g - 1, 1, 0, ptd)
                if this and ahead:
                    by_feature(u + 1, g % 2, 0)
                if last:
                    weigh(g - 1, 1, 1, ptd)
                if this and ahead:
                    by_feature(u + 1, g % 2, 1)
                if last and g % 2 == 0:
                    project(g // 2 - 1)
                if this and ahead:
                    by_feature(u + 1, g % 2, 2)
            P.barrier()

        def feed(l, m):
            w = l2[l % 2]
            sh = shift()
            ln = layernorm(XN, XN, sh)

            def affine(b, p, t):
                return P.act(lambda e: e.activation(chunk(b), p, ACT.Identity, bias=w["b"], scale=w["g"]), t)

            xt = turn(XN, ln, (6, 7), affine)
            hT, gl = m["hT"], m["gl"]
            hf, glf = [None, None], [None] * 3
            hid = {}
            n = 0

            def y(b):
                k = 6 + b % 2
                ms = []
                for j in range(4):
                    o = ps[:, k, 128 * j:128 * j + 128]
                    for c, rows in enumerate((128, 128, 85)):
                        ms.append((o, hT[b % 2][0:rows, c, 128 * j:128 * j + 128], w["W2"][0:rows, c, :], c == 0, False))
                    ms.append((o, onesf[0:1, :], w["b2"][0:1], False, True))
                t = P.pe(matmuls(*ms), hid[b], free[k])
                hf[b % 2] = t
                add_rows(b, k, t)

            for b in range(B + 1):
                if b < B:
                    toks = []
                    for c, rows in enumerate((128, 128, 85)):
                        r = n % 3
                        n += 1
                        k = 2 * r
                        p1, p2 = ps[0:rows, k, :], ps[0:rows, k + 1, :]
                        t = P.pe(matmuls((p2, w["W1"][:, 341 + 128 * c:341 + 128 * c + rows], chunk(b), True, True),
                                         (p1, w["W1"][:, 128 * c:128 * c + rows], chunk(b), True, True)),
                                 xt[b], free[k], free[k + 1])
                        a = P.act(lambda e, c=c, r=r, rows=rows, p2=p2: e.activation(
                            gl[r][0:rows], p2, ACT.Gelu, bias=w["b1"][0:rows, 3 + c:4 + c]), t, glf[r])
                        o = hT[b % 2][0:rows, c, :]
                        s = P.dve(lambda e, c=c, r=r, rows=rows, p1=p1, o=o: e.scalar_tensor_tensor(
                            o, p1, w["b1"][0:rows, c:c + 1], gl[r][0:rows], ALU.add, ALU.mult), a, hf[b % 2])
                        glf[r] = free[k] = free[k + 1] = s
                        toks.append(s)
                    hid[b] = toks
                if b >= 1:
                    y(b - 1)
            return P.barrier()

        def l2_ffn():
            at[0] = base5
            m = dict(
                Qbd=[view(words(2 * 8 * 4 * 64), "p (b c w h q) -> p b c w h q", b=2, c=8, w=4, h=2) for _ in range(2)],
                kT=[tile4(2, 8, 160) for _ in range(2)], T1=[words(1024) for _ in range(2)], T2=words(1024),
                SQ=words(1024), PB=[tile4(8, 2, 64) for _ in range(2)], PT=tile3(8, 128),
                VW=[tile3(2, 1024) for _ in range(2)], oT=tile4(8, 2, 128), CT=tile4(4, 2, 64), SN=tile4(4, 2, 64),
                ss=[words(2 * H) for _ in range(2)], sr=[words(2 * H) for _ in range(2)],
                stmp=[words(2 * H) for _ in range(2)],
                mxs=[words(16) for _ in range(2)], sms=[words(16) for _ in range(2)],
                xV=[tile3(4, 128) for _ in range(2)], ssf=[None, None], mxf=[None, None])
            m["xV"] = [view(z, "p w (b k) -> p w b k", b=2) for z in m["xV"]]
            end = at[0]
            keep = view(mem[:, base5:base5 + 2 * 4096], "p (r n) -> p r n", r=2)
            at[0] = base5 + 2 * 4096
            m["hT"] = [tile3(3, 512) for _ in range(2)]
            m["gl"] = [words(512) for _ in range(3)]
            at[0] = end
            P.pool(lambda e: e.memset(keep, 0.0), P.loaded("xw0"), P.loaded("xw1"), small)
            P.barrier()
            rows = kept.rearrange("(t p) d -> p t d", p=128)
            P.load("kept", rows, X)
            layernorm(X, X, before_write=P.loaded("kept"))
            P.barrier()
            for l in range(DEPTH):
                m["ssf"], m["mxf"] = [None, None], [None, None]
                attention(l, m)
                now = feed(l, m)
                if l + 2 < DEPTH:
                    load_l2(l + 2)
            P.load("back", XN, rows, now)
            P.dve(lambda e: e.tensor_tensor(X, X, XN, ALU.add), P.loaded("back"))
            P.barrier()

        if 1 in stages:
            load_moe0()
        if 0 in stages:
            xcond("0")
        if 1 in stages:
            l0_ffn()
        if 2 in stages:
            xcond("1")
        if 3 in stages:
            l1_ffn()
        if 4 in stages:
            l2_xcond()
        if 5 in stages:
            l2_ffn()
        if 7 in stages:
            load_moe3()
        if 6 in stages:
            xcond("3")
        if 7 in stages:
            l3_ffn()
        P.load("out", out.rearrange("(t p) d -> p t d", p=128), X)
        P.queue["sync"].append((None, [P.loaded(n) for n in P.sems if n not in ENGINES], None, 0))

        block = ctx.enter_context(nc.Block())

        @block.sync
        def _(e):
            P.emit("sync", e)

        @block.gpsimd
        def _(e):
            P.emit("gpsimd", e)

        @block.scalar
        def _(e):
            P.emit("scalar", e)

        @block.tensor
        def _(e):
            P.emit("tensor", e)

        @block.vector
        def _(e):
            P.emit("vector", e)


def constants():
    n, dh = S, 64
    half = np.arange(0, dh, 2, dtype=np.float32)
    inv = (1.0 / np.float32(10000.0) ** (half / np.float32(dh))).astype(np.float32)
    pos = np.arange(n, dtype=np.float32)
    fr = pos[:, None] * inv[None, :]
    fr = np.concatenate([fr, fr], -1).astype(np.float64)
    basis = ((half + np.float32(0.4 * dh)) / np.float32(1.4 * dh)).astype(np.float64)
    power = (pos.astype(np.float64) - n // 2) / 16
    scale = basis[None, :] ** power[:, None]
    scale = np.concatenate([scale, scale], -1)
    sign = np.where(np.arange(dh) < dh // 2, -1.0, 1.0)
    c = np.stack([8 * np.cos(fr) * scale, np.cos(fr) / scale], 1)
    s = np.stack([8 * np.sin(fr) * scale * sign, np.sin(fr) / scale * sign], 1)
    rows = lambda z: np.ascontiguousarray(z.reshape(4, 128, 2, dh).transpose(1, 0, 2, 3).astype(np.float32))
    p = np.arange(128)
    q, j = p[:, None] % 32, np.arange(64)[None, :]
    hidden = (j < q) | (j > q + 32)
    start = hidden | ((p[:, None] < 64) & (j < 32))
    return dict(
        ident=np.eye(128, dtype=np.float32), lower=(p[:, None] < p[None, :]).astype(np.float32),
        shiftm=(p[:, None] == p[None, :] - 1).astype(np.float32),
        carrym=((p[:, None] == 127) & (p[None, :] == 0)).astype(np.float32),
        hm=(p[:, None] // 8 == np.arange(16)[None, :]).astype(np.float32), rotc=rows(c), rots=rows(s),
        masks=np.stack([hidden, start], 1).astype(np.float32) * np.float32(NEG),
        idx=np.arange(L, dtype=np.float32), sel3=np.eye(3, dtype=np.float32))


def layout(i):
    c = np.ascontiguousarray
    a = {"x": i["x"].reshape(B * S, D), "ctxT": c(i["ctx_1024"].transpose(2, 0, 1)),
         "ctxk": c(i["ctx_1024"].transpose(1, 0, 2)), "tau": i["condB_tau"], "pt": i["condB_pt"], "len": i["_lenS2"],
         "delta": i["fside_BxS2_0"]}
    for n in "013":
        for k in "qkvo":
            a[f"L{n}W{k}"] = c(i[f"L{n}_xcond_W{k}"].T)
        for k in "qk":
            a[f"L{n}b{k}"] = i[f"L{n}_xcond_b{k}"].reshape(D, 1)
        for k in "vo":
            a[f"L{n}b{k}"] = i[f"L{n}_xcond_b{k}"].reshape(1, D)
    a["lng"], a["lnb"] = i["L0_ffn_ln_gamma"].reshape(D, 1), i["L0_ffn_ln_beta"].reshape(D, 1)
    a["WrT"], a["WgT"] = c(i["L0_ffn_Wr"].T), c(i["L3_ffn_Wg"].T)
    a["W12T"] = c(i["L0_ffn_W12"].transpose(0, 2, 1))
    a["W3T"] = c(i["L0_ffn_W3"].reshape(E, D, 4, 128).transpose(0, 3, 2, 1))
    a["w1T"] = c(i["L1_ffn_w1"].T)
    a["w2T"] = c(i["L1_ffn_w2"].reshape(D, 4, 128).transpose(2, 1, 0))
    a["cvw"] = c(i["L1_ffn_conv_w"].reshape(4, 128, 3).transpose(1, 0, 2))
    a["cvb"] = c(i["L1_ffn_conv_b"].reshape(4, 128).T)
    a["Wa"] = i["L2_xcond_W_a"]
    a["WcT"] = c(i["L2_xcond_W_c"].reshape(D, 2, 128).transpose(2, 1, 0))
    a["Wqkv"], a["W1"], a["W2"] = i["L2_ffn_Wqkv"], i["L2_ffn_W1"], i["L2_ffn_W2"]
    a["L2Wo"] = c(i["L2_ffn_Wo"].reshape(DEPTH, 8, 128, D).transpose(0, 2, 1, 3))
    b1 = np.zeros((DEPTH, 128, 6), np.float32)
    for k in range(2):
        for n, rows in enumerate((128, 128, 85)):
            b1[:, :rows, 3 * k + n] = i["L2_ffn_b1"][:, 341 * k + 128 * n:341 * k + 128 * n + rows]
    a["b1"] = b1
    a["ln_g"], a["ln_b"] = i["L2_ffn_ln_g"].reshape(DEPTH, D, 1), i["L2_ffn_ln_b"].reshape(DEPTH, D, 1)
    a["b2"] = i["L2_ffn_b2"].reshape(DEPTH, 1, D)
    a["qks"] = c(np.stack([i["L2_ffn_q_scale"], i["L2_ffn_k_scale"]], 1))
    a["L3W1"], a["L3W2"] = i["L3_ffn_W1"], i["L3_ffn_W2"]
    a["L3b1"] = c(i["L3_ffn_b1"].reshape(E, 4, 128).transpose(2, 0, 1))
    a["L3b2"] = i["L3_ffn_b2"].reshape(1, E, D)
    a.update(constants())
    return {k: c(v) for k, v in a.items()}


def declare(nc, arrays):
    d = {k: nc.dram_tensor("in_" + k, v.shape, mybir.dt.from_np(v.dtype), kind="ExternalInput").ap()
         for k, v in arrays.items()}
    kept = nc.dram_tensor("kept", (B * S, D), F32, kind="Internal").ap()
    out = nc.dram_tensor("out_x", (B * S, D), F32, kind="ExternalOutput").ap()
    return d, kept, out


def kernel(**inputs):
    import concourse.bacc as bacc
    from concourse.bass_utils import run_bass_kernel_spmd
    arrays = layout({k: np.asarray(v) for k, v in inputs.items()})
    nc = bacc.Bacc("TRN2", target_bir_lowering=False, num_devices=1)
    build(nc, *declare(nc, arrays), range(8))
    r = run_bass_kernel_spmd(nc, [{"in_" + k: v for k, v in arrays.items()}], core_ids=[0])
    return r.results[0]["out_x"].reshape(B, S, D)
```

```python
from contextlib import ExitStack

import numpy as np
import concourse.bass as bass
from concourse import mybir

F32 = mybir.dt.float32
BF16 = mybir.dt.bfloat16
I32 = mybir.dt.int32
U32 = mybir.dt.uint32
ALU = mybir.AluOpType
ACT = mybir.ActivationFunctionType
AX = mybir.AxisListType

B, S, D, L = 4, 512, 128, 77
NT = B * S // 128
H = 16
E = 8
DEPTH = 6
CAP0 = 640
CAP3 = 538
SLOTS = 640
ROUND = float(3 << 22)
NEG = -1.0e30
ENGINES = ("tensor", "vector", "scalar", "gpsimd", "sync")


class Program:

    def __init__(self, nc, ctx):
        self.nc, self.ctx = nc, ctx
        self.queue = {e: [] for e in ENGINES}
        self.sems, self.count = {}, {}
        for e in ENGINES:
            self.semaphore(e)

    def semaphore(self, name):
        self.sems[name] = self.ctx.enter_context(self.nc.semaphore("s_" + name))
        self.count[name] = 0

    def step(self, engine, fn, after):
        self.count[engine] += 1
        self.queue[engine].append((fn, list(flat(after)), engine, 1))
        return (engine, self.count[engine])

    def pe(self, fn, *after):
        return self.step("tensor", fn, after)

    def dve(self, fn, *after):
        return self.step("vector", fn, after)

    def act(self, fn, *after):
        return self.step("scalar", fn, after)

    def pool(self, fn, *after):
        return self.step("gpsimd", fn, after)

    def load(self, group, out, in_, *after, engine="sync"):
        if group not in self.sems:
            self.semaphore(group)
        self.count[group] += 16
        self.queue[engine].append((lambda e: e.dma_start(out, in_), list(flat(after)), group, 16))

    def rows(self, group, out, out_index, in_, in_index, *after):
        if group not in self.sems:
            self.semaphore(group)
        self.count[group] += 16
        at = [None if i is None else bass.IndirectOffsetOnAxis(i, 0) for i in (out_index, in_index)]
        self.queue["gpsimd"].append((lambda e: e.indirect_dma_start(out, at[0], in_, at[1], bounds_check=E * SLOTS - 1,
                                                                    oob_is_err=False), list(flat(after)), group, 16))

    def loaded(self, group):
        return (group, self.count[group])

    def barrier(self):
        now = [(e, self.count[e]) for e in ENGINES[:4]]
        for e in ENGINES:
            self.queue[e].append((None, now, None, 0))
        return now

    def emit(self, engine, eng):
        seen = {}
        for fn, after, sem, by in self.queue[engine]:
            for name, value in after:
                if seen.get(name, 0) < value:
                    eng.wait_ge(self.sems[name], value)
                    seen[name] = value
            if fn is not None:
                fn(eng).then_inc(self.sems[sem], by)


def flat(tokens):
    for t in tokens:
        if t is None:
            continue
        if isinstance(t, list):
            yield from flat(t)
        else:
            yield t


def matmuls(*group):
    def run(e):
        for out, lhsT, rhs, start, stop in group:
            last = e.matmul(out, lhsT, rhs, start=start, stop=stop, skip_group_check=True)
        return last
    return run


def transposes(*group):
    def run(e):
        for out, in_, ident in group:
            last = e.transpose(out, in_, ident)
        return last
    return run


def bc(ap, axis, n):
    ap = ap.unsqueeze(axis)
    shape = list(ap.shape)
    shape[axis] = n
    return ap.to_broadcast(shape)


def build(nc, d, kept, slots, out, stages):
    ctx = ExitStack()
    with ctx:
        P = Program(nc, ctx)
        WORDS = 53100
        mem = ctx.enter_context(nc.sbuf_tensor("mem", [128, WORDS], F32))
        ps = ctx.enter_context(nc.psum_tensor("ps", [128, 8, 512], F32))
        at = [0]

        def words(n):
            a = at[0]
            at[0] += n
            assert at[0] <= WORDS, at[0]
            return mem[:, a:a + n]

        def view(ap, pat, **k):
            return ap.rearrange(pat, **k)

        def tile3(a, b):
            return view(words(a * b), "p (a b) -> p a b", a=a)

        def tile4(a, b, c):
            return view(words(a * b * c), "p (a b c) -> p a b c", a=a, b=b)

        X = tile3(NT, D)
        XN = tile3(NT, D)
        xT = tile3(B, 34 + S)
        ident = words(128)
        onesf = words(128)
        lower = words(128)
        shiftm = words(128)
        carrym = words(128)
        ones3 = words(64).bitcast(BF16)
        hm = words(H)
        iota8 = words(E)
        identb = words(64).bitcast(BF16)
        maskb = view(words(512).bitcast(BF16), "p (m c) -> p m c", m=2)
        rotc = tile4(4, 2, 64)
        rots = tile4(4, 2, 64)
        ctxT = tile3(B, L)
        tauB = words(B)
        ptB = words(B)
        lenI = words(B).bitcast(I32)
        lenB = words(B)
        idx = words(L)
        sel3 = words(3)
        st = tile3(NT, 6)
        mv = tile3(NT, 2)
        va, rs, rt = words(NT), words(NT), words(NT)
        xw = {}

        def xweights(n):
            xw[n] = {k: words(128) for k in ("Wq", "Wk", "Wv", "Wo", "bv", "bo")}
            xw[n].update({k: words(1) for k in ("bq", "bk")})

        WgT = words(E)
        l2 = [dict(Wqkv=words(3072), Wo=tile3(8, 128), qs=tile3(2, 64)) for _ in range(2)]
        l2f = dict(W1=words(682), W2=tile3(3, 128), b1=words(6), g=words(1), b=words(1), b2=words(128))
        base5 = at[0]
        ctxk = tile3(B, D)
        dl3 = view(words(2 * 4 * L).bitcast(BF16), "p (a b c) -> p a b c", a=B, b=4)
        xweights("0")
        xweights("1")
        xw["3"] = xw["0"]
        w1T, w2T = words(512), tile3(4, 128)
        cvw, cvb = tile3(4, 3), words(4)
        Wa, WcT = words(128), tile3(2, 128)
        lng, lnb = words(1), words(1)
        WrT = words(E)
        masks = tile3(2, 64)
        base = at[0]

        free = {b: None for b in range(8)}

        def load_xw(n):
            g = "xw" + n
            for k in ("Wk", "Wv", "Wq", "Wo"):
                P.load(g, xw[n][k], d[f"L{n}{k}"])
            for k in ("bk", "bq"):
                P.load(g, xw[n][k], d[f"L{n}{k}"])
            for k in ("bv", "bo"):
                P.load(g, xw[n][k][0:1], d[f"L{n}{k}"])

        def load_l2(i, *after):
            w, g = l2[i % 2], f"l2_{i}"
            P.load(g, w["Wqkv"], d["Wqkv"][i], *after)
            P.load(g, w["Wo"], d["L2Wo"][i])
            P.load(g, w["qs"], d["qks"][i].partition_broadcast(128))

        def load_l2f(i, *after):
            w, g = l2f, f"l2f_{i}"
            P.load(g, w["W1"], d["W1"][i], *after)
            P.load(g, w["W2"][:, 0:2, :], d["W2"][i, 0:256, :].rearrange("(c p) n -> p c n", p=128))
            P.load(g, w["W2"][0:85, 2, :], d["W2"][i, 256:341, :])
            P.load(g, w["b1"], d["b1"][i])
            P.load(g, w["g"], d["ln_g"][i])
            P.load(g, w["b"], d["ln_b"][i])
            P.load(g, w["b2"][0:1], d["b2"][i])

        late = base + 12288 + 14000

        def make_delta(n, where):
            at[0] = where
            dlf, dl1, dlt = tile3(B, L), tile3(B, L), tile3(B, L)
            dlh = view(words(3 * 2 * L).bitcast(BF16), "p (a b c) -> p a b c", a=3, b=B)
            P.load(n, dlf[0:3], d["delta"].partition_broadcast(3))
            q3 = slice(0, 3)
            t = P.dve(lambda e: e.tensor_scalar(dl1[q3], dlf[q3], float(np.float32(1 / np.sqrt(8.0))), None, ALU.mult),
                      P.loaded(n), P.loaded("first"))
            for j in range(3):
                t = P.dve(lambda e, j=j: e.tensor_copy(dlh[q3, j], dl1[q3]), t)
                if j < 2:
                    t = P.dve(lambda e, j=j: e.tensor_tensor(dl1[q3], dl1[q3], dlh[q3, j], ALU.subtract), t)
            t = P.dve(lambda e: e.tensor_scalar(dlt[q3], dlh[q3, 0], sel3[q3, 0:1], None, ALU.mult), t)
            for j in (1, 2):
                t = P.dve(lambda e, j=j: e.scalar_tensor_tensor(dlt[q3], dlh[q3, j], sel3[q3, j:j + 1], dlt[q3],
                                                                ALU.mult, ALU.add), t)
            for h in range(4):
                t = P.dve(lambda e, h=h: e.tensor_copy(dl3[q3, :, h, :], dlt[q3]), t)
            return t

        g = "first"
        for t, n in ((X, None), (ident, "ident"), (ctxT, "ctxT"), (hm, "hm")):
            P.load(g, t, d[n] if n else d["x"].rearrange("(t p) d -> p t d", p=128))
        P.load(g, tauB, d["tau"].partition_broadcast(128))
        P.load(g, sel3[0:3], d["sel3"])
        load_xw("0")
        first = P.loaded("first")

        zeros = mem[:, late - 1024:late]
        P.pool(lambda e: e.memset(onesf, 1.0))
        P.pool(lambda e: e.memset(xT[:, :, 0:32], 0.0))
        c_zero = P.pool(lambda e: e.memset(zeros, 0.0))
        P.dve(lambda e: e.memset(ones3, 1.0))
        dl3_done = {"0": make_delta("delta", late)}
        dl3_done["1"] = dl3_done["0"]
        P.dve(lambda e: e.tensor_scalar(tauB, tauB, float(np.float32(1 / np.sqrt(8.0))), None, ALU.mult), first)
        P.barrier()

        g = "later"
        for t, n in ((lower, "lower"), (shiftm, "shiftm"), (carrym, "carrym"), (rotc, "rotc"), (rots, "rots"),
                     (masks, "masks")):
            P.load(g, t, d[n])
        P.load(g, ctxk[0:L], d["ctxk"])
        P.load(g, ptB, d["pt"].partition_broadcast(128))
        P.load(g, lenI, d["len"].partition_broadcast(128))
        P.load(g, idx, d["idx"].partition_broadcast(128))
        P.load(g, iota8, d["idx"][0:E].partition_broadcast(128))
        later = P.loaded("later")
        for k in ("x0", "x3"):
            for j in range(E * SLOTS // 1024):
                P.load("zero", slots[k][1024 * j:1024 * j + 1024, :].rearrange("(t p) d -> p t d", p=128),
                       view(zeros, "p (t d) -> p t d", d=D), c_zero)

        def load_rest():
            load_xw("1")
            for t, n in ((w1T, "w1T"), (w2T, "w2T"), (cvw, "cvw"), (cvb, "cvb"), (Wa, "Wa"), (WcT, "WcT"), (lng, "lng"),
                         (lnb, "lnb"), (WrT, "WrT"), (WgT, "WgT")):
                P.load("small", t, d[n])
            load_l2(0)
            load_l2(1)
            load_l2f(0)

        def later_constants():
            P.dve(lambda e: e.tensor_copy(identb, ident))
            for m in range(2):
                P.dve(lambda e, m=m: e.tensor_copy(view(maskb[:, m, :], "p (a k) -> p a k", a=8), bc(masks[:, m, :], 1, 8)),
                      later)
            P.dve(lambda e: e.tensor_copy(lenB, lenI), later)

        def rsqrt(y, a, tmp, *after):
            yi, ai = y.bitcast(I32), a.bitcast(I32)
            t = P.dve(lambda e: e.tensor_scalar(yi, ai, 1, None, ALU.arith_shift_right), *after)
            t = P.dve(lambda e: e.tensor_scalar(yi, yi, -1.0, float(0x5F3759DF), ALU.mult, ALU.add), t)
            for _ in range(3):
                t = P.dve(lambda e: e.tensor_tensor(tmp, y, y, ALU.mult), t)
                t = P.dve(lambda e: e.scalar_tensor_tensor(tmp, tmp, -0.5, a, ALU.mult, ALU.mult), t)
                t = P.dve(lambda e: e.scalar_tensor_tensor(y, tmp, 1.5, y, ALU.add, ALU.mult), t)
            return t

        def norm_steps(src, dst, b, after, out):
            g = range(4 * b, 4 * b + 4)
            c = slice(4 * b, 4 * b + 4)
            y, a, tmp = rs[:, c], va[:, c], rt[:, c]
            yi, ai = y.bitcast(I32), a.bitcast(I32)
            tok = {}

            def stats(i):
                tok[i] = P.dve(lambda e: e.bn_stats(st[:, i, :], src[:, i, :]), after[i])

            def aggregate(i):
                tok[i] = tok["y"] = P.dve(lambda e: e.bn_aggr(mv[:, i, :], st[:, i, :]), tok[i])

            def root(op):
                tok["y"] = P.dve(op, tok["y"])

            def apply(i):
                out[i] = P.dve(lambda e: e.tensor_scalar(dst[:, i, :], src[:, i, :], mv[:, i, 0:1], rs[:, i:i + 1],
                                                         ALU.subtract, ALU.mult), tok["y"])

            ops = [lambda e: e.tensor_scalar(a, mv[:, c, 1], 1e-5, None, ALU.add),
                   lambda e: e.tensor_scalar(yi, ai, 1, None, ALU.arith_shift_right),
                   lambda e: e.tensor_scalar(yi, yi, -1.0, float(0x5F3759DF), ALU.mult, ALU.add)]
            ops += [lambda e: e.tensor_tensor(tmp, y, y, ALU.mult),
                    lambda e: e.scalar_tensor_tensor(tmp, tmp, -0.5, a, ALU.mult, ALU.mult),
                    lambda e: e.scalar_tensor_tensor(y, tmp, 1.5, y, ALU.add, ALU.mult)] * 3
            return ([lambda i=i: stats(i) for i in g] + [lambda i=i: aggregate(i) for i in g]
                    + [lambda op=op: root(op) for op in ops] + [lambda i=i: apply(i) for i in g])

        def layernorm(src, dst, after=None, before_write=None):
            out = {}
            ready = {i: [after[i] if after else None, before_write] for i in range(NT)}
            for b in range(0, B, 2):
                for pair in zip(norm_steps(src, dst, b, ready, out), norm_steps(src, dst, b + 1, ready, out)):
                    for step in pair:
                        step()
            return [out[i] for i in range(NT)]

        def turn(src, ready, bank, evac, batches=None):
            got = []
            for b in batches or range(B):
                k = bank[b % len(bank)]
                t = P.pe(transposes(*[(ps[:, k, 128 * j:128 * j + 128], src[:, 4 * b + j, :], ident)
                                      for j in range(4)]), ready[4 * b:4 * b + 4], free[k])
                free[k] = evac(b, ps[:, k, :], t)
                got.append(free[k])
            return got

        def to_xT(b, p, t):
            return P.act(lambda e: e.activation(xT[:, b, 32:32 + S], p, ACT.Copy), t)

        def chunk(b):
            return xT[:, b, 32:32 + S]

        def tokens(i):
            return xT[:, i // 4, 32 + 128 * (i % 4):160 + 128 * (i % 4)]

        def add_rows(b, k, t):
            free[k] = P.dve(lambda e: e.tensor_tensor(X[:, 4 * b:4 * b + 4, :], X[:, 4 * b:4 * b + 4, :],
                                                      view(ps[:, k, :], "p (a c) -> p a c", a=4), ALU.add), t)
            return free[k]

        def xcond(n, where, arrive=None, last=None):
            at[0] = where
            w, wl = xw[n], P.loaded("xw" + n)
            kTs = words(B * L)
            kbd = tile4(B, H, L)
            vx = tile4(B, H, 9)
            qT = tile3(B, S)
            pb = [words(8 * L) for _ in range(2)]
            pts = [tile3(8, 128) for _ in range(2)]
            mx = [words(8) for _ in range(2)]
            rc = [words(H) for _ in range(2)]
            att = XN
            oT = words(512)
            rows, q, steps = {}, {}, []

            def prepare(b):
                ready = arrive(b) if arrive else {i: None for i in range(NT)}
                steps.extend(norm_steps(X, XN, b, ready, rows))

            def fill(m):
                for _ in range(min(m, len(steps))):
                    steps.pop(0)()

            def queries(b):
                xt = turn(XN, [rows.get(i) for i in range(NT)], (7,), to_xT, (b,))[0]
                t = P.pe(matmuls((ps[:, 7, :], w["Wq"], chunk(b), True, True)), xt, wl, free[7])
                free[7] = q[b] = P.act(lambda e: e.activation(qT[:, b, :], ps[:, 7, :], ACT.Identity, bias=bqs[:, b:b + 1],
                                                              scale=tauB[:, b:b + 1]), t, qs)

            bqs = words(B)
            assert at[0] <= late - 1024
            qs = P.dve(lambda e: e.tensor_tensor(bqs, bc(w["bq"][:, 0], 1, B), tauB, ALU.mult), wl)
            t = P.pe(matmuls((ps[:, 7, 0:B * L], w["Wk"], view(ctxT, "p b l -> p (b l)"), True, True)), wl, free[7])
            k = P.act(lambda e: e.activation(kTs, ps[:, 7, 0:B * L], ACT.Identity, bias=w["bk"]), t)
            free[7] = k
            t = P.pe(matmuls(*[m for b in range(B) for m in (
                (ps[0:L, 6, 128 * b:128 * b + 128], ctxT[:, b, :], w["Wv"], True, False),
                (ps[0:L, 6, 128 * b:128 * b + 128], onesf[0:1, 0:L], w["bv"][0:1], False, True))]), wl, free[6])
            v1 = P.dve(lambda e: e.memset(vx[0:L, :, :, 8:9], 1.0))
            v = P.act(lambda e: e.activation(view(vx, "p b h e -> p (b h) e")[0:L, :, 0:8],
                                             view(ps[0:L, 6, :], "p (a c) -> p a c", c=8), ACT.Copy), t)
            free[6] = v
            kb = {}

            def spread_keys(b):
                kb[b] = P.dve(lambda e: e.tensor_tensor(kbd[:, b], bc(kTs[:, b * L:b * L + L], 1, H), bc(hm, 2, L),
                                                        ALU.mult), k)

            if arrive:
                for b in range(B):
                    spread_keys(b)
            prepare(0)
            fill(99)
            if not arrive:
                spread_keys(0)
                steps.extend([lambda b=b: spread_keys(b) for b in range(1, B)])
            queries(0)

            NU = 2 * NT
            scored, lessened, exped, turned, attd = {}, {}, {}, {}, {}
            pb_free, pts_free = [None, None], [None, None]

            def score(u):
                i, hf, r = u // 2, u % 2, u % 2
                b = i // 4
                ms = []
                for j in range(2):
                    o = ps[:, 2 * r + j, 0:4 * L]
                    h0 = 8 * hf + 4 * j
                    ms += [(o, ones3[0:3, 0:128], view(dl3[0:3, b], "p h l -> p (h l)"), True, False),
                           (o, qT[:, b, 128 * (i % 4):128 * (i % 4) + 128],
                            view(kbd[:, b, h0:h0 + 4, :], "p h l -> p (h l)"), False, True)]
                scored[u] = P.pe(matmuls(*ms), q[b], dl3_done[n], kb[b], free[2 * r])

            def lessen(u):
                r = u % 2
                sc = view(ps[:, 2 * r:2 * r + 2, 0:4 * L], "p a (h l) -> p a h l", h=4)
                m = view(mx[r], "p (a h) -> p a h", a=2)
                o = view(pb[r], "p (a h l) -> p a h l", a=2, h=4)
                t = P.dve(lambda e: e.tensor_reduce(m, sc, AX.X, ALU.max), scored[u])
                fill(1)
                free[2 * r] = lessened[u] = P.dve(lambda e: e.tensor_tensor(o, sc, bc(m, 3, L), ALU.subtract), t, pb_free[r])

            def exponentials(u):
                r = u % 2
                exped[u] = P.act(lambda e: e.activation(pb[r], pb[r], ACT.Exp), lessened[u])

            def turn_p(u):
                r = u % 2
                turned[u] = []
                for j in range(2):
                    k = 4 + j
                    t = P.pe(transposes(*[(ps[0:L, k, 128 * h:128 * h + 128],
                                           pb[r][:, (4 * j + h) * L:(4 * j + h + 1) * L], ident)
                                          for h in range(4)]), exped[u], free[k])
                    pb_free[r] = t
                    o, s = view(pts[r][0:L, 4 * j:4 * j + 4, :], "p h c -> p (h c)"), ps[0:L, k, :]
                    free[k] = P.act(lambda e, o=o, s=s: e.activation(o, s, ACT.Copy), t, pts_free[r])
                    turned[u].append(free[k])

            def weigh(u):
                i, hf, r = u // 2, u % 2, u % 2
                b, z = i // 4, i % 2
                av = view(ps[:, 6 + z, 0:144], "p (h c) -> p h c", h=H)
                t = P.pe(matmuls(*[(av[:, 8 * hf + h, :], pts[r][0:L, h, :], vx[0:L, b, 8 * hf + h, :], True, True)
                                   for h in range(8)]), turned[u], v, v1, free[6 + z])
                pts_free[r] = t
                if hf == 1:
                    t = P.dve(lambda e: e.reciprocal(rc[z], av[:, :, 8]), t, attd.get(i - 2))
                    fill(1)
                    free[6 + z] = attd[i] = P.dve(lambda e: e.tensor_tensor(
                        view(att[:, i, :], "p (h c) -> p h c", h=H), av[:, :, 0:8], bc(rc[z], 2, 8), ALU.mult), t)

            def project(b, part):
                if part == 0:
                    t = P.pe(transposes(*[(ps[:, 7, 128 * j:128 * j + 128], att[:, 4 * b + j, :], ident)
                                          for j in range(4)]), attd[4 * b + 3], free[7])
                    free[7] = P.act(lambda e: e.activation(oT, ps[:, 7, :], ACT.Copy), t)
                else:
                    t = P.pe(matmuls(*[m for j in range(4) for m in (
                        (ps[:, 7, 128 * j:128 * j + 128], oT[:, 128 * j:128 * j + 128], w["Wo"], True, False),
                        (ps[:, 7, 128 * j:128 * j + 128], onesf[0:1, :], w["bo"][0:1], False, True))]), free[7])
                    add_rows(b, 7, t)

            for u in range(NU + 6):
                if u < NU:
                    score(u)
                    lessen(u)
                if 1 <= u <= NU:
                    turn_p(u - 1)
                if u < NU:
                    exponentials(u)
                if 2 <= u < NU + 2:
                    weigh(u - 2)
                done, at_ = (u - 2) // 8 - 1, (u - 2) % 8
                if done >= 0 and done < B and at_ in (0, 1):
                    project(done, at_)
                if u < NU:
                    b, at_ = u // 8 + 1, u % 8
                    if b < B:
                        if at_ == 0:
                            prepare(b)
                        fill(4)
                        if at_ == 6:
                            fill(99)
                            queries(b)
            if last:
                last()
            P.barrier()

        def places(probs, k_major, cap, *after):
            m8, ix, ixf = tile3(NT, 8), tile3(NT, 8), tile3(2, NT)
            oh = tile4(2, NT, E)
            a, c = tile4(2, NT, E), tile4(2, NT, E)
            pre = tile4(2, NT, E)
            rank, kept, wt, pos = (tile3(2, NT) for _ in range(4))
            put, get = (tile3(2, NT) for _ in range(2))
            iu = ix.bitcast(U32)
            for i in range(NT):
                t = P.dve(lambda e, i=i: e.max(m8[:, i, :], probs[:, i, :]), *after)
            for i in range(NT):
                t = P.dve(lambda e, i=i: e.max_index(iu[:, i, :], m8[:, i, :], probs[:, i, :]), t)
            for k in range(2):
                t2 = P.dve(lambda e, k=k: e.tensor_copy(ixf[:, k, :], iu[:, :, k]), t)
            for k in range(2):
                t = P.dve(lambda e, k=k: e.tensor_tensor(oh[:, k], bc(iota8, 1, NT), bc(ixf[:, k, :], 2, E),
                                                         ALU.is_equal), t2)
            n = 2 * NT * E
            fl = lambda z: view(z, "p k t e -> p (k t e)")
            t = P.pe(matmuls((ps[:, 0, 0:n], lower, fl(oh), True, True),
                             (ps[:, 1, 0:n], onesf, fl(oh), True, True)), t, free[0], free[1])
            x1 = P.dve(lambda e: e.tensor_copy(fl(pre), ps[:, 0, 0:n]), t)
            t = P.dve(lambda e: e.tensor_copy(fl(a), ps[:, 1, 0:n]), t)
            free[0] = free[1] = t
            src, dst = a, c
            for s in (1, 2, 4, 8):
                t1 = P.dve(lambda e, s=s, o=dst, i=src: e.tensor_tensor(o[:, :, s:, :], i[:, :, s:, :], i[:, :, :NT - s, :],
                                                                      ALU.add), t)
                t = P.dve(lambda e, s=s, o=dst, i=src: e.tensor_copy(o[:, :, :s, :], i[:, :, :s, :]), t)
                src, dst = dst, src
            assert src is a
            t = P.dve(lambda e: e.tensor_tensor(fl(pre), fl(pre), fl(a), ALU.add), t, x1)
            t = P.dve(lambda e: e.tensor_tensor(fl(pre), fl(pre), ps[:, 1, 0:n], ALU.subtract), t)
            free[1] = t
            r0, r1 = pre[:, 0], pre[:, 1]
            if k_major:
                t = P.dve(lambda e: e.tensor_tensor(r1, r1, bc(a[:, 0, NT - 1, :], 1, NT), ALU.add), t)
            else:
                t = P.dve(lambda e: e.tensor_tensor(r0, r0, r1, ALU.add), t)
                t = P.dve(lambda e: e.tensor_copy(r1, r0), t)
            t = P.dve(lambda e: e.tensor_tensor(fl(pre), fl(pre), fl(oh), ALU.mult), t)
            t = P.dve(lambda e: e.tensor_reduce(rank, pre, AX.X, ALU.add), t)
            kd = P.dve(lambda e: e.tensor_scalar(kept, rank, float(cap), None, ALU.is_lt), t)
            wd = P.dve(lambda e: e.tensor_tensor(wt, kept, m8[:, :, 0:2].rearrange("p t k -> p k t"), ALU.mult), kd)
            t = P.dve(lambda e: e.scalar_tensor_tensor(pos, ixf, float(SLOTS), rank, ALU.mult, ALU.add), kd)
            t = P.dve(lambda e: e.scalar_tensor_tensor(pos, kept, -16384.0, pos, ALU.mult, ALU.add), t)
            pd = P.dve(lambda e: e.tensor_scalar(put.bitcast(I32), pos, 16384.0, None, ALU.add), t)
            t = P.dve(lambda e: e.tensor_scalar(rank, rank, float(cap - 1), None, ALU.min), pd)
            t = P.dve(lambda e: e.scalar_tensor_tensor(pos, ixf, float(SLOTS), rank, ALU.mult, ALU.add), t)
            gd = P.dve(lambda e: e.tensor_copy(get.bitcast(I32), pos), t)
            return (wt, wd), (put.bitcast(U32), pd), (get.bitcast(U32), gd)

        def softmax8(lg, probs, eps, *after):
            m, s = words(NT), words(NT)
            t = P.dve(lambda e: e.tensor_reduce(m, lg, AX.X, ALU.max), *after)
            t = P.dve(lambda e: e.tensor_tensor(probs, lg, bc(m, 2, E), ALU.subtract), t)
            t = P.act(lambda e: e.activation(probs, probs, ACT.Exp), t)
            t = P.dve(lambda e: e.tensor_reduce(s, probs, AX.X, ALU.add), t)
            if eps:
                t = P.dve(lambda e: e.tensor_scalar(s, s, eps, None, ALU.add), t)
            t = P.dve(lambda e: e.reciprocal(s, s), t)
            return P.dve(lambda e: e.tensor_tensor(probs, probs, bc(s, 2, E), ALU.mult), t)

        def router(wT, lg, xt, lo, hi):
            t = P.pe(matmuls(*[(ps[:, 2, E * i:E * i + E], tokens(i), wT, True, True) for i in range(NT)]), xt, small, free[2])
            free[2] = P.dve(lambda e: e.tensor_scalar(lg, view(ps[:, 2, 0:NT * E], "p (t e) -> p t e", e=E), lo, hi,
                                                      ALU.max, ALU.min), t)
            return free[2]

        def experts(tag, cap, wt, put, get, rows, columns, up, y, down, bias, wl):
            xs, ys = slots["x" + tag], slots["y" + tag]
            xe = tile4(E, 5, 128)
            gathered = view(xe, "p e t d -> p (e t d)")[:, 0:2 * NT * 128].rearrange("p (k t d) -> p k t d", k=2, t=NT)
            xTe = [words(SLOTS) for _ in range(2)]
            hT = [tile3(4, SLOTS) for _ in range(2)]
            ye = [tile3(5, 128) for _ in range(2)]
            halves = [slice(0, (cap + 1) // 2), slice((cap + 1) // 2, cap)]
            for i in range(NT):
                for k in range(2):
                    P.rows("put" + tag, xs, put[0][:, k, i:i + 1], XN[:, i, :], None, put[1], rows[i], P.loaded("zero"))
            for e in range(E):
                P.load(f"xe{tag}{e}", xe[:, e], xs[SLOTS * e:SLOTS * e + SLOTS, :].rearrange("(t p) d -> p t d", p=128),
                       P.loaded("put" + tag))
            xT_free, h_free = [None, None], [None, None]
            y_free = [P.pool(lambda e, r=r: e.memset(ye[r][:, 4, :], 0.0)) for r in range(2)]
            hid, cols = {}, {}
            cell = [0]

            def turn_in(e):
                t = P.pe(transposes(*[(ps[:, 6, 128 * j:128 * j + 128], xe[:, e, j, :], ident) for j in range(4)]),
                         P.loaded(f"xe{tag}{e}"), free[6])
                t2 = P.pe(transposes((ps[:, 7, 0:128], xe[:, e, 4, :], ident)), free[7])
                free[6] = columns(xTe[e % 2][:, 0:512], ps[:, 6, :], t, xT_free[e % 2])
                free[7] = cols[e] = columns(xTe[e % 2][:, 512:640], ps[:, 7, 0:128], t2, xT_free[e % 2])

            def upward(e, chunks):
                for c in chunks:
                    for z in halves:
                        hid.setdefault(e, []).append(up(e, c, xTe[e % 2][:, z], hT[e % 2][:, c, z], cell[0],
                                         [cols[e], wl], h_free[e % 2], z.stop - z.start))
                        cell[0] += 1
                xT_free[e % 2] = ("tensor", P.count["tensor"])

            def downward(e):
                r = e % 2
                ms = []
                for j in range(5):
                    m = min(128, cap - 128 * j)
                    o = ps[0:m, 6 + j // 4, 128 * (j % 4):128 * (j % 4) + 128]
                    ms += [(o, hT[r][:, c, 128 * j:128 * j + m], down[:, e, c, :], c == 0, c == 3) for c in range(4)]
                h_free[r] = t = P.pe(matmuls(*ms), hid[e], free[6], free[7])
                m = cap - 512
                free[6] = y(e, view(ye[r][:, 0:4, :], "p t d -> p (t d)"), ps[:, 6, :], 4, 128, t, y_free[r], wl)
                free[7] = y(e, ye[r][0:m, 4, :], ps[0:m, 7, 0:128], 1, m, t, y_free[r], wl)
                g = f"ye{tag}{e}"
                P.load(g, ys[SLOTS * e:SLOTS * e + SLOTS, :].rearrange("(t p) d -> p t d", p=128), ye[r], free[6], free[7])
                y_free[r] = P.loaded(g)

            turn_in(0)
            for e in range(E + 1):
                if e < E:
                    upward(e, (0, 1))
                    if e + 1 < E:
                        turn_in(e + 1)
                    upward(e, (2, 3))
                if e >= 1:
                    downward(e - 1)
            stored = [P.loaded(f"ye{tag}{e}") for e in range(E)]
            P.barrier()
            for b in range(B):
                for i in range(4 * b, 4 * b + 4):
                    for k in range(2):
                        P.rows(f"get{tag}{b}", gathered[:, k, i, :], None, ys, get[0][:, k, i:i + 1], get[1], stored)

            def arrive(b):
                out = {}
                for i in range(4 * b, 4 * b + 4):
                    t = P.dve(lambda en, i=i: en.scalar_tensor_tensor(
                        X[:, i, :], gathered[:, 0, i, :], wt[0][:, 0, i:i + 1], X[:, i, :], ALU.mult, ALU.add),
                        P.loaded(f"get{tag}{b}"), wt[1])
                    out[i] = t
                for i in range(4 * b, 4 * b + 4):
                    out[i] = P.dve(lambda en, i=i: en.scalar_tensor_tensor(
                        X[:, i, :], gathered[:, 1, i, :], wt[0][:, 1, i:i + 1], X[:, i, :], ALU.mult, ALU.add), out[i])
                return out

            return arrive

        def l0_ffn():
            at[0] = base
            W12 = tile3(E, 1024)
            W3 = tile4(E, 4, 128)
            lg, probs = tile3(NT, E), tile3(NT, E)
            sg = [words(320) for _ in range(3)]
            sgf = [None] * 3
            wl = P.loaded("moe0")
            ln = layernorm(X, XN)
            ln = layernorm(XN, XN, ln)

            def columns(o, p, t, *after):
                return P.act(lambda e: e.activation(o, p, ACT.Identity, bias=lnb, scale=lng), t, small, *after)

            xt = turn(XN, ln, (6, 7), lambda b, p, t: columns(chunk(b), p, t))
            t = router(WrT, lg, xt, -10000.0, 10000.0)
            t = softmax8(lg, probs, 1e-12, t)
            wt, put, get = places(probs, False, CAP0, t)

            def up(e, c, cols, o, cell, ready, hfree, n):
                r = cell % 3
                k = 2 * r
                t = P.pe(matmuls((ps[:, k, 0:n], W12[:, e, 128 * c:128 * c + 128], cols, True, True),
                                 (ps[:, k + 1, 0:n], W12[:, e, 512 + 128 * c:640 + 128 * c], cols, True, True)),
                         ready, free[k], free[k + 1])
                a = P.act(lambda en: en.activation(sg[r][:, 0:n], ps[:, k, 0:n], ACT.Silu), t, sgf[r])
                m = P.dve(lambda en: en.tensor_tensor(o, ps[:, k + 1, 0:n], sg[r][:, 0:n], ALU.mult), a, hfree)
                sgf[r] = free[k] = free[k + 1] = m
                return m

            def y(e, o, p, nt, rows, t, *after):
                return P.act(lambda en: en.activation(o, p, ACT.Copy), t, *after)

            return experts("0", CAP0, wt, put, get, ln, columns, up, y, W3, None, wl)

        def l3_ffn():
            at[0] = base
            W1 = tile3(E, 512)
            W2 = tile4(E, 4, 128)
            b1 = tile3(E, 4)
            b2 = tile3(E, 128)
            at[0] = max(at[0], base + 12288)
            lg, probs = tile3(NT, E), tile3(NT, E)
            wl = P.loaded("moe3")
            ln = layernorm(X, XN)
            xt = turn(XN, ln, (6, 7), to_xT)
            t = router(WgT, lg, xt, -3.0e38, 3.0e38)
            t = softmax8(lg, probs, 0.0, t)
            wt, put, get = places(probs, True, CAP3, t)

            def columns(o, p, t, *after):
                return P.dve(lambda e: e.tensor_copy(o, p), t, *after)

            def up(e, c, cols, o, cell, ready, hfree, n):
                k = cell % 6
                t = P.pe(matmuls((ps[:, k, 0:n], W1[:, e, 128 * c:128 * c + 128], cols, True, True)), ready, free[k])
                free[k] = P.act(lambda en: en.activation(o, ps[:, k, 0:n], ACT.Gelu, bias=b1[:, e, c:c + 1]), t, hfree)
                return free[k]

            def y(e, o, p, nt, rows, t, *after):
                if nt == 1:
                    return P.dve(lambda en: en.tensor_tensor(o, p, b2[0:rows, e, :], ALU.add), t, *after)
                return P.dve(lambda en: en.tensor_tensor(view(o, "p (t d) -> p t d", t=nt), view(p, "p (t d) -> p t d", t=nt),
                                                         bc(b2[0:rows, e, :], 1, nt), ALU.add), t, *after)

            return experts("3", CAP3, wt, put, get, ln, columns, up, y, W2, b2, wl)

        def load_moe0():
            at[0] = base
            W12 = tile3(E, 1024)
            W3 = tile4(E, 4, 128)
            for e in range(E):
                P.load("moe0", W12[:, e, :], d["W12T"][e])
                P.load("moe0", W3[:, e], d["W3T"][e])

        def load_moe3():
            at[0] = base
            W1 = tile3(E, 512)
            W2 = tile4(E, 4, 128)
            b1 = tile3(E, 4)
            b2 = tile3(E, 128)
            for e in range(E):
                P.load("moe3", W1[:, e, :], d["L3W1"][e])
                P.load("moe3", W2[:, e], d["L3W2"][e].rearrange("(c p) n -> p c n", p=128))
            P.load("moe3", b1, d["L3b1"])
            P.load("moe3", b2, d["L3b2"].partition_broadcast(128))

        def l1_ffn():
            at[0] = base
            hp = tile4(B, 4, S + 2)
            y = tile4(4, B, S)
            hs = view(view(hp, "p b c s -> p b (c s)")[:, :, 0:2048], "p b (t c) -> p b t c", t=4)
            q2 = view(words(2 * 4 * 256).bitcast(BF16), "p (r t c) -> p r t c", r=2, t=4)
            q2T = view(words(2 * 256).bitcast(BF16), "p (r c n) -> p r c n", r=2, c=4)
            amax, sc1, inv = words(NT), words(NT), words(NT)
            inv2 = words(NT)
            wq1 = words(512)
            wq2 = view(words(256).bitcast(BF16), "p (c n) -> p c n", c=4)
            wt = words(512)
            ws, wm, wr = words(2), words(2), words(2)
            w2f = view(w2T, "p c n -> p (c n)")
            t = P.dve(lambda e: e.tensor_reduce(ws[:, 0:1], w1T, AX.X, ALU.add, apply_absolute_value=True), small)
            t = P.dve(lambda e: e.tensor_reduce(ws[:, 1:2], w2f, AX.X, ALU.add, apply_absolute_value=True), small)
            t = P.pe(matmuls((ps[:, 0, 0:2], onesf, ws, True, True)), t, free[0])
            t = P.dve(lambda e: e.tensor_scalar(wm, ps[:, 0, 0:2], 1.0 / 65536, 1e-5, ALU.mult, ALU.max), t)
            free[0] = t
            t = P.dve(lambda e: e.reciprocal(wr, wm), t)
            a = P.dve(lambda e: e.tensor_scalar(wt, w1T, wr[:, 0:1], ROUND, ALU.mult, ALU.add), t)
            a = P.dve(lambda e: e.tensor_scalar(wt, wt, ROUND, -1.0, ALU.subtract, ALU.max), a)
            w1d = P.dve(lambda e: e.tensor_scalar(wq1, wt, 1.0, wm[:, 0:1], ALU.min, ALU.mult), a)
            a = P.dve(lambda e: e.tensor_scalar(wt, w2f, wr[:, 1:2], ROUND, ALU.mult, ALU.add), w1d)
            a = P.dve(lambda e: e.tensor_scalar(wt, wt, ROUND, -1.0, ALU.subtract, ALU.max), a)
            w2d = P.dve(lambda e: e.tensor_scalar(view(wq2, "p c n -> p (c n)"), wt, 1.0, None, ALU.min), a)
            pads = [P.pool(lambda e, s=s: e.memset(hp[:, :, :, s:s + 1], 0.0)) for s in (0, S + 1)]

            def scales(c, src, *after):
                t = P.dve(lambda e: e.tensor_reduce(amax[:, c], src, AX.X, ALU.max, apply_absolute_value=True), *after)
                t = P.dve(lambda e: e.tensor_scalar(amax[:, c], amax[:, c], 1e-5, None, ALU.max), t)
                t1 = P.dve(lambda e: e.tensor_scalar(inv[:, c], amax[:, c], 1.0 / 127, None, ALU.mult), t)
                t = P.dve(lambda e: e.reciprocal(sc1[:, c], amax[:, c]), t)
                return P.dve(lambda e: e.tensor_scalar(sc1[:, c], sc1[:, c], 127.0, None, ALU.mult), t), t1

            xt, rows = {}, {}

            def prepare(b0):
                for pair in zip(*[norm_steps(X, XN, b, {i: None for i in range(NT)}, rows) for b in (b0, b0 + 1)]):
                    for step in pair:
                        step()
                g = range(4 * b0, 4 * b0 + 8)
                t = scales(slice(4 * b0, 4 * b0 + 8), XN[:, 4 * b0:4 * b0 + 8, :], [rows[i] for i in g])
                a = {i: P.dve(lambda e, i=i: e.tensor_scalar(XN[:, i, :], XN[:, i, :], sc1[:, i:i + 1], ROUND,
                                                             ALU.mult, ALU.add), t[0]) for i in g}
                a = {i: P.dve(lambda e, i=i: e.tensor_scalar(XN[:, i, :], XN[:, i, :], ROUND, -128.0,
                                                             ALU.subtract, ALU.max), a[i]) for i in g}
                for i in g:
                    rows[i] = P.dve(lambda e, i=i: e.tensor_scalar(XN[:, i, :], XN[:, i, :], 127.0, inv[:, i:i + 1],
                                                                   ALU.min, ALU.mult), a[i], t[1])
                for b in (b0, b0 + 1):
                    xt[b] = turn(XN, [rows.get(i) for i in range(NT)], (6, 7), to_xT, (b,))[0]

            conved, silu, hsd, inv2d, q2d, q2free = {}, {}, {}, {}, {}, [None, None]

            def hidden(n):
                b, c, k = n // 4, n % 4, n % 4
                o = y[:, c, b, :]
                t = P.pe(matmuls((ps[:, k, :], wq1[:, 128 * c:128 * c + 128], chunk(b), True, True)), xt[b], w1d, free[k])
                m = P.act(lambda e: e.activation(o, ps[:, k, :], ACT.Identity, bias=cvb[:, c:c + 1], scale=cvw[:, c, 1:2]),
                          t, small)
                t = free[k] = P.act(lambda e: e.activation(hp[:, b, c, 1:S + 1], ps[:, k, :], ACT.Copy), t)
                for s in (0, 2):
                    t = P.dve(lambda e, s=s: e.scalar_tensor_tensor(
                        o, hp[:, b, c, s:s + S], cvw[:, c, s:s + 1], o, ALU.mult, ALU.add), t, m, pads)
                conved[n] = t

            def activate(n):
                b, c = n // 4, n % 4
                silu[n] = P.act(lambda e: e.activation(y[:, c, b, :], y[:, c, b, :], ACT.Silu), conved[n])

            def back(i):
                b, j, k = i // 4, i % 4, 4 + i % 2
                t = P.pe(transposes(*[(ps[:, k, 128 * c:128 * c + 128], y[:, c, b, 128 * j:128 * j + 128], ident)
                                      for c in range(4)]), [silu[4 * b + c] for c in range(4)], free[k])
                hsd[i] = free[k] = P.act(lambda e: e.activation(hs[:, b, j, :], ps[:, k, :], ACT.Copy), t)

            def round_off(b):
                c, r = slice(4 * b, 4 * b + 4), b % 2
                t = scales(c, hs[:, b], [hsd[4 * b + j] for j in range(4)])
                inv2d[b] = P.dve(lambda e: e.tensor_scalar(inv2[:, c], inv[:, c], wm[:, 1:2], None, ALU.mult), t[1])
                a = [P.dve(lambda e, j=j: e.tensor_scalar(hs[:, b, j, :], hs[:, b, j, :], sc1[:, 4 * b + j:4 * b + j + 1],
                                                          ROUND, ALU.mult, ALU.add), t[0]) for j in range(4)]
                a = [P.dve(lambda e, j=j: e.tensor_scalar(hs[:, b, j, :], hs[:, b, j, :], ROUND, -128.0,
                                                          ALU.subtract, ALU.max), a[j]) for j in range(4)]
                for j in range(4):
                    q2d[4 * b + j] = P.dve(lambda e, j=j: e.tensor_scalar(q2[:, r, j, :], hs[:, b, j, :], 127.0, None,
                                                                          ALU.min), a[j], q2free[r])

            turned, qf = {}, [None, None]

            def columns(i):
                b, j, r = i // 4, i % 4, i % 2
                pt = ps[:, 4 + r, 0:256].bitcast(BF16)
                t = P.pe(transposes(*[(pt[:, 128 * c:128 * c + 128], q2[:, b % 2, j, 128 * c:128 * c + 128], identb)
                                      for c in range(4)]), q2d[i], free[4 + r])
                q2free[b % 2] = t
                turned[i] = free[4 + r] = P.act(lambda e: e.activation(view(q2T[:, r], "p c n -> p (c n)"), pt, ACT.Copy),
                                                t, qf[r])

            def downward(i):
                b, r, k = i // 4, i % 2, 6 + i % 2
                t = P.pe(matmuls(*[(ps[:, k, 0:128], q2T[:, r, c, :], wq2[:, c, :], c == 0, c == 3) for c in range(4)]),
                         turned[i], w2d, free[k])
                qf[r] = t
                free[k] = P.dve(lambda e: e.scalar_tensor_tensor(X[:, i, :], ps[:, k, 0:128], inv2[:, i:i + 1],
                                                                 X[:, i, :], ALU.mult, ALU.add), t, inv2d[b])

            prepare(0)
            for n in range(4 * B + 14):
                if n == 6:
                    prepare(2)
                if n < 4 * B:
                    hidden(n)
                if 1 <= n <= 4 * B:
                    activate(n - 1)
                if 0 <= n - 6 < 4 * B:
                    back(n - 6)
                if n >= 9 and (n - 9) % 4 == 0 and (n - 9) // 4 < B:
                    round_off((n - 9) // 4)
                if 0 <= n - 13 < 4 * B:
                    columns(n - 13)
                if 0 <= n - 14 < 4 * B:
                    downward(n - 14)
            P.barrier()

        def l2_xcond():
            at[0] = base
            st_, en_ = words(B), words(B)
            m1, keep, neg, gs = tile3(B, L), tile3(B, L), tile3(B, L), tile3(B, L)
            zT = tile3(B, S)
            sb = [tile3(4, L) for _ in range(2)]
            mx = words(NT)
            sm = words(NT)
            pT = [words(512) for _ in range(2)]
            cT = [words(512) for _ in range(2)]
            th = [words(512) for _ in range(2)]
            ib = bc(idx, 1, B)
            t = P.dve(lambda e: e.tensor_scalar(st_, ptB, 16.0, 0.0, ALU.subtract, ALU.max))
            t2 = P.dve(lambda e: e.tensor_scalar(en_, ptB, 16.0, None, ALU.add))
            t2 = P.dve(lambda e: e.tensor_tensor(en_, en_, lenB, ALU.min), t2)
            t = P.dve(lambda e: e.tensor_tensor(m1, ib, bc(st_, 2, L), ALU.is_lt), t)
            t2 = P.dve(lambda e: e.tensor_tensor(neg, ib, bc(en_, 2, L), ALU.is_gt), t2)
            t = P.dve(lambda e: e.tensor_tensor(m1, m1, neg, ALU.max), t, t2)
            t1 = P.dve(lambda e: e.tensor_scalar(keep, m1, -1.0, 1.0, ALU.mult, ALU.add), t)
            t2 = P.dve(lambda e: e.tensor_scalar(neg, m1, -1.0e9, None, ALU.mult), t)
            t = P.dve(lambda e: e.tensor_tensor(gs, ib, bc(ptB, 2, L), ALU.subtract))
            t = P.act(lambda e: e.activation(gs, gs, ACT.Square), t)
            gd = P.act(lambda e: e.activation(gs, gs, ACT.Exp, scale=-1.0 / 128), t)
            ln = layernorm(X, XN)
            xt = turn(XN, ln, (6, 7), to_xT)
            z = []
            for b in range(B):
                k = 6 + b % 2
                t = P.pe(matmuls((ps[:, k, :], Wa, chunk(b), True, True)), xt[b], small, free[k])
                free[k] = P.act(lambda e, b=b, k=k: e.activation(zT[:, b, :], ps[:, k, :], ACT.Copy), t)
                z.append(free[k])
            pTf, cTf, thf = [None, None], [None, None], [None, None]
            sf, ex, turned = [None, None], {}, {}

            def attend(b):
                k = b % 2
                s = sb[k]
                c = slice(4 * b, 4 * b + 4)
                p = view(ps[:, k, 0:4 * L], "p (t l) -> p t l", t=4)
                t = P.pe(matmuls(*[(p[:, j, :], zT[:, b, 128 * j:128 * j + 128], ctxT[:, b, :], True, True)
                                   for j in range(4)]), z[b], free[k])
                t = free[k] = P.dve(lambda e: e.tensor_tensor(s, p, bc(keep[:, b, :], 1, 4), ALU.mult), t, t1, sf[k])
                t = P.dve(lambda e: e.tensor_tensor(s, s, bc(neg[:, b, :], 1, 4), ALU.add), t, t2)
                t = P.dve(lambda e: e.tensor_reduce(mx[:, c], s, AX.X, ALU.max), t)
                t = P.dve(lambda e: e.tensor_tensor(s, s, bc(mx[:, c], 2, L), ALU.subtract), t)
                ex[b] = P.act(lambda e: e.activation(s, s, ACT.Exp), t)

            def weights(b):
                s = sb[b % 2]
                c = slice(4 * b, 4 * b + 4)
                t = P.dve(lambda e: e.tensor_reduce(sm[:, c], s, AX.X, ALU.add), ex[b])
                t = P.dve(lambda e: e.reciprocal(sm[:, c], sm[:, c]), t)
                t = P.dve(lambda e: e.tensor_tensor(s, s, bc(sm[:, c], 2, L), ALU.mult), t)
                ex[b] = P.dve(lambda e: e.tensor_tensor(s, s, bc(gs[:, b, :], 1, 4), ALU.mult), t, gd)

            def tp(b):
                k = 2 + b % 2
                t = P.pe(transposes(*[(ps[0:L, k, 128 * j:128 * j + 128], sb[b % 2][:, j, :], ident) for j in range(4)]),
                         ex[b], free[k])
                sf[b % 2] = t
                turned[b] = free[k] = P.act(lambda e: e.activation(pT[b % 2][0:L], ps[0:L, k, :], ACT.Copy), t, pTf[b % 2])

            context, gated = {}, {}

            def weigh(b):
                r = b % 2
                k = 4 + r
                pTf[r] = t = P.pe(matmuls((ps[:, k, :], ctxk[0:L, b, :], pT[r][0:L], True, True)), turned[b], free[k])
                context[b] = free[k] = P.act(lambda e: e.activation(cT[r], ps[:, k, :], ACT.Copy), t, cTf[r])

            def gate(b):
                r = b % 2
                t = P.pe(matmuls(*[m for j in range(4) for m in (
                    (ps[:, 6 + r, 128 * j:128 * j + 128], cT[r][:, 128 * j:128 * j + 128], WcT[:, 0, :], True, False),
                    (ps[:, 6 + r, 128 * j:128 * j + 128], tokens(4 * b + j), WcT[:, 1, :], False, True))]), context[b],
                    free[6 + r])
                cTf[r] = t
                gated[b] = free[6 + r] = P.act(lambda e: e.activation(th[r], ps[:, 6 + r, :], ACT.Tanh), t, thf[r])

            def add(b):
                r = b % 2
                thf[r] = P.dve(lambda e: e.tensor_tensor(X[:, 4 * b:4 * b + 4, :], X[:, 4 * b:4 * b + 4, :],
                                                         view(th[r], "p (a c) -> p a c", a=4), ALU.add), gated[b])

            for b in range(B + 4):
                if b < B:
                    attend(b)
                if 1 <= b <= B:
                    weights(b - 1)
                    tp(b - 1)
                if 0 <= b - 2 < B:
                    weigh(b - 2)
                if 0 <= b - 3 < B:
                    gate(b - 3)
                if 0 <= b - 4 < B:
                    add(b - 4)
            P.barrier()

        def l2_ffn():
            at[0] = base5
            Qbd = [view(words(2 * 8 * 4 * 64), "p (b c w h q) -> p b c w h q", b=2, c=8, w=4, h=2) for _ in range(2)]
            kT = [tile4(2, 8, 160) for _ in range(2)]
            clear = view(mem[:, base5:base5 + 2 * 4096], "p (r n) -> p r n", r=2)
            VN = [tile3(2, 1024) for _ in range(2)]
            VS = tile3(2, 1024)
            xn = view(XN, "p t d -> p (t d)")
            T1 = [[words(1024), words(1024)], [words(1024), xn[:, 1024:2048]]]
            T2, SQ = words(1024), words(1024)
            PB = [tile4(8, 2, 64) for _ in range(2)]
            PT = view(words(2048), "p (c b h w q) -> p c b h w q", c=8, b=2, h=2, w=2)
            oT = tile4(8, 2, 128)
            CT, SN = tile4(4, 2, 64), tile4(4, 2, 64)
            ss, sr, stmp = ([words(2 * H) for _ in range(2)] for _ in range(3))
            mxs, sms = ([words(16) for _ in range(2)] for _ in range(2))
            warm = words(1)
            queries = view(Qbd[0], "p b c w h q -> p (b c w h q)")
            hT = tile3(3, 512), view(queries[:, 0:1536], "p (c n) -> p c n", c=3)
            gl = [[xn[:, 0:512], xn[:, 512:1024], words(512)], [queries[:, 1536 + 512 * c:2048 + 512 * c] for c in range(3)]]
            zeroed = P.pool(lambda e: e.memset(xT[:, :, 32:33], 0.0))
            zeroed = P.pool(lambda e: e.memset(VS, 0.0), zeroed)
            zeroed = P.pool(lambda e: e.memset(clear, 0.0), P.loaded("xw0"), P.loaded("xw1"), small, zeroed)
            zeroed = P.pool(lambda e: e.memset(view(PT, "p c b h w q -> p (c b h w q)"), 0.0), zeroed)
            rows = kept.rearrange("(t p) d -> p t d", p=128)
            P.load("kept", rows, X)
            normed_rows = layernorm(X, X, before_write=P.loaded("kept"))

            xready = {b: normed_rows[4 * b + 3] for b in range(B)}
            xfree = {b: None for b in range(B)}
            xt, tables, tables_free = {}, {}, None
            NU = 4 * 2 * DEPTH
            NG = 2 * NU
            h3 = lambda z: view(z, "p (h c) -> p h c", c=64)

            def place(u):
                hl, t4 = divmod(u, 4)
                return hl, hl // 2, hl % 2, t4

            def turn_x(hl, bb, k):
                b = 2 * (hl % 2) + bb
                t = P.pe(transposes(*[(ps[:, k, 128 * j:128 * j + 128], X[:, 4 * b + j, :], ident) for j in range(4)]),
                         xready[b], free[k])
                P.act(lambda e: e.activation(xT[0:64, b, 32:32 + S], ps[0:64, k, :], ACT.Copy), t, xfree[b], zeroed)
                free[k] = xt[(hl, bb)] = P.act(lambda e: e.activation(xT[64:128, b, 33:32 + S], ps[64:128, k, 0:S - 1],
                                                                      ACT.Copy), t)

            def make_tables(l):
                w = l2[l % 2]
                for k in range(2):
                    P.pool(lambda e, k=k: e.tensor_tensor(CT[:, :, k, :], rotc[:, :, k, :], bc(w["qs"][:, k, :], 1, 4),
                                                          ALU.mult), P.loaded(f"l2_{l}"), tables_free)
                    for a in range(2):
                        tables[l] = P.pool(lambda e, k=k, a=a: e.tensor_tensor(
                            SN[:, :, k, 32 * a:32 * a + 32], rots[:, :, k, 32 * a:32 * a + 32],
                            bc(w["qs"][:, k, 32 - 32 * a:64 - 32 * a], 1, 4), ALU.mult))

            def evacuate(n, out, src, *after):
                if n % 2 == 0:
                    return P.act(lambda e: e.activation(out, src, ACT.Copy), *after)
                return P.dve(lambda e: e.tensor_copy(out, src), *after)

            T2f, SQf, added = [None, None], None, [None, None]
            T1f, ssf, mxf = [[None, None], [None, None]], [None, None], [None, None]
            Qf, Kf = [None, None], [None, None]
            qd, kd, normed = {}, {}, {}

            def columns(u, bb):
                hl, l, bp, t4 = place(u)
                return xT[:, 2 * bp + bb, 32 + 128 * t4:160 + 128 * t4]

            def rotate(r, i):
                u, bb = divmod(r, 2)
                nonlocal SQf, tables_free
                hl, l, bp, t4 = place(u)
                w = l2[l % 2]
                k, j = i // 2, i % 2
                z = bb
                t1, hh, cols = T1[z][k], slice(8 * j, 8 * j + 8), slice(512 * j, 512 * j + 512)
                o = (0, 1, 2, 5)[i]
                p = P.pe(matmuls((ps[:, o, :], columns(u, bb),
                                  w["Wqkv"][:, 1024 * k + 512 * j:1024 * k + 512 * j + 512], True, True)),
                         xt[(hl, bb)], P.loaded(f"l2_{l}"), free[o])
                xfree[2 * bp + bb] = p
                src = h3(ps[:, o, :])
                s1 = P.act(lambda e: e.activation(SQ[:, cols], ps[:, o, :], ACT.Square), p, SQf)
                a1 = P.dve(lambda e: e.tensor_tensor(h3(t1)[:, hh], src, bc(CT[:, t4, k, :], 1, 8), ALU.mult),
                           s1, tables[l], T1f[z][k])
                fill()
                for a in range(2):
                    a2 = P.dve(lambda e, a=a: e.tensor_tensor(
                        h3(T2)[:, hh, 32 * a:32 * a + 32], src[:, :, 32 - 32 * a:64 - 32 * a],
                        bc(SN[:, t4, k, 32 * a:32 * a + 32], 1, 8), ALU.mult), s1, T2f[j])
                    fill()
                free[o] = tables_free = a2
                T2f[j] = P.pool(lambda e: e.tensor_tensor(t1[:, cols], t1[:, cols], T2[:, cols], ALU.add), a1, a2)
                added[k] = T2f[j]
                if j == 1:
                    SQf = P.dve(lambda e: e.tensor_reduce(ss[z][:, H * k:H * k + H], h3(SQ), AX.X, ALU.add), s1, ssf[z])
                if i == 3:
                    summed[z] = [SQf, list(added)]
                fill()

            spare, summed, root = [], {}, {}

            def fill(n=1):
                for _ in range(n):
                    if spare:
                        spare.pop(0)()

            def inverse_root(name, y, a, tmp, least, after):
                yi, ai = y.bitcast(I32), a.bitcast(I32)
                ops = [lambda e: e.tensor_scalar(a, a, least, None, ALU.max),
                       lambda e: e.tensor_scalar(yi, ai, 1, None, ALU.arith_shift_right),
                       lambda e: e.tensor_scalar(yi, yi, -1.0, float(0x5F3759DF), ALU.mult, ALU.add)]
                ops += [lambda e: e.tensor_tensor(tmp, y, y, ALU.mult),
                        lambda e: e.scalar_tensor_tensor(tmp, tmp, -0.5, a, ALU.mult, ALU.mult),
                        lambda e: e.scalar_tensor_tensor(y, tmp, 1.5, y, ALU.add, ALU.mult)] * 3
                root[name] = after

                def queue(op):
                    root[name] = P.dve(op, root[name])

                spare.extend([lambda op=op: queue(op) for op in ops])

            def norms(r):
                z = r % 2
                inverse_root(z, sr[z], ss[z], stmp[z], 1e-24, summed[z][0])

            def unit_length(r):
                z = r % 2
                fill(len(spare))
                for k, engine in ((0, P.dve), (1, P.pool)):
                    normed[(r, k)] = engine(lambda e, k=k: e.tensor_tensor(
                        h3(T1[z][k]), h3(T1[z][k]), bc(sr[z][:, H * k:H * k + H], 2, 64), ALU.mult),
                        root[z], summed[z][1][k])
                ssf[z] = [normed[(r, 0)], normed[(r, 1)]]

            def by_feature(r, i):
                u, bb = divmod(r, 2)
                z = bb
                ur, k, j = u % 2, i // 2, i % 2
                o = (2, 0, 1, 7)[i]
                x = P.pe(transposes(*[(ps[:, o, 128 * c:128 * c + 128],
                                       T1[z][k][:, 128 * (4 * j + c):128 * (4 * j + c) + 128], ident) for c in range(4)]),
                         normed[(r, k)], free[o])
                if j == 1:
                    T1f[z][k] = x
                if k == 0:
                    pv = view(ps[:, o, :], "p (c w q) -> p c w q", c=4, w=4)
                    for hp in range(2):
                        q = slice(64 * hp, 64 * hp + 64)
                        free[o] = evacuate(0, Qbd[ur][q, bb, 4 * j:4 * j + 4, :, hp, :], pv[q], x, Qf[ur], zeroed)
                    qd.setdefault(u, []).append(free[o])
                else:
                    pv = view(ps[:, o, :], "p (c q) -> p c q", c=4)
                    free[o] = evacuate(0, kT[ur][:, bb, 4 * j:4 * j + 4, 32:160], pv, x, Kf[ur])
                    kd.setdefault(u, []).append(free[o])
                if i == 3 and bb == 1:
                    if u % 4 == 0:
                        cp = P.pool(lambda e: e.memset(kT[ur][:, :, :, 0:32], 0.0), Kf[ur])
                    else:
                        cp = P.pool(lambda e: e.tensor_copy(kT[ur][:, :, :, 0:32], kT[1 - ur][:, :, :, 128:160]),
                                    kd[u - 1], Kf[ur])
                    kpad[u] = cp

            kpad = {}
            soft, PBf, PTf, oTf = {}, [None, None], None, None
            vd, vs, VNf, VSf, unit_out, expd, lessened = {}, {}, [None, None], zeroed, {}, {}, {}

            def windows(g):
                return (1, 3) if g % 2 == 0 else (0, 2)

            def scores(g, wi):
                u, r = g // 2, g % 2
                ur, k, wn = u % 2, 3 + wi, windows(g)[wi]
                ms = [(ps[:, k, :], identb, maskb[:, 1 if u % 4 == 0 and wn == 0 else 0, :], True, False)]
                for bb in range(2):
                    for c in range(8):
                        ms.append((ps[64 * bb:64 * bb + 64, k, 64 * c:64 * c + 64],
                                   view(Qbd[ur][:, bb, c, wn], "p h q -> p (h q)"),
                                   kT[ur][:, bb, c, 32 * wn:32 * wn + 64], False, c == 7))
                t = P.pe(matmuls(*ms), qd[u], kd[u], kpad[u] if wn == 0 else None, free[k])
                if r == 1 and wi == 1:
                    Qf[ur], Kf[ur] = t, [t, kpad.get(u + 1)]
                s = view(ps[:, k, :], "p (c j) -> p c j", c=8)
                mxv = mxs[r][:, 8 * wi:8 * wi + 8]
                t = P.dve(lambda e: e.tensor_reduce(mxv, s, AX.X, ALU.max), t, mxf[r])
                fill()
                free[k] = P.dve(lambda e: e.tensor_tensor(PB[r][:, :, wi, :], s, bc(mxv, 2, 64), ALU.subtract), t, PBf[r])
                fill()
                lessened.setdefault(g, []).append(free[k])

            def exponentials(g):
                fl = view(PB[g % 2], "p c b j -> p (c b j)")
                expd[g] = P.act(lambda e: e.activation(fl, fl, ACT.Exp), lessened.pop(g))

            def normalise(g):
                r = g % 2
                f3 = view(PB[r], "p c b j -> p (c b) j")
                t = P.dve(lambda e: e.tensor_reduce(sms[r], f3, AX.X, ALU.add), expd[g])
                fill(2)
                t = P.dve(lambda e: e.reciprocal(sms[r], sms[r]), t)
                fill()
                soft[g] = P.pool(lambda e: e.tensor_tensor(f3, f3, bc(sms[r], 2, 64), ALU.mult), t)
                mxf[r] = soft[g]

            def values(u, n):
                hl, l, bp, t4 = place(u)
                bb, j = n // 2, n % 2
                k = (3, 4)[j]
                t = P.pe(matmuls((ps[:, k, :], columns(u, bb), l2[l % 2]["Wqkv"][:, 2048 + 512 * j:2560 + 512 * j],
                                  True, True)), xt[(hl, bb)], P.loaded(f"l2_{l}"), free[k])
                xfree[2 * bp + bb] = t
                free[k] = evacuate(0, VN[u % 2][:, bb, 512 * j:512 * j + 512], ps[:, k, :], t, VNf[u % 2], vs.get(u - 1))
                vd.setdefault(u, []).append(free[k])

            def shift_values(u):
                if u % 4:
                    P.load("vs", VS[0:32], VN[1 - u % 2][96:128], VSf, vd[u - 1])
                P.load("vs", VS[32:128], VN[u % 2][0:96], VSf, vd[u])
                vs[u] = P.loaded("vs")

            def turn_p(g, j):
                r = g % 2
                k = 5 + j
                t = P.pe(transposes(*[(ps[:, k, 128 * c:128 * c + 128],
                                       view(PB[r][:, 4 * j + c], "p b j -> p (b j)"), ident) for c in range(4)]),
                         soft[g], free[k])
                PBf[r] = t
                moved = []
                for wi in range(2):
                    h = slice(64 * wi, 64 * wi + 64)
                    moved.append(evacuate(j * wi, view(PT[h, 4 * j:4 * j + 4, :, :, wi, :], "p c b h q -> p (c b h) q"),
                                       view(ps[h, k, :], "p (n q) -> p n q", q=32), t, PTf, zeroed))
                free[k] = moved
                return moved

            def weigh(g, bb, ptd):
                nonlocal PTf, VSf
                u, s = g // 2, g % 2
                k = 7 - bb
                src, have = (VN[u % 2], vd[u]) if s == 0 else (VS, vs[u])
                ms = [(ps[64 * hp:64 * hp + 64, k, 64 * c:64 * c + 64],
                       src[:, bb, 128 * c + 64 * hp:128 * c + 64 * hp + 64],
                       view(PT[:, c, bb, hp], "p w q -> p (w q)"), True, True) for c in range(8) for hp in range(2)]
                t = P.pe(matmuls(*ms), ptd, have, free[k])
                if bb == 1:
                    PTf = t
                    if s == 0:
                        VNf[u % 2] = t
                    else:
                        VSf = t
                o = view(oT[:, :, bb, :], "p c (w s q) -> p c w s q", w=2, s=2)[:, :, :, 1 - s, :]
                free[k] = P.act(lambda e: e.activation(o, view(ps[:, k, :], "p (c w q) -> p c w q", c=8, w=2), ACT.Copy), t,
                                oTf if s == 0 else None)
                unit_out.setdefault(u, []).append(free[k])

            def project(u):
                nonlocal oTf
                hl, l, bp, t4 = place(u)
                w = l2[l % 2]
                ms = []
                for bb in range(2):
                    ms += [(ps[:, 3, 128 * bb:128 * bb + 128], oT[:, c, bb, :], w["Wo"][:, c, :], c == 0, c == 7)
                           for c in range(8)]
                t = P.pe(matmuls(*ms), unit_out[u], P.loaded(f"l2_{l}"), free[3])
                oTf = t
                xv = view(X, "p (b t) c -> p b t c", t=4)[:, 2 * bp:2 * bp + 2, t4, :]
                free[3] = P.dve(lambda e: e.tensor_tensor(xv, xv, view(ps[:, 3, 0:256], "p (b c) -> p b c", b=2), ALU.add), t,
                                xt[(hl, 0)], xt[(hl, 1)])
                xready[2 * bp] = xready[2 * bp + 1] = free[3]
                if bp == 1 and t4 == 3 and l + 2 < DEPTH:
                    load_l2(l + 2, t, tables[l])

            wf = l2f
            f_xn, f_rows, f_cols, f_hid = {}, {}, {}, {}
            hTf, glf = [None, None], [None, None]

            def f_shift(hl):
                l, bp = divmod(hl, 2)
                c = slice(8 * bp, 8 * bp + 8)
                after = xready[2 * bp], xready[2 * bp + 1]
                a = P.pool(lambda e: e.tensor_copy(XN[:, 0:8, 0:64], X[:, c, 0:64]), *after, glf[0])
                xs = view(X[:, c, 64:128], "p (b t) c -> p b t c", b=2)
                o = view(ps[:, 7, :], "p (b t c) -> p b t c", b=2, t=4)
                t = P.pe(matmuls((ps[:, 7, :], shiftm, X[:, c, 64:128], True, False),
                                 (o[:, :, 1:4, :], carrym, xs[:, :, 0:3, :], False, True)), *after, free[7])
                free[7] = P.act(lambda e: e.activation(XN[:, 0:8, 64:128], view(ps[:, 7, :], "p (t c) -> p t c", t=8),
                                                       ACT.Copy), t, glf[0])
                f_xn[hl] = [a, free[7]]

            def f_stats(hl):
                l, bp = divmod(hl, 2)
                c = slice(8 * bp, 8 * bp + 8)
                a = [P.dve(lambda e, i=i: e.bn_stats(st[:, 8 * bp + i, :], XN[:, i, :]), f_xn[hl]) for i in range(8)]
                a = [P.dve(lambda e, i=i: e.bn_aggr(mv[:, 8 * bp + i, :], st[:, 8 * bp + i, :]), a[i]) for i in range(8)]
                a = P.dve(lambda e: e.tensor_scalar(va[:, c], mv[:, c, 1], 1e-5, None, ALU.add), a)
                inverse_root("rows", rs[:, c], va[:, c], rt[:, c], 1e-5, a)

            def f_norm(hl):
                l, bp = divmod(hl, 2)
                fill(len(spare))
                for i in range(8):
                    j = 8 * bp + i
                    f_rows[(hl, i)] = P.dve(lambda e, i=i, j=j: e.tensor_scalar(
                        XN[:, i, :], XN[:, i, :], mv[:, j, 0:1], rs[:, j:j + 1], ALU.subtract, ALU.mult), root["rows"])

            def f_turn(hl, bb):
                l, bp = divmod(hl, 2)
                b, k = 2 * bp + bb, 7 - bb
                t = P.pe(transposes(*[(ps[:, k, 128 * j:128 * j + 128], XN[:, 4 * bb + j, :], ident) for j in range(4)]),
                         f_rows[(hl, 4 * bb + 3)], free[k])
                glf[0] = t
                free[k] = f_cols[(hl, bb)] = P.act(lambda e: e.activation(
                    xT[:, b, 33:33 + S], ps[:, k, :], ACT.Identity, bias=wf["b"], scale=wf["g"]), t, xfree[b],
                    P.loaded(f"l2f_{l}"))

            def f_up(hl, bb, c, z=0):
                l, bp = divmod(hl, 2)
                b, n = 2 * bp + bb, (128, 128, 85)[c]
                cols = xT[:, b, 33:33 + S]
                p2, p1 = ps[0:n, 6, :], ps[0:n, 4, :]
                t = P.pe(matmuls((p2, wf["W1"][:, 341 + 128 * c:341 + 128 * c + n], cols, True, True)), f_cols[(hl, bb)],
                         free[6])
                xfree[b] = t1 = P.pe(matmuls((p1, wf["W1"][:, 128 * c:128 * c + n], cols, True, True)), free[4])
                free[6] = a = P.act(lambda e: e.activation(gl[z][c][0:n], p2, ACT.Identity, bias=wf["b1"][0:n, 3 + c:4 + c]),
                                    t, glf[z])
                free[4] = s = P.act(lambda e: e.activation(hT[z][0:n, c, :], p1, ACT.Identity, bias=wf["b1"][0:n, c:c + 1]),
                                    t1, hTf[z])
                f_part[(hl, bb, c)] = a, s

            f_part = {}

            def f_gate(hl, bb, z=0):
                for c, n in enumerate((128, 128, 85)):
                    a, s = f_part[(hl, bb, c)]
                    a = P.act(lambda e, c=c, n=n: e.activation(gl[z][c][0:n], gl[z][c][0:n], ACT.Gelu), a)
                    glf[z] = P.dve(lambda e, c=c, n=n: e.tensor_tensor(hT[z][0:n, c, :], hT[z][0:n, c, :], gl[z][c][0:n],
                                                                       ALU.mult), a, s)
                f_hid[(hl, bb)] = [glf[z]]
                P.act(lambda e: e.activation(warm, onesf[:, 0:1], ACT.Exp))

            def f_down(hl, bb, z=0):
                l, bp = divmod(hl, 2)
                b = 2 * bp + bb
                ms = []
                for j in range(4):
                    o = ps[:, 7, 128 * j:128 * j + 128]
                    ms += [(o, hT[z][0:n, c, 128 * j:128 * j + 128], wf["W2"][0:n, c, :], c == 0, False)
                           for c, n in enumerate((128, 128, 85))]
                    ms.append((o, onesf[0:1, :], wf["b2"][0:1], False, True))
                hTf[z] = t = P.pe(matmuls(*ms), f_hid[(hl, bb)], free[7])
                xready[b] = add_rows(b, 7, t)
                if bp == 1 and bb == 1 and l + 1 < DEPTH:
                    load_l2f(l + 1, t)

            def beside(hl, w, when):
                if hl + 1 < 2 * DEPTH:
                    if (w, when) in ((5, 0), (6, 0)):
                        turn_x(hl + 1, w - 5, 7)
                    if (w, when) == (4, 2) and hl % 2 == 1:
                        make_tables((hl + 1) // 2)
                if hl >= 1:
                    f = hl - 1
                    plan = {(0, 2): lambda: f_shift(f), (1, 0): lambda: f_stats(f), (1, 3): lambda: f_norm(f),
                            (2, 1): lambda: (f_turn(f, 0), f_turn(f, 1)),
                            (2, 2): lambda: f_up(f, 0, 0), (3, 1): lambda: f_up(f, 0, 1), (3, 2): lambda: f_up(f, 0, 2),
                            (4, 0): lambda: f_gate(f, 0), (4, 1): lambda: (f_down(f, 0), f_up(f, 1, 0)),
                            (4, 2): lambda: f_up(f, 1, 1), (5, 0): lambda: (f_up(f, 1, 2), f_gate(f, 1)),
                            (5, 1): lambda: f_down(f, 1)}
                    if (w, when) in plan:
                        plan[(w, when)]()

            make_tables(0)
            for bb in range(2):
                turn_x(0, bb, 6 + bb)
            for r in range(2):
                for i in range(4):
                    rotate(r, i)
                norms(r)
                unit_length(r)
            for n in range(4):
                values(0, n)
            for r in range(2):
                for i in range(4):
                    by_feature(r, i)
            for i in range(4):
                rotate(2, i)
            norms(2)
            for g in range(NG + 1):
                u, s = divmod(g, 2)
                hl, w = divmod(g, 8)
                this, last, turned, placed = g < NG, g >= 1, g + 3 < NG, g + 2 < NG
                if last:
                    ptd = [turn_p(g - 1, 0), turn_p(g - 1, 1)]
                if this:
                    beside(hl, w, 0)
                    scores(g, 0)
                    scores(g, 1)
                if turned:
                    rotate(g + 3, 0)
                    rotate(g + 3, 1)
                if this:
                    exponentials(g)
                if last:
                    weigh(g - 1, 0, ptd)
                    weigh(g - 1, 1, ptd)
                if placed:
                    unit_length(g + 2)
                if turned:
                    rotate(g + 3, 2)
                if this:
                    normalise(g)
                if turned:
                    rotate(g + 3, 3)
                if this:
                    beside(hl, w, 3)
                if turned:
                    norms(g + 3)
                if this:
                    beside(hl, w, 1)
                if s == 0 and last:
                    project(u - 1)
                if s == 0 and this:
                    shift_values(u)
                if s == 1 and this and u + 1 < NU:
                    for n in range(4):
                        values(u + 1, n)
                if placed:
                    for i in range(4):
                        by_feature(g + 2, i)
                if this:
                    beside(hl, w, 2)
            f = 2 * DEPTH - 1
            hTf[1] = glf[1] = Qf[0]
            f_shift(f)
            f_stats(f)
            f_norm(f)
            for bb in range(2):
                f_turn(f, bb)
            for bb in range(2):
                for c in range(3):
                    f_up(f, bb, c, bb)
                f_gate(f, bb, bb)
            for bb in range(2):
                f_down(f, bb, bb)
            now = P.barrier()
            P.load("back", XN, rows, now)
            P.dve(lambda e: e.tensor_tensor(X, X, XN, ALU.add), P.loaded("back"))
            P.barrier()

        if 1 in stages:
            load_moe0()
        load_rest()
        small = P.loaded("small")
        if 0 in stages:
            xcond("0", base + 12288, last=later_constants)
        else:
            later_constants()
            P.barrier()
        arrive = l0_ffn() if 1 in stages else None
        if 2 in stages:
            xcond("1", base, arrive)
        elif arrive:
            for b in range(B):
                arrive(b)
            P.barrier()
        if 3 in stages:
            l1_ffn()
        if 4 in stages:
            l2_xcond()
        if 5 in stages:
            l2_ffn()
        if 7 in stages:
            load_moe3()
        if 6 in stages:
            load_xw("3")
            dl3_done["3"] = make_delta("delta3", late)
            xcond("3", base + 12288)
        rows = out.rearrange("(t p) d -> p t d", p=128)
        if 7 in stages:
            arrive = l3_ffn()
            for b in range(B):
                P.load("out", rows[:, 4 * b:4 * b + 4, :], X[:, 4 * b:4 * b + 4, :], list(arrive(b).values()))
        else:
            P.barrier()
            P.load("out", rows, X)
        P.queue["sync"].append((None, [P.loaded(n) for n in P.sems if n not in ENGINES], None, 0))

        block = ctx.enter_context(nc.Block())

        @block.sync
        def _(e):
            P.emit("sync", e)

        @block.gpsimd
        def _(e):
            P.emit("gpsimd", e)

        @block.scalar
        def _(e):
            P.emit("scalar", e)

        @block.tensor
        def _(e):
            P.emit("tensor", e)

        @block.vector
        def _(e):
            P.emit("vector", e)


def constants():
    n, dh = S, 64
    half = np.arange(0, dh, 2, dtype=np.float32)
    inv = (1.0 / np.float32(10000.0) ** (half / np.float32(dh))).astype(np.float32)
    pos = np.arange(n, dtype=np.float32)
    fr = pos[:, None] * inv[None, :]
    fr = np.concatenate([fr, fr], -1).astype(np.float64)
    basis = ((half + np.float32(0.4 * dh)) / np.float32(1.4 * dh)).astype(np.float64)
    power = (pos.astype(np.float64) - n // 2) / 16
    scale = basis[None, :] ** power[:, None]
    scale = np.concatenate([scale, scale], -1)
    sign = np.where(np.arange(dh) < dh // 2, -1.0, 1.0)
    c = np.stack([8 * np.cos(fr) * scale, np.cos(fr) / scale], 1)
    s = np.stack([8 * np.sin(fr) * scale * sign, np.sin(fr) / scale * sign], 1)
    rows = lambda z: np.ascontiguousarray(z.reshape(4, 128, 2, dh).transpose(1, 0, 2, 3).astype(np.float32))
    p = np.arange(128)
    q, j = p[:, None] % 32, np.arange(64)[None, :]
    hidden = (j < q) | (j > q + 32)
    start = hidden | (j < 32)
    return dict(
        ident=np.eye(128, dtype=np.float32), lower=(p[:, None] < p[None, :]).astype(np.float32),
        shiftm=(p[:, None] == p[None, :] - 1).astype(np.float32),
        carrym=((p[:, None] == 127) & (p[None, :] == 0)).astype(np.float32),
        hm=(p[:, None] // 8 == np.arange(16)[None, :]).astype(np.float32), rotc=rows(c), rots=rows(s),
        masks=np.stack([hidden, start], 1).astype(np.float32) * np.float32(NEG),
        idx=np.arange(L, dtype=np.float32), sel3=np.eye(3, dtype=np.float32))


def layout(i):
    c = np.ascontiguousarray
    a = {"x": i["x"].reshape(B * S, D), "ctxT": c(i["ctx_1024"].transpose(2, 0, 1)),
         "ctxk": c(i["ctx_1024"].transpose(1, 0, 2)), "tau": i["condB_tau"], "pt": i["condB_pt"], "len": i["_lenS2"],
         "delta": i["fside_BxS2_0"]}
    for n in "013":
        for k in "qkvo":
            a[f"L{n}W{k}"] = c(i[f"L{n}_xcond_W{k}"].T)
        for k in "qk":
            a[f"L{n}b{k}"] = i[f"L{n}_xcond_b{k}"].reshape(D, 1)
        for k in "vo":
            a[f"L{n}b{k}"] = i[f"L{n}_xcond_b{k}"].reshape(1, D)
    a["lng"], a["lnb"] = i["L0_ffn_ln_gamma"].reshape(D, 1), i["L0_ffn_ln_beta"].reshape(D, 1)
    a["WrT"], a["WgT"] = c(i["L0_ffn_Wr"].T), c(i["L3_ffn_Wg"].T)
    a["W12T"] = c(i["L0_ffn_W12"].transpose(0, 2, 1))
    a["W3T"] = c(i["L0_ffn_W3"].reshape(E, D, 4, 128).transpose(0, 3, 2, 1))
    a["w1T"] = c(i["L1_ffn_w1"].T)
    a["w2T"] = c(i["L1_ffn_w2"].reshape(D, 4, 128).transpose(2, 1, 0))
    a["cvw"] = c(i["L1_ffn_conv_w"].reshape(4, 128, 3).transpose(1, 0, 2))
    a["cvb"] = c(i["L1_ffn_conv_b"].reshape(4, 128).T)
    a["Wa"] = i["L2_xcond_W_a"]
    a["WcT"] = c(i["L2_xcond_W_c"].reshape(D, 2, 128).transpose(2, 1, 0))
    a["Wqkv"], a["W1"], a["W2"] = i["L2_ffn_Wqkv"], i["L2_ffn_W1"], i["L2_ffn_W2"]
    a["L2Wo"] = c(i["L2_ffn_Wo"].reshape(DEPTH, 8, 128, D).transpose(0, 2, 1, 3))
    b1 = np.zeros((DEPTH, 128, 6), np.float32)
    for k in range(2):
        for n, rows in enumerate((128, 128, 85)):
            b1[:, :rows, 3 * k + n] = i["L2_ffn_b1"][:, 341 * k + 128 * n:341 * k + 128 * n + rows]
    a["b1"] = b1
    a["ln_g"], a["ln_b"] = i["L2_ffn_ln_g"].reshape(DEPTH, D, 1), i["L2_ffn_ln_b"].reshape(DEPTH, D, 1)
    a["b2"] = i["L2_ffn_b2"].reshape(DEPTH, 1, D)
    a["qks"] = c(np.stack([i["L2_ffn_q_scale"], i["L2_ffn_k_scale"]], 1))
    a["L3W1"], a["L3W2"] = i["L3_ffn_W1"], i["L3_ffn_W2"]
    a["L3b1"] = c(i["L3_ffn_b1"].reshape(E, 4, 128).transpose(2, 0, 1))
    a["L3b2"] = i["L3_ffn_b2"]
    a.update(constants())
    return {k: c(v) for k, v in a.items()}


def declare(nc, arrays):
    d = {k: nc.dram_tensor("in_" + k, v.shape, mybir.dt.from_np(v.dtype), kind="ExternalInput").ap()
         for k, v in arrays.items()}
    kept = nc.dram_tensor("kept", (B * S, D), F32, kind="Internal").ap()
    out = nc.dram_tensor("out_x", (B * S, D), F32, kind="ExternalOutput").ap()
    slots = {k: nc.dram_tensor(k, (E * SLOTS, D), F32, kind="Internal").ap() for k in ("x0", "y0", "x3", "y3")}
    return d, kept, slots, out


def kernel(**inputs):
    import concourse.bacc as bacc
    from concourse.bass_utils import run_bass_kernel_spmd
    arrays = layout({k: np.asarray(v) for k, v in inputs.items()})
    nc = bacc.Bacc("TRN2", target_bir_lowering=False, num_devices=1)
    build(nc, *declare(nc, arrays), range(8))
    r = run_bass_kernel_spmd(nc, [{"in_" + k: v for k, v in arrays.items()}], core_ids=[0])
    return r.results[0]["out_x"].reshape(B, S, D)
```
